# Optimizing a Trainium2 kernel written in Bass

```python
import numpy as np
import jax
import jax.numpy as jnp

def _softmax(x, axis=-1):
    return jax.nn.softmax(x, axis=axis)

def _gelu(x):
    return jax.nn.gelu(x, approximate=True)

def _silu(x):
    return jax.nn.silu(x)

def _sigmoid(x):
    return jax.nn.sigmoid(x)

def _layernorm(x, axis=-1, eps=1e-05):
    m = jnp.mean(x, axis=axis, keepdims=True)
    v = jnp.var(x, axis=axis, keepdims=True)
    return (x - m) / jnp.sqrt(v + eps)

def _scatter_add(tgt, idx, src, axis=0):
    return tgt.at[idx].add(src)

def _segment_sum(src, seg, n):
    return jax.ops.segment_sum(src, seg, n)
kernel_name = 'mk_recurrent_d2_jaxref_r8_169dac'

def setup_inputs(seed: int=0):
    np.random.seed(seed)
    _w = jnp.asarray

    def _L0_attn_setup():
        import jax, jax.numpy as jnp
        import numpy as np
        from jax import lax
        B, S, D = (8, 128, 128)
        DH = D // 2
        H = 8
        DK = DH // H
        DFF = 4 * D
        ALPHA, BETA = (0.1, 0.1)
        EPS = 1e-05
        PARAM_SPECS = [('wq1', (DH, DH)), ('bq1', (DH,)), ('wk1', (DH, DH)), ('bk1', (DH,)), ('wv1', (DH, DH)), ('bv1', (DH,)), ('wo1', (DH, DH)), ('bo1', (DH,)), ('wq2', (DH, DH)), ('bq2', (DH,)), ('wk2', (DH, DH)), ('bk2', (DH,)), ('wv2', (DH, DH)), ('bv2', (DH,)), ('wo2', (DH, DH)), ('bo2', (DH,)), ('g1', (DH,)), ('be1', (DH,)), ('g2', (DH,)), ('be2', (DH,)), ('w_ff1', (DFF, D)), ('b_ff1', (DFF,)), ('w_ff2', (D, DFF)), ('b_ff2', (D,)), ('g_ff', (D,)), ('be_ff', (D,))]

        def layernorm(x, g, b):
            m = jnp.mean(x, axis=-1, keepdims=True)
            v = jnp.mean(jnp.square(x - m), axis=-1, keepdims=True)
            return (x - m) * lax.rsqrt(v + EPS) * g + b

        def mha(xin, wq, bq, wk, bk, wv, bv, wo, bo):
            b, s, _ = xin.shape
            q = (xin @ wq.T + bq).reshape(b, s, H, DK)
            k = (xin @ wk.T + bk).reshape(b, s, H, DK)
            v = (xin @ wv.T + bv).reshape(b, s, H, DK)
            scores = jnp.einsum('bshd,bthd->bhst', q, k) * (1.0 / np.sqrt(DK).astype(np.float32))
            a = jax.nn.softmax(scores, axis=-1)
            o = jnp.einsum('bhst,bthd->bshd', a, v).reshape(b, s, DH)
            return o @ wo.T + bo

        def holt(x, alpha, beta):
            x0 = x[:, 0]

            def step(carry, xt):
                level, trend = carry
                nl = alpha * xt + (1.0 - alpha) * (level + trend)
                nt = beta * (nl - level) + (1.0 - beta) * trend
                return ((nl, nt), nl)
            _, lv = lax.scan(step, (x0, jnp.zeros_like(x0)), jnp.swapaxes(x[:, 1:], 0, 1))
            return jnp.concatenate([x0[:, None], jnp.swapaxes(lv, 0, 1)], axis=1)
        key = jax.random.key(seed)
        inp = {'x': jax.random.normal(jax.random.fold_in(key, 0), (B, S, D), jnp.float32)}
        for i, (name, shape) in enumerate(PARAM_SPECS):
            k = jax.random.fold_in(key, i + 1)
            if name.startswith('g'):
                inp[name] = jnp.ones(shape, jnp.float32)
            elif name.startswith('b'):
                inp[name] = jnp.zeros(shape, jnp.float32)
            else:
                inp[name] = jax.random.normal(k, shape, jnp.float32) * 0.02
        return inp
    _L0_attn_in = _L0_attn_setup()

    def _L0_ffn_setup():
        import jax, jax.numpy as jnp
        import numpy as np
        DIM = 128
        INTER = 128
        E = 32
        K = 4
        G = 8
        LG = 4
        ROUTE_SCALE = 1.0
        CAP_FACTOR = 1.25
        B, S = (4, 256)

        def _gate(xf, wg):
            logits = xf @ wg.T
            scores = jax.nn.softmax(logits, axis=-1)
            sg = scores.reshape(-1, G, E // G)
            group_scores = sg.max(axis=-1)
            _, gtop = jax.lax.top_k(group_scores, LG)
            keep_g = jnp.sum(jax.nn.one_hot(gtop, G, dtype=jnp.float32), axis=1) > 0
            masked = jnp.where(keep_g[:, :, None], sg, -jnp.inf).reshape(-1, E)
            _, idx = jax.lax.top_k(masked, K)
            w = jnp.take_along_axis(scores, idx, axis=1)
            w = w / (w.sum(-1, keepdims=True) + 1e-09) * ROUTE_SCALE
            return (w.astype(xf.dtype), idx)

        def _forward(x, wg, w1, w2, w3, sw1, sw2, sw3):
            shape = x.shape
            xf = x.reshape(-1, DIM)
            N = xf.shape[0]
            cap = max(1, int(CAP_FACTOR * N * K / E))
            w, idx = _gate(xf, wg)
            fe = idx.reshape(-1)
            oh = jax.nn.one_hot(fe, E, dtype=jnp.int32)
            pos = (jnp.cumsum(oh, axis=0) * oh).sum(-1) - 1
            keep = pos < cap
            dest = jnp.where(keep, fe * cap + pos, E * cap)
            tok = jnp.arange(N * K, dtype=jnp.int32) // K
            buf_tok = jnp.full((E * cap + 1,), N, jnp.int32).at[dest].set(tok)[:-1]
            buf_w = jnp.zeros((E * cap + 1,), x.dtype).at[dest].set(w.reshape(-1))[:-1]
            xp = jnp.concatenate([xf, jnp.zeros((1, DIM), x.dtype)], axis=0)
            xe = xp[buf_tok].reshape(E, cap, DIM)
            h = jax.nn.silu(jnp.einsum('ecd,edh->ech', xe, w1)) * jnp.einsum('ecd,edh->ech', xe, w3)
            out = jnp.einsum('ech,ehd->ecd', h, w2) * buf_w.reshape(E, cap, 1)
            y = jnp.zeros((N + 1, DIM), x.dtype).at[buf_tok].add(out.reshape(E * cap, DIM))[:N]
            z = jax.nn.silu(xf @ sw1) * (xf @ sw3) @ sw2
            return (y + z).reshape(shape)
        key = jax.random.key(seed)
        ks = jax.random.split(key, 9)
        sd = DIM ** (-0.5)
        si = INTER ** (-0.5)
        x = jax.random.normal(ks[0], (B, S, DIM), jnp.float32)
        wg = jax.random.normal(ks[1], (E, DIM), jnp.float32) * sd
        w1 = jax.random.normal(ks[2], (E, DIM, INTER), jnp.float32) * sd
        w3 = jax.random.normal(ks[3], (E, DIM, INTER), jnp.float32) * sd
        w2 = jax.random.normal(ks[4], (E, INTER, DIM), jnp.float32) * si
        sw1 = jax.random.normal(ks[5], (DIM, INTER), jnp.float32) * sd
        sw3 = jax.random.normal(ks[6], (DIM, INTER), jnp.float32) * sd
        sw2 = jax.random.normal(ks[7], (INTER, DIM), jnp.float32) * si
        return dict(x=x, wg=wg, w1=w1, w2=w2, w3=w3, sw1=sw1, sw2=sw2, sw3=sw3)
    _L0_ffn_in = _L0_ffn_setup()

    def _L1_attn_setup():
        import jax, jax.numpy as jnp
        import numpy as np
        D_MODEL = 128
        D_STATE = 64
        HEADDIM = 64
        EXPAND = 2
        D_INNER = D_MODEL * EXPAND
        NHEADS = D_INNER // HEADDIM
        D_IN_PROJ = 2 * D_INNER + 2 * D_STATE + NHEADS
        BATCH, SEQLEN = (4, 512)

        def layernorm(x, w, b, eps=1e-05):
            mu = jnp.mean(x, axis=-1, keepdims=True)
            var = jnp.mean(jnp.square(x - mu), axis=-1, keepdims=True)
            return (x - mu) * jax.lax.rsqrt(var + eps) * w + b

        def _selective_scan(x_multi, A, Bm, Cm, dt):
            Bb, L, H, P = x_multi.shape
            N = Bm.shape[-1]
            dA = jnp.minimum(jnp.exp(dt * A[None, None, :]), 0.99)

            def step(h, inp):
                x_t, B_t, C_t, dA_t = inp
                dBx = jnp.einsum('bhp,bn->bhpn', x_t, B_t)
                h = jnp.clip(dA_t[:, :, None, None] * h + dBx, -10.0, 10.0)
                y_t = jnp.einsum('bn,bhpn->bhp', C_t, h)
                return (h, y_t)
            h0 = jnp.zeros((Bb, H, P, N), dtype=x_multi.dtype)
            xs = (jnp.moveaxis(x_multi, 1, 0), jnp.moveaxis(Bm, 1, 0), jnp.moveaxis(Cm, 1, 0), jnp.moveaxis(dA, 1, 0))
            _, y = jax.lax.scan(step, h0, xs)
            return jnp.moveaxis(y, 0, 1)
        key = jax.random.key(seed)
        ks = jax.random.split(key, 5)
        x = jax.random.normal(ks[0], (BATCH, SEQLEN, D_MODEL), dtype=jnp.float32)
        in_proj_w = jax.random.normal(ks[1], (D_IN_PROJ, D_MODEL), dtype=jnp.float32) * 0.5 * np.sqrt(2.0 / (D_IN_PROJ + D_MODEL))
        out_proj_w = jax.random.normal(ks[2], (D_MODEL, D_INNER), dtype=jnp.float32) * 0.5 * np.sqrt(2.0 / (D_MODEL + D_INNER))
        A_log = jnp.log(jnp.arange(1, NHEADS + 1, dtype=jnp.float32))
        dt_bias = jax.random.normal(ks[3], (NHEADS,), dtype=jnp.float32) * 0.01 + 0.1
        Dparam = jnp.ones((NHEADS,), dtype=jnp.float32)
        return {'x': x, 'in_proj_w': in_proj_w, 'out_proj_w': out_proj_w, 'A_log': A_log, 'dt_bias': dt_bias, 'Dparam': Dparam, 'ln_w': jnp.ones((D_INNER,), jnp.float32), 'ln_b': jnp.zeros((D_INNER,), jnp.float32), 'ni_w': jnp.ones((D_MODEL,), jnp.float32), 'ni_b': jnp.zeros((D_MODEL,), jnp.float32), 'no_w': jnp.ones((D_MODEL,), jnp.float32), 'no_b': jnp.zeros((D_MODEL,), jnp.float32)}
    _L1_attn_in = _L1_attn_setup()

    def _L1_ffn_setup():
        import jax, jax.numpy as jnp
        import numpy as np
        B, S, H = (8, 512, 128)
        NAV = 128
        E = 8
        F = 2 * H
        key = jax.random.key(seed)
        ks = jax.random.split(key, 12)

        def w(k, shape, fan_in):
            return jax.random.normal(k, shape, dtype=jnp.float32) / np.sqrt(fan_in)
        return {'hidden_states': jax.random.normal(ks[0], (B, S, H), dtype=jnp.float32), 'Wp1': w(ks[1], (H, NAV), H), 'bp1': jnp.zeros((NAV,), jnp.float32), 'Wp2': w(ks[2], (NAV, E), NAV), 'bp2': jnp.zeros((E,), jnp.float32), 'W1': w(ks[3], (E, H, F), H), 'b1': jnp.zeros((E, F), jnp.float32), 'W2': w(ks[4], (E, F, H), F), 'b2': jnp.zeros((E, H), jnp.float32), 'Wo': w(ks[5], (H, H), H), 'bo': jnp.zeros((H,), jnp.float32)}
    _L1_ffn_in = _L1_ffn_setup()
    _d = {'L0_attn_x': _L0_attn_in['x'], 'L0_attn_wq1': _L0_attn_in['wq1'], 'L0_attn_bq1': _L0_attn_in['bq1'], 'L0_attn_wk1': _L0_attn_in['wk1'], 'L0_attn_bk1': _L0_attn_in['bk1'], 'L0_attn_wv1': _L0_attn_in['wv1'], 'L0_attn_bv1': _L0_attn_in['bv1'], 'L0_attn_wo1': _L0_attn_in['wo1'], 'L0_attn_bo1': _L0_attn_in['bo1'], 'L0_attn_wq2': _L0_attn_in['wq2'], 'L0_attn_bq2': _L0_attn_in['bq2'], 'L0_attn_wk2': _L0_attn_in['wk2'], 'L0_attn_bk2': _L0_attn_in['bk2'], 'L0_attn_wv2': _L0_attn_in['wv2'], 'L0_attn_bv2': _L0_attn_in['bv2'], 'L0_attn_wo2': _L0_attn_in['wo2'], 'L0_attn_bo2': _L0_attn_in['bo2'], 'L0_attn_g1': _L0_attn_in['g1'], 'L0_attn_be1': _L0_attn_in['be1'], 'L0_attn_g2': _L0_attn_in['g2'], 'L0_attn_be2': _L0_attn_in['be2'], 'L0_attn_w_ff1': _L0_attn_in['w_ff1'], 'L0_attn_b_ff1': _L0_attn_in['b_ff1'], 'L0_attn_w_ff2': _L0_attn_in['w_ff2'], 'L0_attn_b_ff2': _L0_attn_in['b_ff2'], 'L0_attn_g_ff': _L0_attn_in['g_ff'], 'L0_attn_be_ff': _L0_attn_in['be_ff'], 'L0_ffn_wg': _L0_ffn_in['wg'], 'L0_ffn_w1': _L0_ffn_in['w1'], 'L0_ffn_w2': _L0_ffn_in['w2'], 'L0_ffn_w3': _L0_ffn_in['w3'], 'L0_ffn_sw1': _L0_ffn_in['sw1'], 'L0_ffn_sw2': _L0_ffn_in['sw2'], 'L0_ffn_sw3': _L0_ffn_in['sw3'], 'L1_attn_in_proj_w': _L1_attn_in['in_proj_w'], 'L1_attn_out_proj_w': _L1_attn_in['out_proj_w'], 'L1_attn_A_log': _L1_attn_in['A_log'], 'L1_attn_dt_bias': _L1_attn_in['dt_bias'], 'L1_attn_Dparam': _L1_attn_in['Dparam'], 'L1_attn_ln_w': _L1_attn_in['ln_w'], 'L1_attn_ln_b': _L1_attn_in['ln_b'], 'L1_attn_ni_w': _L1_attn_in['ni_w'], 'L1_attn_ni_b': _L1_attn_in['ni_b'], 'L1_attn_no_w': _L1_attn_in['no_w'], 'L1_attn_no_b': _L1_attn_in['no_b'], 'L1_ffn_Wp1': _L1_ffn_in['Wp1'], 'L1_ffn_bp1': _L1_ffn_in['bp1'], 'L1_ffn_Wp2': _L1_ffn_in['Wp2'], 'L1_ffn_bp2': _L1_ffn_in['bp2'], 'L1_ffn_W1': _L1_ffn_in['W1'], 'L1_ffn_b1': _L1_ffn_in['b1'], 'L1_ffn_W2': _L1_ffn_in['W2'], 'L1_ffn_b2': _L1_ffn_in['b2'], 'L1_ffn_Wo': _L1_ffn_in['Wo'], 'L1_ffn_bo': _L1_ffn_in['bo']}
    _x0 = _d['L0_attn_x']
    _d['L0_attn_x'] = jax.random.normal(jax.random.fold_in(jax.random.key(seed), 1), (2, 2048, 128), dtype=_x0.dtype)
    del _x0
    return _d

def reference(L0_attn_x, L0_attn_wq1, L0_attn_bq1, L0_attn_wk1, L0_attn_bk1, L0_attn_wv1, L0_attn_bv1, L0_attn_wo1, L0_attn_bo1, L0_attn_wq2, L0_attn_bq2, L0_attn_wk2, L0_attn_bk2, L0_attn_wv2, L0_attn_bv2, L0_attn_wo2, L0_attn_bo2, L0_attn_g1, L0_attn_be1, L0_attn_g2, L0_attn_be2, L0_attn_w_ff1, L0_attn_b_ff1, L0_attn_w_ff2, L0_attn_b_ff2, L0_attn_g_ff, L0_attn_be_ff, L0_ffn_wg, L0_ffn_w1, L0_ffn_w2, L0_ffn_w3, L0_ffn_sw1, L0_ffn_sw2, L0_ffn_sw3, L1_attn_in_proj_w, L1_attn_out_proj_w, L1_attn_A_log, L1_attn_dt_bias, L1_attn_Dparam, L1_attn_ln_w, L1_attn_ln_b, L1_attn_ni_w, L1_attn_ni_b, L1_attn_no_w, L1_attn_no_b, L1_ffn_Wp1, L1_ffn_bp1, L1_ffn_Wp2, L1_ffn_bp2, L1_ffn_W1, L1_ffn_b1, L1_ffn_W2, L1_ffn_b2, L1_ffn_Wo, L1_ffn_bo):

    def _L0_attn_ref(x, wq1, bq1, wk1, bk1, wv1, bv1, wo1, bo1, wq2, bq2, wk2, bk2, wv2, bv2, wo2, bo2, g1, be1, g2, be2, w_ff1, b_ff1, w_ff2, b_ff2, g_ff, be_ff):
        import jax, jax.numpy as jnp
        import numpy as np
        from jax import lax
        B, S, D = (8, 128, 128)
        DH = D // 2
        H = 8
        DK = DH // H
        DFF = 4 * D
        ALPHA, BETA = (0.1, 0.1)
        EPS = 1e-05
        PARAM_SPECS = [('wq1', (DH, DH)), ('bq1', (DH,)), ('wk1', (DH, DH)), ('bk1', (DH,)), ('wv1', (DH, DH)), ('bv1', (DH,)), ('wo1', (DH, DH)), ('bo1', (DH,)), ('wq2', (DH, DH)), ('bq2', (DH,)), ('wk2', (DH, DH)), ('bk2', (DH,)), ('wv2', (DH, DH)), ('bv2', (DH,)), ('wo2', (DH, DH)), ('bo2', (DH,)), ('g1', (DH,)), ('be1', (DH,)), ('g2', (DH,)), ('be2', (DH,)), ('w_ff1', (DFF, D)), ('b_ff1', (DFF,)), ('w_ff2', (D, DFF)), ('b_ff2', (D,)), ('g_ff', (D,)), ('be_ff', (D,))]

        def layernorm(x, g, b):
            m = jnp.mean(x, axis=-1, keepdims=True)
            v = jnp.mean(jnp.square(x - m), axis=-1, keepdims=True)
            return (x - m) * lax.rsqrt(v + EPS) * g + b

        def mha(xin, wq, bq, wk, bk, wv, bv, wo, bo):
            b, s, _ = xin.shape
            q = (xin @ wq.T + bq).reshape(b, s, H, DK)
            k = (xin @ wk.T + bk).reshape(b, s, H, DK)
            v = (xin @ wv.T + bv).reshape(b, s, H, DK)
            scores = jnp.einsum('bshd,bthd->bhst', q, k) * (1.0 / np.sqrt(DK).astype(np.float32))
            a = jax.nn.softmax(scores, axis=-1)
            o = jnp.einsum('bhst,bthd->bshd', a, v).reshape(b, s, DH)
            return o @ wo.T + bo

        def holt(x, alpha, beta):
            x0 = x[:, 0]

            def step(carry, xt):
                level, trend = carry
                nl = alpha * xt + (1.0 - alpha) * (level + trend)
                nt = beta * (nl - level) + (1.0 - beta) * trend
                return ((nl, nt), nl)
            _, lv = lax.scan(step, (x0, jnp.zeros_like(x0)), jnp.swapaxes(x[:, 1:], 0, 1))
            return jnp.concatenate([x0[:, None], jnp.swapaxes(lv, 0, 1)], axis=1)
        xh = x[:, :, :DH]
        x1 = layernorm(xh + mha(xh, wq1, bq1, wk1, bk1, wv1, bv1, wo1, bo1), g1, be1)
        xs = holt(x, ALPHA, BETA)
        xsh = xs[:, :, :DH]
        x2 = layernorm(xsh + mha(xsh, wq2, bq2, wk2, bk2, wv2, bv2, wo2, bo2), g2, be2)
        y = jnp.concatenate([x1, x2], axis=-1)
        y_ff = jax.nn.relu(y @ w_ff1.T + b_ff1) @ w_ff2.T + b_ff2
        return layernorm(y + y_ff, g_ff, be_ff)

    def _L0_ffn_ref(x, wg, w1, w2, w3, sw1, sw2, sw3):
        import jax, jax.numpy as jnp
        import numpy as np
        DIM = 128
        INTER = 128
        E = 32
        K = 4
        G = 8
        LG = 4
        ROUTE_SCALE = 1.0
        CAP_FACTOR = 1.25
        B, S = (4, 256)

        def _gate(xf, wg):
            logits = xf @ wg.T
            scores = jax.nn.softmax(logits, axis=-1)
            sg = scores.reshape(-1, G, E // G)
            group_scores = sg.max(axis=-1)
            _, gtop = jax.lax.top_k(group_scores, LG)
            keep_g = jnp.sum(jax.nn.one_hot(gtop, G, dtype=jnp.float32), axis=1) > 0
            masked = jnp.where(keep_g[:, :, None], sg, -jnp.inf).reshape(-1, E)
            _, idx = jax.lax.top_k(masked, K)
            w = jnp.take_along_axis(scores, idx, axis=1)
            w = w / (w.sum(-1, keepdims=True) + 1e-09) * ROUTE_SCALE
            return (w.astype(xf.dtype), idx)

        def _forward(x, wg, w1, w2, w3, sw1, sw2, sw3):
            shape = x.shape
            xf = x.reshape(-1, DIM)
            N = xf.shape[0]
            cap = max(1, int(CAP_FACTOR * N * K / E))
            w, idx = _gate(xf, wg)
            fe = idx.reshape(-1)
            oh = jax.nn.one_hot(fe, E, dtype=jnp.int32)
            pos = (jnp.cumsum(oh, axis=0) * oh).sum(-1) - 1
            keep = pos < cap
            dest = jnp.where(keep, fe * cap + pos, E * cap)
            tok = jnp.arange(N * K, dtype=jnp.int32) // K
            buf_tok = jnp.full((E * cap + 1,), N, jnp.int32).at[dest].set(tok)[:-1]
            buf_w = jnp.zeros((E * cap + 1,), x.dtype).at[dest].set(w.reshape(-1))[:-1]
            xp = jnp.concatenate([xf, jnp.zeros((1, DIM), x.dtype)], axis=0)
            xe = xp[buf_tok].reshape(E, cap, DIM)
            h = jax.nn.silu(jnp.einsum('ecd,edh->ech', xe, w1)) * jnp.einsum('ecd,edh->ech', xe, w3)
            out = jnp.einsum('ech,ehd->ecd', h, w2) * buf_w.reshape(E, cap, 1)
            y = jnp.zeros((N + 1, DIM), x.dtype).at[buf_tok].add(out.reshape(E * cap, DIM))[:N]
            z = jax.nn.silu(xf @ sw1) * (xf @ sw3) @ sw2
            return (y + z).reshape(shape)
        return _forward(x, wg, w1, w2, w3, sw1, sw2, sw3)

    def _L1_attn_ref(x, in_proj_w, out_proj_w, A_log, dt_bias, Dparam, ln_w, ln_b, ni_w, ni_b, no_w, no_b):
        import jax, jax.numpy as jnp
        import numpy as np
        D_MODEL = 128
        D_STATE = 64
        HEADDIM = 64
        EXPAND = 2
        D_INNER = D_MODEL * EXPAND
        NHEADS = D_INNER // HEADDIM
        D_IN_PROJ = 2 * D_INNER + 2 * D_STATE + NHEADS
        BATCH, SEQLEN = (4, 512)

        def layernorm(x, w, b, eps=1e-05):
            mu = jnp.mean(x, axis=-1, keepdims=True)
            var = jnp.mean(jnp.square(x - mu), axis=-1, keepdims=True)
            return (x - mu) * jax.lax.rsqrt(var + eps) * w + b

        def _selective_scan(x_multi, A, Bm, Cm, dt):
            Bb, L, H, P = x_multi.shape
            N = Bm.shape[-1]
            dA = jnp.minimum(jnp.exp(dt * A[None, None, :]), 0.99)

            def step(h, inp):
                x_t, B_t, C_t, dA_t = inp
                dBx = jnp.einsum('bhp,bn->bhpn', x_t, B_t)
                h = jnp.clip(dA_t[:, :, None, None] * h + dBx, -10.0, 10.0)
                y_t = jnp.einsum('bn,bhpn->bhp', C_t, h)
                return (h, y_t)
            h0 = jnp.zeros((Bb, H, P, N), dtype=x_multi.dtype)
            xs = (jnp.moveaxis(x_multi, 1, 0), jnp.moveaxis(Bm, 1, 0), jnp.moveaxis(Cm, 1, 0), jnp.moveaxis(dA, 1, 0))
            _, y = jax.lax.scan(step, h0, xs)
            return jnp.moveaxis(y, 0, 1)
        Bb, L, Dm = x.shape
        x_norm = layernorm(x, ni_w, ni_b)
        zxbcdt = jnp.einsum('bld,ed->ble', x_norm, in_proj_w)
        z = zxbcdt[..., :D_INNER]
        x_ssm = zxbcdt[..., D_INNER:2 * D_INNER]
        Bm = zxbcdt[..., 2 * D_INNER:2 * D_INNER + D_STATE]
        Cm = zxbcdt[..., 2 * D_INNER + D_STATE:2 * D_INNER + 2 * D_STATE]
        dt = zxbcdt[..., 2 * D_INNER + 2 * D_STATE:]
        dt = jnp.clip(jax.nn.softplus(dt + dt_bias[None, None, :]), 0.001, 0.1)
        A = -jnp.exp(A_log)
        x_multi = x_ssm.reshape(Bb, L, NHEADS, HEADDIM)
        y = _selective_scan(x_multi, A, Bm, Cm, dt)
        y = y + x_multi * Dparam[None, None, :, None]
        y = y.reshape(Bb, L, D_INNER)
        y = y * jax.nn.silu(z)
        y = layernorm(y, ln_w, ln_b)
        y = jnp.einsum('ble,de->bld', y, out_proj_w)
        y = jnp.clip(y, -10.0, 10.0)
        y = layernorm(y, no_w, no_b)
        return y

    def _L1_ffn_ref(hidden_states, Wp1, bp1, Wp2, bp2, W1, b1, W2, b2, Wo, bo):
        import jax, jax.numpy as jnp
        import numpy as np
        B, S, H = (8, 512, 128)
        NAV = 128
        E = 8
        F = 2 * H
        last = hidden_states[:, -1, :]
        logits = jax.nn.gelu(last @ Wp1 + bp1, approximate=False) @ Wp2 + bp2
        action_probs = jax.nn.softmax(logits, axis=-1)
        sel = jnp.argmax(action_probs, axis=-1)
        w1 = W1[sel]
        w2 = W2[sel]
        h = jax.nn.gelu(jnp.einsum('bsh,bhf->bsf', hidden_states, w1) + b1[sel][:, None, :], approximate=False)
        reasoned = jnp.einsum('bsf,bfh->bsh', h, w2) + b2[sel][:, None, :]
        out = reasoned @ Wo + bo
        return hidden_states + 0.3 * out
    x = L0_attn_x
    xn = _layernorm(x, axis=-1)
    s = _L0_attn_ref(xn, L0_attn_wq1, L0_attn_bq1, L0_attn_wk1, L0_attn_bk1, L0_attn_wv1, L0_attn_bv1, L0_attn_wo1, L0_attn_bo1, L0_attn_wq2, L0_attn_bq2, L0_attn_wk2, L0_attn_bk2, L0_attn_wv2, L0_attn_bv2, L0_attn_wo2, L0_attn_bo2, L0_attn_g1, L0_attn_be1, L0_attn_g2, L0_attn_be2, L0_attn_w_ff1, L0_attn_b_ff1, L0_attn_w_ff2, L0_attn_b_ff2, L0_attn_g_ff, L0_attn_be_ff)
    g = _silu(_L0_ffn_ref(xn, L0_ffn_wg, L0_ffn_w1, L0_ffn_w2, L0_ffn_w3, L0_ffn_sw1, L0_ffn_sw2, L0_ffn_sw3))
    x = x + s * g
    xn = _layernorm(x, axis=-1)
    s = _L1_attn_ref(xn, L1_attn_in_proj_w, L1_attn_out_proj_w, L1_attn_A_log, L1_attn_dt_bias, L1_attn_Dparam, L1_attn_ln_w, L1_attn_ln_b, L1_attn_ni_w, L1_attn_ni_b, L1_attn_no_w, L1_attn_no_b)
    g = _silu(_L1_ffn_ref(xn, L1_ffn_Wp1, L1_ffn_bp1, L1_ffn_Wp2, L1_ffn_bp2, L1_ffn_W1, L1_ffn_b1, L1_ffn_W2, L1_ffn_b2, L1_ffn_Wo, L1_ffn_bo))
    x = x + s * g
    return x

_drawn_inputs = setup_inputs


def setup_inputs(seed=0):
    import zlib

    import numpy as np

    out = dict(_drawn_inputs(seed))
    spreads = {'L0_attn_bq1': (0.0, 0.8),
     'L0_attn_bk1': (0.0, 2.0),
     'L0_attn_bv1': (0.0, 0.8),
     'L0_attn_bo1': (0.0, 0.296),
     'L0_attn_bq2': (0.0, 2.0),
     'L0_attn_bk2': (0.0, 2.0),
     'L0_attn_bv2': (0.0, 0.463),
     'L0_attn_bo2': (0.0, 0.1),
     'L0_attn_g1': (1.0, 0.2),
     'L0_attn_be1': (0.0, 0.1),
     'L0_attn_g2': (1.0, 0.2),
     'L0_attn_be2': (0.0, 0.268),
     'L0_attn_b_ff1': (0.0, 0.571),
     'L0_attn_b_ff2': (0.0, 0.1),
     'L0_attn_g_ff': (1.0, 0.2),
     'L0_attn_be_ff': (0.0, 0.1),
     'L1_attn_Dparam': (1.0, 0.2),
     'L1_attn_ln_w': (1.0, 0.2),
     'L1_attn_ln_b': (0.0, 0.1),
     'L1_attn_ni_w': (1.0, 0.2),
     'L1_attn_ni_b': (0.0, 0.1),
     'L1_attn_no_w': (1.0, 0.2),
     'L1_attn_no_b': (0.0, 0.1),
     'L1_ffn_bp1': (0.0, 0.1),
     'L1_ffn_bp2': (0.0, 0.1),
     'L1_ffn_b1': (0.0, 0.75),
     'L1_ffn_b2': (0.0, 0.534),
     'L1_ffn_bo': (0.0, 0.612)}
    factors = {'L0_attn_wq1': 8.0,
     'L0_attn_wk1': 8.0,
     'L0_attn_wv1': 8.0,
     'L0_attn_wo1': 7.898,
     'L0_attn_wq2': 64.0,
     'L0_attn_wk2': 8.0,
     'L0_attn_wv2': 22.673,
     'L0_attn_wo2': 4.621}
    for name, (base, spread) in spreads.items():
        noise = np.random.default_rng([zlib.crc32(name.encode()), seed]).standard_normal(out[name].shape)
        drawn = base * np.exp(spread * noise) if base else spread * noise
        out[name] = jnp.asarray(drawn.astype(out[name].dtype))
    for name, factor in factors.items():
        out[name] = (out[name] * factor).astype(out[name].dtype)
    return out
```

```python
from contextlib import ExitStack

import concourse.bass as bass
import numpy as np
from concourse import mybir

ALU = mybir.AluOpType
ACT = mybir.ActivationFunctionType
F32 = mybir.dt.float32
BF16 = mybir.dt.bfloat16
X_AX = mybir.AxisListType.X

P = 128
B, S, D = 2, 2048, 128
N = B * S
NT = N // P
NB = N // 512
TB = NT // NB
H, DK, DH = 8, 8, 64
G = 2 * H
UNITS = G * B
EPS = 1e-5
DI, DS, NH1, HP = 256, 64, 4, 64
E1, F1 = 8, 256
HMAX = 10.0
BOUND = 0.9 * HMAX * HMAX
GT = 16
ALPHA, BETA = 0.1, 0.1
KROWS = 9 * DK
TCH = S // P
STEPS = 2 * TCH
DFF = 512
TURN, TURNED = 7, 16
E, NG, KTOP, GTOP = 32, 8, 4, 4
NE = E + 1
CAP = int(1.25 * N * KTOP / E)
LN4, LN7, LN9 = NB, 3 * NB, 5 * NB


class Chain:

    def __init__(self, eng, sem):
        self.eng, self.sem, self.n, self.base = eng, sem, 0, 0

    def link(self, ins):
        ins.then_inc(self.sem, 1)
        self.n += 1
        self.eng.wait_ge(self.sem, self.base + self.n)


def repeat(eng, trips, body, chain=None):
    n0 = chain.n if chain else 0
    body(0)
    if trips > 1:
        per = chain.n - n0 if chain else 0
        with eng.Fori(1, trips) as j:
            if chain and per:
                chain.base = (j - 1) * per
            body(j)
        if chain and per:
            assert chain.n - n0 == 2 * per
            chain.base, chain.n = 0, n0 + trips * per


def loop_only(eng, trips, body):
    with eng.Fori(0, trips) as j:
        body(j)


def after(eng, sem, count):
    if not isinstance(count, int) or count > 0:
        eng.wait_ge(sem, count)


def layernorm_core(v, ch, src, cen, sq, mean, var, rstd, width, var_ready, std_ready, count):
    shape = list(src.shape)
    ch.link(v.tensor_reduce(mean, src, X_AX, ALU.add))
    ch.link(v.tensor_scalar(mean, mean, 1.0 / width, None, ALU.mult))
    ch.link(v.tensor_tensor(cen, src, mean.unsqueeze(2).broadcast_to(shape), ALU.subtract))
    ch.link(v.tensor_tensor(sq, cen, cen, ALU.mult))
    ch.link(v.tensor_reduce(var, sq, X_AX, ALU.add))
    v.tensor_scalar(var, var, 1.0 / width, EPS, ALU.mult, ALU.add).then_inc(var_ready, 1)
    v.wait_ge(std_ready, count)
    ch.link(v.reciprocal(rstd, rstd))


def build(nc, a, out):
    x_v = a["x"].rearrange("b (t p) d -> p (b t) d", p=P)
    out_v = out.rearrange("b (t p) d -> p (b t) d", p=P)

    with ExitStack() as ctx:
        def sb(name, shape, dt=F32):
            return ctx.enter_context(nc.sbuf_tensor(name, shape, dt))

        def sem(name):
            return ctx.enter_context(nc.semaphore(name))

        def dram(name, shape, dt=F32):
            return nc.dram_tensor(name, shape, dt, kind="Internal").ap()

        xnt_d = dram("xnt_d", (P, N))
        xn_d = dram("xn_d", (N, D))
        xct_d = dram("xct_d", (P, N))
        ql_d = dram("ql_d", (3, P, N), BF16)
        kl_d = dram("kl_d", (3, P, N), BF16)
        zs_d = dram("zs_d", (N, DI))
        xs_d = dram("xs_d", (N, DI))
        b_d = dram("b_d", (N, DS))
        bt_d = dram("bt_d", (DS, N))
        ct_d = dram("ct_d", (DS, N))
        lda_d = dram("lda_d", (N, NH1))
        y_d = dram("y_d", (N, DI))
        o_d = dram("o_d", (2, G, 2 * DK, N))

        PS = ctx.enter_context(nc.psum_tensor("PS", [P, 7, 512], F32))
        PT = ctx.enter_context(nc.psum_tensor("PT", [P, 1024], BF16))

        X = sb("X", [P, NT, D])
        ident = sb("ident", [P, P])
        identb = sb("identb", [P, P], BF16)
        cst = sb("cst", [P, a["consts"].shape[1]])
        rows = sb("rows", [P, a["rowc"].shape[1]])
        wsq = sb("wsq", [P, 4, P])
        wff1 = sb("wff1", [P, DFF])
        wff2 = sb("wff2", [P, DFF // P, D])
        bcol = sb("bcol", [P, a["bcol"].shape[1]])
        brow = sb("brow", [1, a["brow"].shape[1]])
        affine = sb("affine", [P, a["affine"].shape[0], P])
        ones1 = sb("ones1", [1, P])
        wgT = sb("wgT", [P, E])
        S0 = sb("S0", [P, NT, D])
        VP = sb("VP", [P, NT, P])

        XNT = sb("XNT", [P, N])
        YM = sb("YM", [P, NT, D])
        EW = [sb(f"EW{i}", [P, 3, P]) for i in range(3)]
        SG = [sb(f"SG{i}", [P, 512]) for i in range(2)]
        HH = [sb(f"HH{i}", [P, 512]) for i in range(2)]
        wcol = [sb(f"wcol{i}", [P, NT]) for i in range(3)]
        onesq = sb("onesq", [P, P])
        io = sb("io", [P, E])
        ltg = sb("ltg", [P, NG, NG])
        WT = sb("WT", [P, NT, NE])
        gs = sb("gs", [P, 3, NT])
        gmx = sb("gmx", [P, NT, NG])

        wa = [sb(f"wa{i}", [P, TB, P]) for i in range(6)]
        st = sb("st", [P, 3, 8])

        stacks = sb("stacks", [P, 8 * S], BF16)
        QS = [stacks[:, i * S:(i + 1) * S] for i in range(4)]
        KS = [stacks[:, (4 + i) * S:(5 + i) * S] for i in range(4)]
        VH = [sb(f"VH{i}", [P, TCH, 32]) for i in range(4)]
        probs = sb("probs", [P, 4 * 1024])
        PR = [probs[:, i * 1024:(i + 1) * 1024] for i in range(4)]
        gt = [stacks[:, i * S:(i + 1) * S].bitcast(F32).rearrange("p (t e) -> p t e", e=E) for i in range(6)]
        gcmp = [probs[:, i * 2048:(i + 1) * 2048].rearrange("p (t g q) -> p t g q", g=NG, q=NG) for i in range(2)]
        XN2 = S0
        S2 = YM
        YS = stacks[:, :].bitcast(F32).rearrange("p (t c) -> p t c", c=DI)
        bs = [sb(f"bs{i}", [P, B, DS]) for i in range(2)]
        DT = sb("DT", [P, NT, NH1])
        dtt = sb("dtt", [P, 2, NT, NH1])
        alog = sb("alog", [P, 3, NH1])
        win = sb("win", [P, 2 * DI + DS + NH1 + DS])
        wout = sb("wout", [P, 2, D])
        sc_aff = sb("sc_aff", [P, 3, DI])
        lb, DE, DM, MM0 = (VP[:, 8 * i:8 * i + 8, :] for i in range(4))
        MM = [MM0, YM[:, 0:8, :]]
        heads = lambda t: t.rearrange("p (b h t) -> p b h t", b=B, h=NH1)
        ym_flat, head_cols = YM.rearrange("p t c -> p (t c)"), B * NH1 * P
        E2 = [heads(probs[0:DS, 0:head_cols]), heads(ym_flat[0:DS, 2560:2560 + head_cols])]
        CTD = [[probs[0:DS, 1024 + b * 512:1536 + b * 512].rearrange("p (h t) -> p h t", h=NH1) for b in range(B)],
               [wa[b][0:DS, :, :] for b in range(B)]]
        E2b = [heads(wa[2 + i].rearrange("p t c -> p (t c)")[0:DS, :].bitcast(BF16)) for i in range(2)]
        RB = [heads(probs[:, 2048 + i * 512:2560 + i * 512].bitcast(BF16)) for i in range(2)]
        DMb = [ym_flat[:, 1024 + i * 512:1536 + i * 512].bitcast(BF16).rearrange("p (i t) -> p i t", t=P) for i in range(2)]
        BD = [heads(t) for t in (probs[:, 3072:3584], ym_flat[:, 2048:2560])]
        ldc = sb("ldc", [P, B, NH1])
        nls = sb("nls", [P, B * NH1])
        HS = sb("HS", [DS, B, NH1, HP])
        hst2 = sb("hst2", [DS, B, NH1, HP])
        VR = sb("VR", [DS, NH1, P], BF16)
        VS = PT[:, :].bitcast(F32).rearrange("p (h t) -> p h t", h=NH1)
        nmx2 = dtt[:, 0, :, :]
        MXV = sb("MXV", [P, B, TCH, 2 * NH1])
        FW1 = stacks[:, :].bitcast(F32)[:, 0:E1 * (2 * F1 + 3)].rearrange("p (e c) -> p e c", e=E1)
        SW1 = [sb(f"SW1_{b}", [P, 2 * F1 + 3]) for b in range(B)]
        wp = sb("wp", [P, P + 1 + E1])
        wo1 = sb("wo1", [P, D])
        r1 = sb("r1", [1, E1 + D])
        io1 = sb("io1", [1, E1])
        lg1 = sb("lg1", [1, 4, B, E1])
        s1_ = sb("s1_", [1, 2, B])
        hn = sb("hn", [P, B])
        oh = sb("oh", [P, B * E1])

        OE = SG
        mxp = sb("mxp", [P, TCH, 4])
        nmx = sb("nmx", [P, 2, TCH])
        spl = sb("spl", [P, P // TCH, TCH], BF16)
        mT = sb("mT", [3 * TCH, P], BF16)

        vp_flat = VP.rearrange("p t c -> p (t c)")
        wb = [vp_flat[:, i * 512:(i + 1) * 512].rearrange("p (t c) -> p t c", t=2) for i in range(3)]
        ylT = vp_flat[:, 1536:2048]
        hx = bs
        hst = sb("hst", [2, B, DH])
        hout = [HH[i][0:DH, 0:B * P].rearrange("p (b s) -> p b s", b=B) for i in range(2)]

        dve_chain, act_chain = sem("dve_chain"), sem("act_chain")
        ch = Chain(nc.vector, dve_chain)

        c_ld, x_ld = sem("c_ld"), sem("x_ld")
        ones_set = sem("ones_set")
        var_ready, std_ready = sem("var_ready"), sem("std_ready")
        xn_ready, xnT_ready, xnT_out = sem("xn_ready"), sem("xnT_ready"), sem("xnT_out")
        xn_st, xnt_st = sem("xn_st"), sem("xnt_st")
        hx_ld = [sem("hx_ld0"), sem("hx_ld1")]
        hst_ld, h_state, h_out = (sem(n) for n in ("hst_ld", "h_state", "h_out"))
        h_st = [sem("h_st0"), sem("h_st1")]
        xc_ld, qk_ready, v_ready, q_out, k_out, v_out, qs_ready, ks_ready = (
            sem(n) for n in ("xc_ld", "qk_ready", "v_ready", "q_out", "k_out", "v_out", "qs_ready", "ks_ready"))
        ql_st, kl_st = sem("ql_st"), sem("kl_st")
        qk_ld = [sem(f"qk_ld{i}") for i in range(4)]
        m_ld = [sem(f"m_ld{i}") for i in range(4)]
        vh_ready, mxs_ready, mx_done, spl_ready, mt_ready, mt_out = (
            sem(n) for n in ("vh_ready", "mxs_ready", "mx_done", "spl_ready", "mt_ready", "mt_out"))
        sc_ready, exp_done, pv_done, o_evac = (
            sem(n) for n in ("sc_ready", "exp_done", "pv_done", "o_evac"))
        oe_st = [sem("oe_st0"), sem("oe_st1")]
        at_ld, at_sum, r_ready, y_ready, yT_ready, yT_out, f_ready, f_out, ff_ready, at_free = (
            sem(n) for n in ("at_ld", "at_sum", "r_ready", "y_ready", "yT_ready", "yT_out",
                             "f_ready", "f_out", "ff_ready", "at_free"))
        sp_passed = sem("sp_passed")
        out_st = sem("out_st")
        clip_chain = sem("clip_chain")
        h_zero, h_level, h_carried, vh_set = sem("h_zero"), sem("h_level"), sem("h_carried"), sem("vh_set")
        GROUPS = UNITS // 4
        (xn2_ready, xn2T_ready, xn2T_out, xnn_ready, xnnT_ready, xnnT_out, bct_ready, bct_out, bct_st, zx_ready, zx_out,
         bd_ready, bd_out) = (sem(n) for n in ("xn2_ready", "xn2T_ready", "xn2T_out", "xnn_ready", "xnnT_ready",
         "xnnT_out", "bct_ready", "bct_out", "bct_st", "zx_ready", "zx_out", "bd_ready", "bd_out"))
        zx_st = [sem("zx_st0"), sem("zx_st1")]
        b_st = [sem("b_st0"), sem("b_st1")]
        dt_step, dt_act, w1_ld = (sem(n) for n in ("dt_step", "dt_act", "w1_ld"))
        c_ld8 = [sem("c_ld8_0"), sem("c_ld8_1")]
        lb_set, la_ready, dif_done, d_done, el_done, dm_done, opb_ready, vr_out, ops_ready, c_done, y_out, hs_done = (
            sem(n) for n in ("lb_set", "la_ready", "dif_done", "d_done", "el_done", "dm_done", "opb_ready", "vr_out", "ops_ready", "c_done", "y_out", "hs_done"))
        bnd_read = sem("bnd_read")
        okv = sb("okv", [P, 1])
        flag = sb("flag", [1, 1], mybir.dt.int32)
        g_x = VP.rearrange("p t c -> p (t c)").rearrange("p (t c) -> p t c", c=DI)
        g_hc = probs.rearrange("p (t c) -> p t c", c=DI)
        g_y = YM.rearrange("p t c -> p (t c)")[0:B, :]
        g_b, g_c = HH[0][:, 0:GT], HH[0][:, GT:2 * GT]
        g_dec = HH[1][:, 0:GT * NH1].rearrange("p (t h) -> p t h", h=NH1)
        g_h = wa[5].rearrange("p t c -> p (t c)")[:, 0:DI].rearrange("p (h q) -> p h q", h=NH1)
        ok_ready, cnt1_ready, flag_set, lda_st, g_ld, g_dec_done, g_hc_done, g_mm, g_y_out, g_st, g_back = (
            sem(n) for n in ("ok_ready", "cnt1_ready", "flag_set", "lda_st", "g_ld", "g_dec_done", "g_hc_done", "g_mm", "g_y_out",
                             "g_st", "g_back"))
        z_ld, fw_ld = sem("z_ld"), sem("fw_ld")
        yl_ready, ylT_ready, ylT_out, pr_ready, s2_done = (
            sem(n) for n in ("yl_ready", "ylT_ready", "ylT_out", "pr_ready", "s2_done"))
        a1_ready, a1_out, l1_ready, l1_max, l1_exp, oh_ready, ohb_ready, sel1_done = (
            sem(n) for n in ("a1_ready", "a1_out", "l1_ready", "l1_max", "l1_exp", "oh_ready", "ohb_ready", "sel1_done"))
        fh_ready, fh_out, rt_ready, rt_out, fo_ready, gin_ready, g_ready, fin_ready = (
            sem(n) for n in ("fh_ready", "fh_out", "rt_ready", "rt_out", "fo_ready", "gin_ready", "g_ready", "fin_ready"))
        TRI = cst[:, P + 2:2 * P + 2]

        def aff1(i):
            return affine[:, 4 + i, :].unsqueeze(1).broadcast_to([P, TB, P])
        xnt_ld, lg_ready, lg_out, lmx, lexp, sel_done, cnt_ready, wt_done = (
            sem(n) for n in ("xnt_ld", "lg_ready", "lg_out", "lmx", "lexp", "sel_done", "cnt_ready", "wt_done"))
        ew_ld = [sem(f"ew_ld{i}") for i in range(3)]
        mh_ready, sg_done, hh_done, mo_ready, ym_done, ym_all, g_done, x1_done = (
            sem(n) for n in ("mh_ready", "sg_done", "hh_done", "mo_ready", "ym_done", "ym_all", "g_done", "x1_done"))
        FH = PR
        CONSTS = [(ident[:, :], "ident"), (cst[:, :], "consts"), (rows[:, :], "rowc"),
                  (wff1[:, :], "wff1"), (bcol[:, :], "bcol"), (brow[:, :], "brow"), (wsq[:, :, :], "wsq"),
                  (wff2[:, :, :], "wff2"), (ones1[:, :], "ones"),
                  (onesq[:, :], "onesq"), (wgT[:, :], "wgT")]
        CONSTS1 = [(win[:, :], "win"), (wout[:, :, :], "wout"), (wp[:, :], "wp"), (wo1[:, :], "wo1"),
                   (r1[:, :], "r1"), (io1[:, :], "io1")]
        NCONST1 = len(CONSTS1) + 2
        NCONST = len(CONSTS) + 3

        def f_(t):
            return t.rearrange("p t c -> p (t c)")

        def aff(i):
            return affine[:, i, :].unsqueeze(1).broadcast_to([P, TB, P])

        block = ctx.enter_context(nc.Block())

        def load_expert(sp, hold, e, w):
            hold(mo_ready, NB * (e - 2))
            sp.dma_start(EW[w][:, :, :], a["ew"][bass.ds(e, 1)].rearrange("o p m c -> (o p) m c")).then_inc(ew_ld[w], 16)

        @block.sync
        def _(sp):
            def hold(sem_, count):
                after(sp, sem_, count)
                if not isinstance(count, int):
                    sp.sem_inc(sp_passed, 1)

            sp.dma_start(X[:, :, :], x_v).then_inc(x_ld, 16)
            for dst, src in CONSTS:
                sp.dma_start(dst, a[src]).then_inc(c_ld, 16)
            sp.dma_start(io[:, :], a["io"].partition_broadcast(P)).then_inc(c_ld, 16)
            sp.dma_start(ltg[:, :, :], a["ltg"].partition_broadcast(P)).then_inc(c_ld, 16)
            sp.dma_start(affine[:, :, :], a["affine"].partition_broadcast(P)).then_inc(c_ld, 16)

            def store_xn(j):
                hold(xn_ready, j + 1)
                sp.dma_start(xn_d.rearrange("(t p) d -> p t d", p=P)[:, bass.ds(j * TB, TB), :], wa[1][:, :, :]).then_inc(xn_st, 16)
                hold(xnT_out, j + 1)
                sp.dma_start(xnt_d[:, bass.ds(j * 512, 512)], f_(wa[2])).then_inc(xnt_st, 16)
                sp.dma_start(xct_d[0:DH, bass.ds(j * 512, 512)], f_(wa[2])[0:DH]).then_inc(xnt_st, 16)
            repeat(sp, NB, store_xn)

            hold(xn_st, 16 * NB)
            hold(xnt_st, 32 * NB)
            hold(h_zero, 1)
            xnb = xn_d.rearrange("(b s) d -> s b d", b=B)
            sp.dma_start(hst[0:1, :, :], xnb[0:1, :, 0:DH]).then_inc(hst_ld, 16)

            def holt_tiles(j):
                for w in range(2):
                    t = 2 * j + w
                    hold(h_state, t - 1)
                    sp.dma_start(hx[w][:, :, :], xnb[bass.ds(t * P, P), :, 0:DH]).then_inc(hx_ld[w], 16)
                for w in range(2):
                    t = 2 * j + w
                    hold(h_out, t + 1)
                    sp.dma_start(xct_d.rearrange("d (b s) -> d b s", b=B)[DH:P, :, bass.ds(t * P, P)],
                                 hout[w][:, :, :]).then_inc(h_st[w], 16)
            repeat(sp, TCH // 2, holt_tiles)
            for w in range(2):
                hold(h_st[w], 16 * (TCH // 2))

            def qkv_block(j):
                hold(v_ready, j)
                sp.dma_start(f_(wa[0]), xct_d[:, bass.ds(j * 512, 512)]).then_inc(xc_ld, 16)
                for parts, src, ready, stored in ((ql_d, QS, qs_ready, ql_st), (kl_d, KS, ks_ready, kl_st)):
                    hold(ready, j + 1)
                    for lv in range(3):
                        sp.dma_start(parts[lv, :, bass.ds(j * 512, 512)], src[lv][:, 0:512]).then_inc(stored, 16)
            repeat(sp, NB, qkv_block)
            hold(ql_st, 48 * NB)
            hold(kl_st, 48 * NB)
            hold(ones_set, 8)

            def load_unit(u, g, b, w):
                hold(pv_done, TCH * (u - 3))
                for r in range(3):
                    q_src = ql_d[r, bass.ds(g * DK, DK), b * S:(b + 1) * S].unsqueeze(0).broadcast_to([3, DK, S])
                    sp.dma_start(QS[w][24 * r:24 * r + 24, :], q_src).then_inc(qk_ld[w], 16)
                    k_src = kl_d[:, bass.ds(g * DK, DK), b * S:(b + 1) * S]
                    sp.dma_start(KS[w][24 * r:24 * r + 24, :], k_src).then_inc(qk_ld[w], 16)

            def store_half(u, g, b, half):
                hold(o_evac, 2 * u + half + 1)
                for jg in range(4):
                    col = b * S + half * 1024 + (jg % 2) * 512
                    sp.dma_start(o_d[jg // 2, bass.ds(g, 1), :, col:col + 512],
                                 OE[half][32 * jg:32 * jg + 16, :]).then_inc(oe_st[half], 16)

            for u in range(4):
                load_unit(u, u // 2, u % 2, u)

            def load_max(u, w):
                hold(mt_out, u + 1)
                sp.dma_start(QS[w][KROWS:KROWS + 3, :], mT[:, :]).then_inc(m_ld[w], 16)

            load_max(0, 0)

            def group(k, last=False):
                for w in range(4):
                    u, g = 4 * k + w, 2 * k + w // 2
                    if not (last and w == 3):
                        load_max(u + 1, (w + 1) % 4)
                    store_half(u, g, w % 2, 0)
                    store_half(u, g, w % 2, 1)
                    if not last:
                        load_unit(u + 4, g + 2, w % 2, w)
            repeat(sp, GROUPS - 1, group)
            group(GROUPS - 1, True)
            for half in range(2):
                hold(oe_st[half], 64 * UNITS)

            def attn_block(j):
                hold(at_free, j)
                c = bass.ds(j * 512, 512)
                for i in range(4):
                    sp.dma_start(f_(wa[i]), o_d[i % 2, :, (i // 2) * DK:(i // 2 + 1) * DK, c]).then_inc(at_ld, 16)
                sp.dma_start(f_(wa[4]), xct_d[:, c]).then_inc(at_ld, 16)
            repeat(sp, NB, attn_block)
            hold(at_free, NB)
            sp.dma_start(XNT[:, :], xnt_d).then_inc(xnt_ld, 16)
            for e in range(3):
                load_expert(sp, hold, e, e)

            def experts(k):
                for w in range(3):
                    load_expert(sp, hold, 3 * k + w + 3, w)
            repeat(sp, NE // 3 - 1, experts)
            for dst, src in CONSTS1:
                sp.dma_start(dst, a[src]).then_inc(w1_ld, 16)
            sp.dma_start(alog[:, 0:2, :], a["alog"].partition_broadcast(P)).then_inc(w1_ld, 16)
            sp.dma_start(sc_aff[:, :, :], a["sc_aff"].partition_broadcast(P)).then_inc(w1_ld, 16)

            def store_proj(j):
                hold(bct_out, 2 * j + 2)
                sp.dma_start(bt_d[:, bass.ds(j * 512, 512)], HH[0][0:DS, :]).then_inc(bct_st, 16)
                sp.dma_start(ct_d[:, bass.ds(j * 512, 512)], HH[1][0:DS, :]).then_inc(bct_st, 16)
                for t in range(TB):
                    tok = bass.ds((TB * j + t) * P, P)
                    hold(zx_out, 2 * (TB * j + t) + 2)
                    sp.dma_start(zs_d[tok, :], SG[t % 2][:, 0:DI]).then_inc(zx_st[t % 2], 16)
                    sp.dma_start(xs_d[tok, :], SG[t % 2][:, DI:2 * DI]).then_inc(zx_st[t % 2], 16)
                    hold(bd_out, TB * j + t + 1)
                    sp.dma_start(b_d[tok, :], bs[t % 2][:, 0, :]).then_inc(b_st[t % 2], 16)
            repeat(sp, NB, store_proj)
            hold(bct_st, 32 * NB)
            for w in range(2):
                hold(zx_st[w], 32 * NT // 2)
                hold(b_st[w], 16 * NT // 2)

            def load_chunk(k):
                for w in range(2):
                    c = 2 * k + w
                    hold(c_done, c - 1)
                    tok = bass.ds(c * P, P)
                    bview = lambda d: d.rearrange("(b s) n -> s b n", b=B)[tok]
                    tview = lambda d: d.rearrange("n (b s) -> n b s", b=B)[:, :, tok]
                    sp.dma_start(SG[w].rearrange("p (b n) -> p b n", b=B), bview(xs_d)).then_inc(c_ld8[w], 16)
                    sp.dma_start(bs[w][:, :, :], bview(b_d)).then_inc(c_ld8[w], 16)
                    sp.dma_start(HH[w][0:DS, 0:256].rearrange("p (b s) -> p b s", b=B), tview(bt_d)).then_inc(c_ld8[w], 16)
                    sp.dma_start(HH[w][0:DS, 256:512].rearrange("p (b s) -> p b s", b=B), tview(ct_d)).then_inc(c_ld8[w], 16)
            repeat(sp, TCH // 2, load_chunk)
            hold(hs_done, TCH)

            hold(flag_set, 1)
            with sp.If(sp.value_load(flag[:, :], min_val=0, max_val=1) > 0):
                sp.dma_start(lda_d.rearrange("(t p) h -> p t h", p=P), DT[:, :, :]).then_inc(lda_st, 16)
                hold(lda_st, 16)

                def clip_io(k):
                    hold(g_hc_done, k)
                    hold(g_mm, 2 * k)
                    for b in range(B):
                        tok = bass.ds(k * GT + b * S, GT)
                        rows_ = slice(b * DS, (b + 1) * DS)
                        sp.dma_start(g_x[rows_], xs_d[tok, :].partition_broadcast(DS)).then_inc(g_ld, 16)
                        sp.dma_start(g_b[rows_], bt_d[:, tok]).then_inc(g_ld, 16)
                        sp.dma_start(g_c[rows_], ct_d[:, tok]).then_inc(g_ld, 16)
                        sp.dma_start(g_dec[rows_], lda_d[tok, :].partition_broadcast(DS)).then_inc(g_ld, 16)
                    hold(g_y_out, 2 * k + 2)
                    for b in range(B):
                        sp.dma_start(y_d[bass.ds(k * GT + b * S, GT), :].rearrange("t c -> (t c)").unsqueeze(0), g_y[b:b + 1, :]).then_inc(g_st, 16)
                repeat(sp, S // GT, clip_io)
                hold(g_st, 16 * B * S // GT)
                sp.dma_start(YS, y_d.rearrange("(t p) c -> p t c", p=P)).then_inc(g_back, 16)
                hold(g_back, 16)

            def load_gate(k):
                hold(yl_ready, k)
                tiles = bass.ds(2 * k, 2)
                sp.dma_start(SG[0].rearrange("p (t c) -> p t c", t=2), xs_d.rearrange("(t p) c -> p t c", p=P)[:, tiles, :]).then_inc(z_ld, 16)
                sp.dma_start(SG[1].rearrange("p (t c) -> p t c", t=2), zs_d.rearrange("(t p) c -> p t c", p=P)[:, tiles, :]).then_inc(z_ld, 16)
            repeat(sp, NT // 2, load_gate)
            hold(s2_done, NT // 2)
            sp.dma_start(FW1, a["ew1"]).then_inc(fw_ld, 16)
            def store_out(j):
                hold(fin_ready, j + 1)
                sp.dma_start(out_v[:, bass.ds(TB * j, TB), :], X[:, bass.ds(TB * j, TB), :]).then_inc(out_st, 16)
            repeat(sp, NB, store_out)
            hold(out_st, 16 * NB)

        @block.vector
        def _(v):
            link = ch.link
            link(v.memset(spl[:, :, :], 0.0))
            v.memset(hst[:, :, :], 0.0).then_inc(h_zero, 1)
            v.wait_ge(x_ld, 16)
            v.wait_ge(c_ld, 16 * NCONST)
            link(v.tensor_copy(identb[:, :], ident[:, :]))

            def ln_x(j):
                after(v, xnT_ready, j)
                layernorm_core(v, ch, X[:, bass.ds(j * TB, TB), :], wa[0][:, :, :], wa[3][:, :, :], st[:, 0, 0:TB], st[:, 1, 0:TB],
                               st[:, 2, 0:TB], D, var_ready, std_ready, j + 1)
                after(v, xn_st, 16 * j)
                v.tensor_tensor(wa[1][:, :, :], wa[0][:, :, :], st[:, 2, 0:TB].unsqueeze(2).broadcast_to([P, TB, P]), ALU.mult).then_inc(xn_ready, 1)
                v.wait_ge(xn_ready, j + 1)
            repeat(v, NB, ln_x, ch)

            def carry(t):
                v.wait_ge(h_state, t + 1)
                v.tensor_copy(hst[:, :, :], PS[0:2, 4, 0:P].rearrange("p (b d) -> p b d", b=B)).then_inc(h_carried, 1)
            repeat(v, TCH, carry)

            def split_qk(j):
                for full, evacuated, parts, ready, stored in ((wa[1], q_out, QS, qs_ready, ql_st), (wa[2], k_out, KS, ks_ready, kl_st)):
                    f = f_(full)
                    v.wait_ge(evacuated, j + 1)
                    after(v, stored, 48 * j)
                    link(v.tensor_copy(parts[0][:, 0:512], f))
                    link(v.tensor_tensor(f, f, parts[0][:, 0:512], ALU.subtract))
                    link(v.tensor_copy(parts[1][:, 0:512], f))
                    link(v.tensor_tensor(f, f, parts[1][:, 0:512], ALU.subtract))
                    v.tensor_copy(parts[2][:, 0:512], f).then_inc(ready, 1)
            repeat(v, NB, split_qk, ch)

            def write_rows(uu, slot, trip):
                v.wait_ge(mt_ready, uu + 1)
                if slot > 0:
                    v.wait_ge(m_ld[slot - 1], 16 * (trip + 1))
                else:
                    after(v, m_ld[3], 16 * trip)
                v.tensor_copy(mT[:, :], PT[0:3 * TCH, 0:P]).then_inc(mt_out, 1)

            def unit_max(uu, slot, trip):
                for n in range(4 * TCH):
                    v.wait_ge(mxs_ready, 4 * TCH * uu + n + 1)
                    v.tensor_reduce(mxp[:, n // 4, n % 4:n % 4 + 1], PS[:, 5 + n % 2, :], X_AX, ALU.max).then_inc(mx_done, 1)
                    if n == TURNED - 1 and not (slot == 0 and isinstance(uu, int)):
                        write_rows(uu - 1, (slot - 1) % 4, trip - (slot == 0))
                v.wait_ge(mx_done, 4 * TCH * (uu + 1))
                link(v.tensor_reduce(nmx[:, 0, :], mxp[:, :, :], X_AX, ALU.max, negate=True))
                if not (slot == 0 and isinstance(uu, int)):
                    v.wait_ge(mt_ready, uu)
                link(v.tensor_copy(spl[:, 0, :], nmx[:, 0, :]))
                link(v.tensor_tensor(nmx[:, 1, :], nmx[:, 0, :], spl[:, 0, :], ALU.subtract))
                link(v.tensor_copy(spl[:, 1, :], nmx[:, 1, :]))
                link(v.tensor_tensor(nmx[:, 0, :], nmx[:, 1, :], spl[:, 1, :], ALU.subtract))
                v.tensor_copy(spl[:, 2, :], nmx[:, 0, :]).then_inc(spl_ready, 1)

            def group_max(k):
                for w in range(4):
                    unit_max(4 * k + w, w, k)
            repeat(v, GROUPS, group_max, ch)
            write_rows(UNITS - 1, 3, GROUPS - 1)

            def finish_attn(j):
                f = [f_(w_) for w_ in wa]
                v.wait_ge(at_ld, 80 * (j + 1))
                link(v.tensor_tensor(f[0], f[0], f[1], ALU.add))
                link(v.tensor_tensor(f[2], f[2], f[3], ALU.add))
                link(v.reciprocal(f[2], f[2]))
                v.tensor_tensor(f[0], f[0], f[2], ALU.mult).then_inc(at_sum, 1)
                v.wait_ge(r_ready, j + 1)
                half = PS[:, 0, :].rearrange("p (t d) -> p t d", d=DH)
                w8 = [wa[i].rearrange("p t (m d) -> p (t m) d", d=DH) for i in range(6)]
                layernorm_core(v, ch, half, w8[1], w8[2], st[:, 0, :], st[:, 1, :], st[:, 2, :], DH, var_ready, std_ready, LN4 + 2 * j + 1)
                link(v.tensor_tensor(w8[1], w8[1], st[:, 2, :].unsqueeze(2).broadcast_to([P, 2 * TB, DH]), ALU.mult))
                link(v.tensor_tensor(wa[1][:, :, :], wa[1][:, :, :], aff(0), ALU.mult))
                v.tensor_tensor(wa[1][:, :, :], wa[1][:, :, :], aff(1), ALU.add).then_inc(y_ready, 1)
                v.wait_ge(ff_ready, j + 1)
                z = PS[:, 0, :].rearrange("p (t d) -> p t d", d=D)
                layernorm_core(v, ch, z, wa[1][:, :, :], wa[2][:, :, :], st[:, 0, 0:TB], st[:, 1, 0:TB], st[:, 2, 0:TB], D, var_ready, std_ready, LN4 + 2 * j + 2)
                link(v.tensor_tensor(wa[1][:, :, :], wa[1][:, :, :], st[:, 2, 0:TB].unsqueeze(2).broadcast_to([P, TB, P]), ALU.mult))
                link(v.tensor_tensor(wa[1][:, :, :], wa[1][:, :, :], aff(2), ALU.mult))
                v.tensor_tensor(S0[:, bass.ds(j * TB, TB), :], wa[1][:, :, :], aff(3), ALU.add).then_inc(at_free, 1)
            repeat(v, NB, finish_attn, ch)

            v.memset(YM[:, :, :], 0.0).then_inc(ym_all, 1)
            v.wait_ge(lg_out, 1)
            L, SC, M, T1, T2, SEL = (t[:, :, :] for t in gt)
            tok = lambda col: col.unsqueeze(2).broadcast_to([P, NT, E])
            exps = io[:, :].unsqueeze(1).broadcast_to([P, NT, E])
            s0, s1 = gs[:, 0, :], gs[:, 1, :]
            link(v.tensor_reduce(s0, L, X_AX, ALU.max))
            v.tensor_tensor(L, L, tok(s0), ALU.subtract).then_inc(lmx, 1)
            v.wait_ge(lexp, 1)
            link(v.tensor_reduce(s0, SC, X_AX, ALU.add))
            link(v.reciprocal(s0, s0))
            link(v.tensor_tensor(SC, SC, tok(s0), ALU.mult))
            GM = gmx[:, :, :]
            link(v.tensor_reduce(GM.rearrange("p t g -> p (t g)"), SC.rearrange("p t (g q) -> p (t g) q", g=NG), X_AX, ALU.max))
            other = GM.unsqueeze(2).broadcast_to([P, NT, NG, NG])
            own = GM.unsqueeze(3).broadcast_to([P, NT, NG, NG])
            c0, c1 = gcmp[0][:, :, :, :], gcmp[1][:, :, :, :]
            link(v.tensor_tensor(c0, other, own, ALU.is_gt))
            link(v.tensor_tensor(c1, other, own, ALU.is_equal))
            flat = lambda c: c.rearrange("p t g q -> p t (g q)")
            link(v.tensor_tensor(flat(c1), flat(c1), ltg.rearrange("p g q -> p (g q)").unsqueeze(1).broadcast_to([P, NT, NG * NG]), ALU.mult))
            link(v.tensor_tensor(flat(c0), flat(c0), flat(c1), ALU.add))
            link(v.tensor_reduce(GM.rearrange("p t g -> p (t g)"), c0.rearrange("p t g q -> p (t g) q"), X_AX, ALU.add))
            link(v.tensor_scalar(GM, GM, GTOP - 0.5, None, ALU.is_lt))
            keep = GM.rearrange("p t g -> p (t g)").unsqueeze(2).broadcast_to([P, NT * NG, E // NG])
            g4 = lambda t: t.rearrange("p t (g q) -> p (t g) q", g=NG)
            link(v.tensor_tensor(g4(M), g4(SC), keep, ALU.mult))
            link(v.tensor_scalar(g4(T1), keep, 2.0, -2.0, ALU.mult, ALU.add))
            link(v.tensor_tensor(M, M, T1, ALU.add))
            link(v.memset(SEL, 0.0))
            for _ in range(KTOP):
                link(v.tensor_reduce(s0, M, X_AX, ALU.max))
                link(v.tensor_tensor(T1, M, tok(s0), ALU.is_equal))
                link(v.tensor_tensor(T1, T1, exps, ALU.mult))
                link(v.tensor_reduce(s1, T1, X_AX, ALU.min))
                link(v.tensor_tensor(T2, exps, tok(s1), ALU.is_equal))
                link(v.tensor_tensor(SEL, SEL, T2, ALU.add))
                link(v.scalar_tensor_tensor(T2.rearrange("p t e -> p (t e)"), T2.rearrange("p t e -> p (t e)"), -4.0, M.rearrange("p t e -> p (t e)"), ALU.mult, ALU.add))
                link(v.tensor_copy(M, T2))
            v.sem_inc(sel_done, 1)
            link(v.tensor_tensor(SC, SC, SEL, ALU.mult))
            link(v.tensor_reduce(s0, SC, X_AX, ALU.add))
            link(v.tensor_scalar(s0, s0, 1e-9, None, ALU.add))
            link(v.reciprocal(s0, s0))
            link(v.tensor_tensor(SC, SC, tok(s0), ALU.mult))
            v.wait_ge(cnt_ready, 1)
            bank = lambda i: PS[:, i:i + 2, :].rearrange("p a (t e) -> p (a t) e", e=E)
            link(v.tensor_copy(T1, bank(2)))
            src, dst = T1, T2
            step = 1
            while step < NT:
                link(v.tensor_copy(dst[:, 0:step, :], src[:, 0:step, :]))
                link(v.tensor_tensor(dst[:, step:NT, :], src[:, step:NT, :], src[:, 0:NT - step, :], ALU.add))
                src, dst, step = dst, src, 2 * step
            link(v.tensor_copy(M, bank(0)))
            link(v.tensor_tensor(M[:, 1:NT, :], M[:, 1:NT, :], src[:, 0:NT - 1, :], ALU.add))
            link(v.tensor_scalar(M, M, CAP + 0.5, None, ALU.is_lt))
            link(v.memset(WT[:, :, E:NE], 1.0))
            v.tensor_tensor(WT[:, :, 0:E], SC, M, ALU.mult).then_inc(wt_done, 1)
            v.wait_ge(wt_done, 1)

            def weighted(q, w, j):
                v.wait_ge(mo_ready, q + 1)
                for t in range(TB):
                    ins = v.scalar_tensor_tensor(YM[:, TB * j + t, :], PS[:, 4 + j % 2, t * P:(t + 1) * P], wcol[w][:, TB * j + t:TB * j + t + 1],
                                                 YM[:, TB * j + t, :], ALU.mult, ALU.add)
                ins.then_inc(ym_done, 1)

            def experts(k):
                for w in range(3):
                    e = 3 * k + w
                    if w == 0:
                        after(v, ym_done, NB * (e - 2))
                    link(v.tensor_copy(wcol[w][:, :].unsqueeze(2), WT[:, :, bass.ds(e, 1)]))
                    for j in range(NB):
                        q = NB * e + j
                        v.wait_ge(sg_done, q + 1)
                        after(v, mo_ready, q - 1)
                        v.tensor_tensor(HH[j % 2][:, :], SG[j % 2][:, :], PS[:, 2 + j % 2, :], ALU.mult).then_inc(hh_done, 1)
                        if not (w == 0 and j == 0 and isinstance(k, int)):
                            weighted(q - 1, (w + (j > 0) + 2) % 3, (j + NB - 1) % NB)
            repeat(v, NE // 3, experts, ch)
            weighted(NB * NE - 1, 2, NB - 1)
            v.wait_ge(ym_done, NB * NE)
            v.sem_inc(ym_all, 1)
            v.wait_ge(g_done, 1)
            link(v.tensor_tensor(YM[:, :, :], YM[:, :, :], S0[:, :, :], ALU.mult))
            v.tensor_tensor(X[:, :, :], X[:, :, :], YM[:, :, :], ALU.add).then_inc(x1_done, 1)

            v.wait_ge(w1_ld, 16 * NCONST1)
            v.wait_ge(x1_done, 1)
            bc = lambda: st[:, 2, 0:TB].unsqueeze(2).broadcast_to([P, TB, P])

            def ln_x1(j):
                after(v, xn2T_ready, j)
                layernorm_core(v, ch, X[:, bass.ds(j * TB, TB), :], wa[0][:, :, :], wa[2][:, :, :], st[:, 0, 0:TB], st[:, 1, 0:TB],
                               st[:, 2, 0:TB], D, var_ready, std_ready, LN7 + 2 * j + 1)
                v.tensor_tensor(wa[1][:, :, :], wa[0][:, :, :], bc(), ALU.mult).then_inc(xn2_ready, 1)
                v.wait_ge(xn2_ready, j + 1)
                link(v.tensor_copy(XN2[:, bass.ds(j * TB, TB), :], wa[1][:, :, :]))
                layernorm_core(v, ch, wa[1][:, :, :], wa[0][:, :, :], wa[2][:, :, :], st[:, 0, 0:TB], st[:, 1, 0:TB],
                               st[:, 2, 0:TB], D, var_ready, std_ready, LN7 + 2 * j + 2)
                link(v.tensor_tensor(wa[0][:, :, :], wa[0][:, :, :], bc(), ALU.mult))
                link(v.tensor_tensor(wa[0][:, :, :], wa[0][:, :, :], aff1(0), ALU.mult))
                after(v, xnnT_ready, j)
                v.tensor_tensor(wa[4][:, :, :], wa[0][:, :, :], aff1(1), ALU.add).then_inc(xnn_ready, 1)
                for t in range(TB):
                    v.wait_ge(bd_ready, TB * j + t + 1)
                    after(v, b_st[t % 2], 16 * (2 * j + t // 2))
                    link(v.tensor_copy(bs[t % 2][:, 0, :], PS[:, 6, 0:DS]))
                    v.tensor_copy(DT[:, bass.ds(TB * j + t, 1), :], PS[:, 6, DS:DS + NH1].unsqueeze(1)).then_inc(bd_out, 1)
            repeat(v, NB, ln_x1, ch)
            v.wait_ge(bd_out, NT)
            t4 = lambda i: alog[:, i, :].unsqueeze(1).broadcast_to([P, NT, NH1])
            d0, d1, d2 = DT[:, :, :], dtt[:, 0, :, :], dtt[:, 1, :, :]
            link(v.tensor_tensor(d0, d0, t4(1), ALU.add))
            link(v.tensor_scalar(d1, d0, -1.0, None, ALU.mult))
            v.tensor_tensor(d1, d1, d0, ALU.min).then_inc(dt_step, 1)
            v.wait_ge(dt_act, 2)
            link(v.tensor_scalar(d0, d0, 0.0, None, ALU.max))
            link(v.tensor_tensor(d0, d0, d2, ALU.add))
            link(v.tensor_scalar(d0, d0, 0.001, 0.1, ALU.max, ALU.min))
            link(v.tensor_tensor(d0, d0, t4(2), ALU.mult))
            link(v.tensor_scalar(d0, d0, -1.0, float(np.log(0.99)), ALU.mult, ALU.min))

            link(v.memset(HS[:, :, :, :], 0.0))
            link(v.memset(VR[:, :, :], 0.0))
            ldt = DT[:, :, :].rearrange("p (b c) h -> p b c h", b=B)
            hf = lambda t: t.rearrange("p b h n -> p (b h) n")

            def spread_decays(c):
                after(v, la_ready, c)
                link(v.tensor_copy(ldc[:, :, :].unsqueeze(2), ldt[:, :, bass.ds(c, 1), :]))
                v.tensor_copy(lb, ldc.rearrange("p b h -> p (b h)").unsqueeze(2).broadcast_to([P, B * NH1, P])).then_inc(lb_set, 1)

            def chunk_operands(c, w, trip, last=False):
                v.wait_ge(la_ready, c + 1)
                link(v.tensor_copy(nls[:, :], PS[:, 2, 0:B * NH1]))
                for b in range(B):
                    for h in range(NH1):
                        i = b * NH1 + h
                        ins = v.tensor_scalar(DE[:, i, :], PS[:, b, h * P:(h + 1) * P], nls[:, i:i + 1], 0.0, ALU.subtract, ALU.min)
                ins.then_inc(dif_done, 1)
                if not last:
                    spread_decays(c + 1)
                v.wait_ge(c_ld8[w], 64 * (trip + 1))
                x4 = SG[w].rearrange("p (b h n) -> p b h n", b=B, h=NH1)
                v.tensor_tensor(RB[w][:, :, :, 0:HP], x4, x4, ALU.mult)
                for b in range(B):
                    bb = bs[w][:, b, :].unsqueeze(1).broadcast_to([P, NH1, DS])
                    v.tensor_tensor(RB[w][:, b, :, HP:P], bb, bb, ALU.mult)
                v.wait_ge(d_done, c + 1)
                v.tensor_tensor(DM, DE, TRI.unsqueeze(1).broadcast_to([P, B * NH1, P]), ALU.mult).then_inc(dm_done, 1)
                for b in range(B):
                    bb = bs[w][:, b, :].unsqueeze(1).broadcast_to([P, NH1, DS])
                    v.tensor_tensor(BD[w][:, b, :, :], DE[:, b * NH1:(b + 1) * NH1, P - 1:P].broadcast_to([P, NH1, DS]), bb, ALU.mult)
                v.wait_ge(dm_done, c + 1)
                for b in range(B):
                    gg = PS[:, 2, P + b * P:2 * P + b * P].unsqueeze(1).broadcast_to([P, NH1, P])
                    v.tensor_tensor(MM[w][:, b * NH1:(b + 1) * NH1, :], DM[:, b * NH1:(b + 1) * NH1, :], gg, ALU.mult)
                v.wait_ge(el_done, c + 1)
                for b in range(B):
                    cc = HH[w][0:DS, 256 + b * P:256 + (b + 1) * P].unsqueeze(1).broadcast_to([DS, NH1, P])
                    ins = v.tensor_tensor(CTD[w][b], E2[w][:, b, :, :], cc, ALU.mult)
                ins.then_inc(ops_ready, 1)

            def chunk_state(c, w):
                link(v.tensor_tensor(hf(hst2[:, :, :, :]), hf(HS[:, :, :, :]), hf(E2[w])[:, :, P - 1:P].broadcast_to([DS, B * NH1, HP]), ALU.mult))
                v.wait_ge(c_done, c + 1)
                v.tensor_tensor(hf(HS[:, :, :, :]), hf(hst2[:, :, :, :]), PS[0:DS, 4, :].rearrange("p (i n) -> p i n", n=HP), ALU.add).then_inc(hs_done, 1)
                for b in range(B):
                    ins = v.tensor_reduce(MXV[:, b, bass.ds(c, 1), :], PS[:, 5 + b, :].rearrange("p (i n) -> p i n", n=HP).unsqueeze(1), X_AX, ALU.max)
                ins.then_inc(bnd_read, 1)
                v.wait_ge(hs_done, c + 1)

            def two_chunks(k, last=False):
                chunk_operands(2 * k + 1, 1, k, last)
                chunk_state(2 * k, 0)
                if not last:
                    chunk_operands(2 * k + 2, 0, k + 1)
                chunk_state(2 * k + 1, 1)
            spread_decays(0)
            chunk_operands(0, 0, 0)
            repeat(v, TCH // 2 - 1, two_chunks, ch)
            two_chunks(TCH // 2 - 1, True)
            v.wait_ge(bnd_read, TCH)

            mv = MXV.rearrange("p b c (h k) -> p (b c) h k", k=2)
            mp_ = nmx2[:, :, :]
            link(v.tensor_tensor(mp_, mv[:, :, :, 0], mv[:, :, :, 1], ALU.mult))
            link(v.tensor_reduce(okv[:, :], mp_.rearrange("p t h -> p (t h)"), X_AX, ALU.max))
            v.tensor_scalar(okv[:, :], okv[:, :], BOUND, None, ALU.is_lt).then_inc(ok_ready, 1)
            v.wait_ge(cnt1_ready, 1)
            v.tensor_scalar(flag[:, :], PS[0:1, 3, 0:1], P - 0.5, None, ALU.is_lt).then_inc(flag_set, 1)
            v.wait_ge(flag_set, 1)
            with v.If(v.value_load(flag[:, :], min_val=0, max_val=1) > 0):
                cchain = Chain(v, clip_chain)
                cchain.link(v.memset(g_h, 0.0))

                def clip_steps(k):
                    v.wait_ge(g_ld, 8 * 16 * (k + 1))
                    v.wait_ge(g_dec_done, k + 1)
                    after(v, g_mm, 2 * k)
                    for t in range(GT):
                        cchain.link(v.tensor_tensor(g_h, g_h, g_dec[:, t, :].unsqueeze(2).broadcast_to([P, NH1, HP]), ALU.mult))
                        hflat = g_h.rearrange("p h q -> p (h q)")
                        cchain.link(v.scalar_tensor_tensor(hflat, g_x[:, t, :], g_b[:, t:t + 1], hflat, ALU.mult, ALU.add))
                        cchain.link(v.tensor_scalar(hflat, hflat, HMAX, -HMAX, ALU.min, ALU.max))
                        ins = v.tensor_scalar(g_hc[:, t, :], hflat, g_c[:, t:t + 1], None, ALU.mult)
                        if t == GT - 1:
                            ins.then_inc(g_hc_done, 1)
                            v.wait_ge(g_hc_done, k + 1)
                        else:
                            cchain.link(ins)
                repeat(v, S // GT, clip_steps, cchain)
                v.wait_ge(g_back, 16)

            def gate(k):
                v.wait_ge(z_ld, 32 * (k + 1))
                y2 = wb[0][:, :, :]
                chan = lambda i: sc_aff[:, i, :].unsqueeze(1).broadcast_to([P, 2, DI])
                g2 = lambda t: t.rearrange("p (t c) -> p t c", t=2)
                link(v.tensor_tensor(y2, g2(SG[0]), chan(0), ALU.mult))
                link(v.tensor_tensor(y2, y2, YS[:, bass.ds(2 * k, 2), :], ALU.add))
                link(v.tensor_tensor(y2, y2, g2(SG[1]), ALU.mult))
                layernorm_core(v, ch, y2, wb[1][:, :, :], wb[2][:, :, :], st[:, 0, 0:2], st[:, 1, 0:2], st[:, 2, 0:2], DI, var_ready, std_ready, LN9 + 2 * k + 1)
                link(v.tensor_tensor(wb[1][:, :, :], wb[1][:, :, :], st[:, 2, 0:2].unsqueeze(2).broadcast_to([P, 2, DI]), ALU.mult))
                link(v.tensor_tensor(wb[1][:, :, :], wb[1][:, :, :], chan(1), ALU.mult))
                v.tensor_tensor(wb[1][:, :, :], wb[1][:, :, :], chan(2), ALU.add).then_inc(yl_ready, 1)
                v.wait_ge(pr_ready, k + 1)
                o = wa[5][:, 0:2, :]
                link(v.tensor_scalar(o, PS[:, 1, 0:2 * D].rearrange("p (t d) -> p t d", t=2), HMAX, -HMAX, ALU.min, ALU.max))
                layernorm_core(v, ch, o, wa[5][:, 2:4, :], wa[3][:, 0:2, :], st[:, 0, 0:2], st[:, 1, 0:2], st[:, 2, 0:2], D, var_ready, std_ready, LN9 + 2 * k + 2)
                o = wa[5][:, 2:4, :]
                link(v.tensor_tensor(o, o, st[:, 2, 0:2].unsqueeze(2).broadcast_to([P, 2, D]), ALU.mult))
                link(v.tensor_tensor(o, o, affine[:, 6, :].unsqueeze(1).broadcast_to([P, 2, D]), ALU.mult))
                v.tensor_tensor(S2[:, bass.ds(2 * k, 2), :], o, affine[:, 7, :].unsqueeze(1).broadcast_to([P, 2, D]), ALU.add).then_inc(s2_done, 1)
                v.wait_ge(s2_done, k + 1)
            repeat(v, NT // 2, gate, ch)

            v.wait_ge(l1_ready, 1)
            q0, q1, q2, q3 = (lg1[:, i, :, :] for i in range(4))
            r_, n_ = s1_[:, 0, :], s1_[:, 1, :]
            b_ = lambda t: t.unsqueeze(2).broadcast_to([1, B, E1])
            link(v.tensor_copy(q0, PS[0:1, 2, 0:B * E1].rearrange("p (b e) -> p b e", b=B)))
            link(v.tensor_reduce(r_, q0, X_AX, ALU.max))
            v.tensor_tensor(q0, q0, b_(r_), ALU.subtract).then_inc(l1_max, 1)
            v.wait_ge(l1_exp, 1)
            link(v.tensor_reduce(r_, q1, X_AX, ALU.add))
            link(v.reciprocal(r_, r_))
            link(v.tensor_tensor(q1, q1, b_(r_), ALU.mult))
            link(v.tensor_reduce(r_, q1, X_AX, ALU.max))
            link(v.tensor_tensor(q2, q1, b_(r_), ALU.is_equal))
            ex = io1[:, :].unsqueeze(1).broadcast_to([1, B, E1])
            link(v.tensor_tensor(q2, q2, ex, ALU.mult))
            link(v.tensor_reduce(n_, q2, X_AX, ALU.min))
            v.tensor_tensor(q3, ex, b_(n_), ALU.is_equal).then_inc(oh_ready, 1)
            v.wait_ge(ohb_ready, 1)
            link(v.tensor_copy(oh[:, :], PS[:, 2, 0:B * E1]))
            v.wait_ge(fw_ld, 16)
            for b in range(B):
                link(v.tensor_scalar(SW1[b][:, :], FW1[:, 0, :], oh[:, b * E1:b * E1 + 1], None, ALU.mult))
                for e in range(1, E1):
                    link(v.scalar_tensor_tensor(SW1[b][:, :], FW1[:, e, :], oh[:, b * E1 + e:b * E1 + e + 1], SW1[b][:, :], ALU.mult, ALU.add))
            v.tensor_copy(oh[:, :], oh[:, :]).then_inc(sel1_done, 1)

            def finish(j):
                v.wait_ge(fo_ready, j + 1)
                after(v, fin_ready, j)
                v.scalar_tensor_tensor(f_(wa[0]), PS[:, 5, :], 0.3, XN2[:, bass.ds(TB * j, TB), :].rearrange("p t d -> p (t d)"), ALU.mult, ALU.add).then_inc(gin_ready, 1)
                v.wait_ge(g_ready, j + 1)
                link(v.tensor_tensor(wa[1][:, :, :], wa[1][:, :, :], S2[:, bass.ds(TB * j, TB), :], ALU.mult))
                xb = X[:, bass.ds(TB * j, TB), :]
                v.tensor_tensor(xb, xb, wa[1][:, :, :], ALU.add).then_inc(fin_ready, 1)
            repeat(v, NB, finish, ch)
            v.wait_ge(fin_ready, NB)

        @block.scalar
        def _(act):
            act.wait_ge(c_ld, 16 * NCONST)

            def ln_x(j):
                act.wait_ge(var_ready, j + 1)
                act.activation(st[:, 2, 0:TB], st[:, 1, 0:TB], ACT.Sqrt).then_inc(std_ready, 1)
                act.wait_ge(xnT_ready, j + 1)
                after(act, xnt_st, 32 * j)
                act.activation(f_(wa[2]), PS[:, 0, :], ACT.Copy).then_inc(xnT_out, 1)
            repeat(act, NB, ln_x)

            def levels(j):
                for w in range(2):
                    act.wait_ge(h_level, 2 * j + w + 1)
                    after(act, h_st[w], 16 * j)
                    act.activation(hout[w].rearrange("p b s -> p (b s)"), PS[0:DH, w, 0:B * P], ACT.Copy).then_inc(h_out, 1)
            repeat(act, TCH // 2, levels)

            def qkv_out(j):
                act.wait_ge(qk_ready, j + 1)
                after(act, qs_ready, j)
                act.activation(f_(wa[1]), PS[:, 0, :], ACT.Identity, bias=bcol[:, 0:1]).then_inc(q_out, 1)
                after(act, ks_ready, j)
                act.activation(f_(wa[2]), PS[:, 1, :], ACT.Identity, bias=bcol[:, 1:2]).then_inc(k_out, 1)
                act.wait_ge(v_ready, j + 1)
                act.activation(VP[:, bass.ds(j * TB, TB), :], PS[:, 2, :].rearrange("p (t c) -> p t c", c=P), ACT.Copy).then_inc(v_out, 1)
            repeat(act, NB, qkv_out)

            def evac(u, trip_halves, half):
                act.wait_ge(pv_done, TCH * u + TCH // 2 * (half + 1))
                after(act, oe_st[half], 64 * u)
                act.activation(OE[half][:, :], PS[:, 4, :], ACT.Copy).then_inc(o_evac, 1)

            def unit_exp(u):
                for i in range(STEPS):
                    T = STEPS * u + i
                    act.wait_ge(sc_ready, T + 1)
                    if i % 2 == 0:
                        after(act, pv_done, TCH * u + i // 2 - 1)
                    act.activation(PR[i % 4][:, :], PS[:, 2 * (i % 2):2 * (i % 2) + 2, :].rearrange("p a c -> p (a c)"), ACT.Exp,
                                   scale=float(1.0 / np.sqrt(np.float32(DK)))).then_inc(exp_done, 1)
                    if i == TCH + 1:
                        evac(u, 0, 0)
                evac(u, 0, 1)

            def group_exp(k):
                for w in range(4):
                    unit_exp(4 * k + w)
            repeat(act, GROUPS, group_exp)

            def finish_attn(j):
                act.wait_ge(var_ready, LN4 + 2 * j + 1)
                act.activation(st[:, 2, :], st[:, 1, :], ACT.Sqrt).then_inc(std_ready, 1)
                act.wait_ge(yT_ready, j + 1)
                act.activation(f_(wa[3]), PS[:, 1, :], ACT.Copy).then_inc(yT_out, 1)
                for f in range(DFF // P):
                    act.wait_ge(f_ready, 4 * j + f + 1)
                    act.activation(FH[f][:, 0:512], PS[:, 2 + f, :], ACT.Relu, bias=bcol[:, 2 + f:3 + f]).then_inc(f_out, 1)
                act.wait_ge(var_ready, LN4 + 2 * j + 2)
                act.activation(st[:, 2, 0:TB], st[:, 1, 0:TB], ACT.Sqrt).then_inc(std_ready, 1)
            repeat(act, NB, finish_attn)

            act.wait_ge(lg_ready, 1)
            act.activation(gt[0].rearrange("p t e -> p (t e)"), PS[:, 0:2, :].rearrange("p a c -> p (a c)"), ACT.Copy).then_inc(lg_out, 1)
            act.wait_ge(lmx, 1)
            act.activation(gt[1][:, :, :], gt[0][:, :, :], ACT.Exp).then_inc(lexp, 1)

            def experts(k):
                for w in range(3):
                    for j in range(NB):
                        q = NB * (3 * k + w) + j
                        act.wait_ge(mh_ready, q + 1)
                        after(act, hh_done, q - 1)
                        act.activation(SG[j % 2][:, :], PS[:, j % 2, :], ACT.Silu).then_inc(sg_done, 1)
            repeat(act, NE // 3, experts)
            act.wait_ge(ym_all, 2)
            act.activation(YM[:, :, :], YM[:, :, :], ACT.Silu).then_inc(g_done, 1)

            act.wait_ge(w1_ld, 16 * NCONST1)

            def proj(j):
                for i in range(2):
                    act.wait_ge(var_ready, LN7 + 2 * j + i + 1)
                    act.activation(st[:, 2, 0:TB], st[:, 1, 0:TB], ACT.Sqrt).then_inc(std_ready, 1)
                    if i == 0:
                        act.wait_ge(xn2T_ready, j + 1)
                        act.activation(XNT[:, bass.ds(j * 512, 512)], PS[:, 0, :], ACT.Copy).then_inc(xn2T_out, 1)
                act.wait_ge(xnnT_ready, j + 1)
                after(act, bd_ready, TB * j)
                act.activation(f_(wa[3]), PS[:, 1, :], ACT.Copy).then_inc(xnnT_out, 1)
                act.wait_ge(bct_ready, j + 1)
                after(act, bct_st, 32 * j)
                act.activation(HH[0][0:DS, :], PS[0:DS, 4, :], ACT.Copy).then_inc(bct_out, 1)
                act.activation(HH[1][0:DS, :], PS[0:DS, 5, :], ACT.Copy).then_inc(bct_out, 1)
                for t in range(TB):
                    act.wait_ge(zx_ready, TB * j + t + 1)
                    after(act, zx_st[t % 2], 32 * (2 * j + t // 2))
                    act.activation(SG[t % 2][:, 0:DI], PS[:, 2 + t % 2, 0:DI], ACT.Silu).then_inc(zx_out, 1)
                    act.activation(SG[t % 2][:, DI:2 * DI], PS[:, 2 + t % 2, DI:2 * DI], ACT.Copy).then_inc(zx_out, 1)
            repeat(act, NB, proj)
            act.wait_ge(dt_step, 1)
            act.activation(alog[:, 2, :], alog[:, 0, :], ACT.Exp).then_inc(dt_act, 1)
            act.activation(dtt[:, 1, :, :], dtt[:, 0, :, :], ACT.Exp).then_inc(act_chain, 1)
            act.wait_ge(act_chain, 1)
            act.activation(dtt[:, 1, :, :], dtt[:, 1, :, :], ACT.Ln, bias=1.0).then_inc(dt_act, 1)

            def chunk_exps(c, w):
                act.wait_ge(dif_done, c + 1)
                act.activation(DE, DE, ACT.Exp).then_inc(d_done, 1)
                after(act, hs_done, c - 1)
                sums = PS[0:DS, 0:2, :].rearrange("p b c -> p (b c)")
                act.activation(E2[w].rearrange("p b h t -> p (b h t)"), sums, ACT.Exp).then_inc(el_done, 1)
                act.activation(E2b[w].rearrange("p b h t -> p (b h t)"), sums, ACT.Exp)
                act.wait_ge(dm_done, c + 1)
                act.activation(DMb[w], DM, ACT.Copy).then_inc(opb_ready, 1)

            def chunk_out(c):
                act.wait_ge(c_done, c + 1)
                for b in range(B):
                    act.activation(VR[32 * b:32 * b + 1, :, :], VS[32 * b:32 * b + 1, :, :], ACT.Copy).then_inc(vr_out, 1)
                act.activation(YS.rearrange("p (b c) n -> p b c n", b=B)[:, :, bass.ds(c, 1), :],
                               PS[:, 3, :].rearrange("p (b n) -> p b n", b=B).unsqueeze(2), ACT.Copy).then_inc(y_out, 1)

            def two_chunks(k, last=False):
                chunk_exps(2 * k + 1, 1)
                chunk_out(2 * k)
                if not last:
                    chunk_exps(2 * k + 2, 0)
                chunk_out(2 * k + 1)
            chunk_exps(0, 0)
            repeat(act, TCH // 2 - 1, two_chunks)
            two_chunks(TCH // 2 - 1, True)
            act.wait_ge(flag_set, 1)
            with act.If(act.value_load(flag[:, :], min_val=0, max_val=1) > 0):
                def clip_out(k):
                    act.wait_ge(g_ld, 8 * 16 * (k + 1))
                    act.activation(HH[1][:, 0:GT * NH1], HH[1][:, 0:GT * NH1], ACT.Exp).then_inc(g_dec_done, 1)
                    for i in range(2):
                        act.wait_ge(g_mm, 2 * k + i + 1)
                        if i == 0:
                            after(act, g_st, 16 * B * k)
                        act.activation(g_y[:, i * 2048:(i + 1) * 2048], PS[0:B, 0:4, :].rearrange("p a c -> p (a c)"), ACT.Copy).then_inc(g_y_out, 1)
                repeat(act, S // GT, clip_out)

            def gate(k):
                act.wait_ge(var_ready, LN9 + 2 * k + 1)
                act.activation(st[:, 2, 0:2], st[:, 1, 0:2], ACT.Sqrt).then_inc(std_ready, 1)
                act.wait_ge(ylT_ready, k + 1)
                act.activation(ylT[:, :], PS[:, 0, :], ACT.Copy).then_inc(ylT_out, 1)
                act.wait_ge(var_ready, LN9 + 2 * k + 2)
                act.activation(st[:, 2, 0:2], st[:, 1, 0:2], ACT.Sqrt).then_inc(std_ready, 1)
            repeat(act, NT // 2, gate)

            act.wait_ge(a1_ready, 1)
            act.activation(hn[:, :], PS[:, 2, 0:B], ACT.Gelu, bias=wp[:, P:P + 1]).then_inc(a1_out, 1)
            act.wait_ge(l1_max, 1)
            act.activation(lg1[:, 1, :, :], lg1[:, 0, :, :], ACT.Exp).then_inc(l1_exp, 1)
            act.wait_ge(sel1_done, 1)

            for b in range(B):
                def ff(k, b=b):
                    j = NB // B * b + k
                    for f in range(2):
                        act.wait_ge(fh_ready, 2 * j + f + 1)
                        act.activation(HH[f][:, :], PS[:, 2 + f, :], ACT.Gelu, bias=SW1[b][:, 2 * F1 + f:2 * F1 + f + 1]).then_inc(fh_out, 1)
                    act.wait_ge(rt_ready, j + 1)
                    act.activation(SG[0][:, :], PS[:, 4, :], ACT.Identity, bias=SW1[b][:, 2 * F1 + 2:2 * F1 + 3]).then_inc(rt_out, 1)
                    act.wait_ge(gin_ready, j + 1)
                    after(act, fin_ready, j)
                    act.activation(f_(wa[1]), f_(wa[0]), ACT.Silu).then_inc(g_ready, 1)
                repeat(act, NB // B, ff) if b == 0 else loop_only(act, NB // B, ff)

        @block.gpsimd
        def _(pool):
            for i in range(4):
                pool.memset(VH[i][:, :, :], 1.0).then_inc(vh_set, 1)
            pool.wait_ge(ql_st, 48 * NB)
            pool.wait_ge(kl_st, 48 * NB)
            pool.wait_ge(vh_set, 4)
            for i in range(4):
                pool.memset(QS[i][64:96, :], 1.0).then_inc(ones_set, 1)
                pool.memset(KS[i][64:96, :], 1.0).then_inc(ones_set, 1)
            pool.wait_ge(ones_set, 8)
            pool.wait_ge(v_out, NB)

            def prepare(k):
                for w in range(4):
                    u, g = 4 * k + w, 2 * k + w // 2
                    after(pool, pv_done, TCH * (u - 3))
                    pool.tensor_copy(VH[w][:, :, 0:DK], VP[:, (w % 2) * TCH:(w % 2 + 1) * TCH, bass.ds(g * DK, DK)]).then_inc(vh_ready, 1)
            repeat(pool, GROUPS, prepare)

        @block.tensor
        def _(pe):
            pe.wait_ge(c_ld, 16 * NCONST)

            def turn(j):
                pe.wait_ge(xn_ready, j + 1)
                after(pe, xnT_out, j)
                for t in range(TB):
                    mm = pe.transpose(PS[:, 0, t * P:(t + 1) * P], wa[1][:, t, :], ident[:, :])
                mm.then_inc(xnT_ready, 1)
            repeat(pe, NB, turn)
            pe.wait_ge(xnT_out, NB)

            def holt(j):
                for w in range(2):
                    t = 2 * j + w
                    pe.wait_ge(hx_ld[w], 16 * (j + 1))
                    if w or not isinstance(j, int):
                        pe.wait_ge(h_carried, t)
                    else:
                        pe.wait_ge(hst_ld, 16)
                    after(pe, h_out, t - 1)
                    for b in range(B):
                        o = PS[0:DH, w, b * P:(b + 1) * P]
                        pe.matmul(o, hx[w][:, b, :], cst[:, 0:P], start=True, stop=False)
                        mm = pe.matmul(o, hst[:, b, :], rows[0:2, 0:P], start=False, stop=True)
                    mm.then_inc(h_level, 1)
                    o = PS[0:2, 4, 0:P]
                    pe.matmul(o, cst[:, P:P + 2], hx[w].rearrange("p b d -> p (b d)"), start=True, stop=False)
                    pe.matmul(o, rows[0:2, P:P + 2], hst.rearrange("p b d -> p (b d)"), start=False, stop=True).then_inc(h_state, 1)
            repeat(pe, TCH // 2, holt)
            pe.wait_ge(h_out, TCH)

            def qkv(j):
                pe.wait_ge(xc_ld, 16 * (j + 1))
                after(pe, k_out, j)
                pe.matmul(PS[:, 0, :], wsq[:, 0, :], f_(wa[0]), start=True, stop=True)
                pe.matmul(PS[:, 1, :], wsq[:, 1, :], f_(wa[0]), start=True, stop=True).then_inc(qk_ready, 1)
                after(pe, v_out, j)
                for t in range(TB):
                    o = PS[:, 2, t * P:(t + 1) * P]
                    pe.matmul(o, wa[0][:, t, :], wsq[:, 2, :], start=True, stop=False)
                    mm = pe.matmul(o, ones1[:, :], brow[:, 0:P], start=False, stop=True)
                mm.then_inc(v_ready, 1)
            repeat(pe, NB, qkv)

            def max_scores(uu, n, w):
                after(pe, mx_done, 4 * TCH * uu + n - 1)
                pe.matmul(PS[:, 5 + n % 2, :], QS[w][0:KROWS, (n // 4) * P:(n // 4 + 1) * P], KS[w][0:KROWS, (n % 4) * 512:(n % 4 + 1) * 512],
                          start=True, stop=True).then_inc(mxs_ready, 1)

            def turn_max(uu):
                pe.wait_ge(spl_ready, uu + 1)
                after(pe, mt_out, uu)
                pe.transpose(PT[:, 0:P], spl.rearrange("p l c -> p (l c)"), identb[:, :]).then_inc(mt_ready, 1)

            def weigh(u, pair, w):
                pe.wait_ge(exp_done, STEPS * u + 2 * pair + 2)
                if pair % (TCH // 2) == 0:
                    after(pe, o_evac, 2 * u + pair // (TCH // 2))
                for odd in range(2):
                    i = 2 * pair + odd
                    kt = i % TCH
                    for qb in range(2):
                        jg = 2 * odd + qb
                        mm = pe.matmul(PS[32 * jg:32 * jg + 32, 4, :], VH[w][:, kt, :], PR[i % 4][:, qb * 512:(qb + 1) * 512],
                                       start=(kt < 2), stop=(kt >= TCH - 2))
                mm.then_inc(pv_done, 1)

            def unit(u, w, trip, last, final):
                nw = (w + 2) % 4
                pe.wait_ge(m_ld[w], 16 * (trip + 1))
                if not last:
                    pe.wait_ge(qk_ld[nw], 96 * (trip + 1 + (w >= 2)))
                n = 0
                for i in range(STEPS):
                    kt, qh = i % TCH, i // TCH
                    after(pe, exp_done, STEPS * u + i - 1)
                    for qb in range(2):
                        q0 = qh * 1024 + qb * 512
                        mm = pe.matmul(PS[:, 2 * (i % 2) + qb, :], KS[w][0:KROWS + 3, kt * P:(kt + 1) * P], QS[w][0:KROWS + 3, q0:q0 + 512],
                                       start=True, stop=True)
                    mm.then_inc(sc_ready, 1)
                    if not last:
                        max_scores(u + 2, n, nw)
                        n += 1
                    if i == 1:
                        pe.wait_ge(vh_ready, u + 1)
                    if i % 2 and i >= 3:
                        weigh(u, (i - 3) // 2, w)
                    if i % 2 and not last:
                        for _ in range(2):
                            max_scores(u + 2, n, nw)
                            n += 1
                    if i == TURN and not final:
                        turn_max(u + 1)
                weigh(u, TCH - 1, w)

            pe.wait_ge(v_out, NB)
            for u in range(2):
                pe.wait_ge(qk_ld[u], 96)
                for n in range(4 * TCH):
                    max_scores(u, n, u)
                    if u == 1 and n == TURNED - 1:
                        turn_max(0)

            def group(k, last=False):
                for w in range(4):
                    unit(4 * k + w, w, k, last and w >= 2, last and w == 3)
            repeat(pe, GROUPS - 1, group)
            group(GROUPS - 1, True)

            pe.wait_ge(o_evac, 2 * UNITS)
            pe.wait_ge(exp_done, STEPS * UNITS)

            def finish_attn(j):
                pe.wait_ge(at_sum, j + 1)
                for t in range(TB):
                    o = PS[:, 0, t * P:(t + 1) * P]
                    pe.matmul(o, wa[0][:, t, :], wsq[:, 3, :], start=True, stop=False)
                    pe.matmul(o, wa[4][:, t, :], ident[:, :], start=False, stop=False)
                    mm = pe.matmul(o, ones1[:, :], brow[:, P:2 * P], start=False, stop=True)
                mm.then_inc(r_ready, 1)
                pe.wait_ge(y_ready, j + 1)
                for t in range(TB):
                    mm = pe.transpose(PS[:, 1, t * P:(t + 1) * P], wa[1][:, t, :], ident[:, :])
                mm.then_inc(yT_ready, 1)
                pe.wait_ge(yT_out, j + 1)
                for f in range(DFF // P):
                    after(pe, f_out, 4 * (j - 1) + f + 1)
                    pe.matmul(PS[:, 2 + f, :], wff1[:, f * P:(f + 1) * P], f_(wa[3]), start=True, stop=True).then_inc(f_ready, 1)
                pe.wait_ge(f_out, 4 * (j + 1))
                for t in range(TB):
                    o = PS[:, 0, t * P:(t + 1) * P]
                    for f in range(DFF // P):
                        pe.matmul(o, FH[f][:, t * P:(t + 1) * P], wff2[:, f, :], start=(f == 0), stop=False)
                    pe.matmul(o, wa[3][:, t, :], ident[:, :], start=False, stop=False)
                    mm = pe.matmul(o, ones1[:, :], brow[:, 2 * P:3 * P], start=False, stop=True)
                mm.then_inc(ff_ready, 1)
            repeat(pe, NB, finish_attn)

            pe.wait_ge(xnt_ld, 16)
            pe.wait_ge(at_free, NB)
            for t in range(NT):
                mm = pe.matmul(PS[:, t // 16, (t % 16) * E:(t % 16 + 1) * E], XNT[:, t * P:(t + 1) * P], wgT[:, :], start=True, stop=True)
            mm.then_inc(lg_ready, 1)
            pe.wait_ge(sel_done, 1)
            pe.wait_ge(lg_out, 1)
            for h in range(2):
                sel = gt[5][:, h * 16:(h + 1) * 16, :].rearrange("p t e -> p (t e)")
                pe.matmul(PS[:, h, :], cst[:, P + 2:2 * P + 2], sel, start=True, stop=True)
                mm = pe.matmul(PS[:, 2 + h, :], onesq[:, :], sel, start=True, stop=True)
            mm.then_inc(cnt_ready, 1)
            pe.wait_ge(wt_done, 1)

            def project(q, w, j):
                pe.wait_ge(hh_done, q + 1)
                after(pe, ym_done, q - 1)
                for t in range(TB):
                    mm = pe.matmul(PS[:, 4 + j % 2, t * P:(t + 1) * P], HH[j % 2][:, t * P:(t + 1) * P], EW[w][:, 2, :], start=True, stop=True)
                mm.then_inc(mo_ready, 1)

            def experts(k):
                for w in range(3):
                    pe.wait_ge(ew_ld[w], 16 * (k + 1))
                    for j in range(NB):
                        q = NB * (3 * k + w) + j
                        after(pe, sg_done, q - 1)
                        after(pe, hh_done, q - 1)
                        pe.matmul(PS[:, j % 2, :], EW[w][:, 0, :], XNT[:, j * 512:(j + 1) * 512], start=True, stop=True)
                        pe.matmul(PS[:, 2 + j % 2, :], EW[w][:, 1, :], XNT[:, j * 512:(j + 1) * 512], start=True, stop=True).then_inc(mh_ready, 1)
                        if not (w == 0 and j == 0 and isinstance(k, int)):
                            project(q - 1, (w + (j > 0) + 2) % 3, (j + NB - 1) % NB)
            repeat(pe, NE // 3, experts)
            project(NB * NE - 1, 2, NB - 1)

            pe.wait_ge(w1_ld, 16 * NCONST1)
            pe.wait_ge(ym_done, NB * NE)

            def proj(j):
                pe.wait_ge(xn2_ready, j + 1)
                after(pe, xn2T_out, j)
                for t in range(TB):
                    mm = pe.transpose(PS[:, 0, t * P:(t + 1) * P], wa[1][:, t, :], ident[:, :])
                mm.then_inc(xn2T_ready, 1)
                pe.wait_ge(xnn_ready, j + 1)
                after(pe, xnnT_out, j)
                for t in range(TB):
                    mm = pe.transpose(PS[:, 1, t * P:(t + 1) * P], wa[4][:, t, :], ident[:, :])
                mm.then_inc(xnnT_ready, 1)
                pe.wait_ge(xnnT_out, j + 1)
                after(pe, bct_out, 2 * j)
                ob, oc = 2 * DI, 2 * DI + DS + NH1
                pe.matmul(PS[0:DS, 4, :], win[:, ob:ob + DS], f_(wa[3]), start=True, stop=True)
                pe.matmul(PS[0:DS, 5, :], win[:, oc:oc + DS], f_(wa[3]), start=True, stop=True).then_inc(bct_ready, 1)
                for t in range(TB):
                    after(pe, zx_out, 2 * (TB * j + t - 1))
                    pe.matmul(PS[:, 2 + t % 2, :], wa[3][:, t, :], win[:, 0:2 * DI], start=True, stop=True).then_inc(zx_ready, 1)
                    after(pe, bd_out, TB * j + t)
                    pe.matmul(PS[:, 6, 0:DS + NH1], wa[3][:, t, :], win[:, ob:oc], start=True, stop=True).then_inc(bd_ready, 1)
            repeat(pe, NB, proj)
            pe.wait_ge(zx_out, 2 * NT)
            pe.wait_ge(bd_out, NT)

            def chunk_sums(c, w, trip):
                pe.wait_ge(lb_set, c + 1)
                after(pe, ops_ready, c)
                after(pe, opb_ready, c)
                for b in range(B):
                    for h in range(NH1):
                        pe.matmul(PS[:, b, h * P:(h + 1) * P], lb[:, b * NH1 + h, :], TRI, start=True, stop=True)
                pe.matmul(PS[:, 2, 0:B * NH1], TRI, ldc.rearrange("p b h -> p (b h)"), start=True, stop=True)
                pe.wait_ge(c_ld8[w], 64 * (trip + 1))
                for b in range(B):
                    mm = pe.matmul(PS[:, 2, P + b * P:2 * P + b * P], HH[w][0:DS, b * P:(b + 1) * P], HH[w][0:DS, 256 + b * P:256 + (b + 1) * P],
                                   start=True, stop=True)
                mm.then_inc(la_ready, 1)

            def chunk_products(c, w):
                pe.wait_ge(ops_ready, c + 1)
                after(pe, hs_done, c)
                after(pe, y_out, c)
                for b in range(B):
                    for h in range(NH1):
                        i, n = b * NH1 + h, (b * NH1 + h) * HP
                        x = SG[w][:, n:n + HP]
                        pe.matmul(PS[:, 3, n:n + HP], MM[w][:, i, :], x, start=True, stop=False)
                        pe.matmul(PS[:, 3, n:n + HP], CTD[w][b][:, h, :], HS[:, b, h, :], start=False, stop=True)
                        pe.matmul(PS[0:DS, 4, n:n + HP], BD[w][:, b, h, :], x, start=True, stop=True)
                pe.wait_ge(opb_ready, c + 1)
                after(pe, vr_out, 2 * c)
                after(pe, bnd_read, c)
                for b in range(B):
                    r = slice(32 * b, 32 * b + 1)
                    for h in range(NH1):
                        o = PS[:, 5 + b, h * P:(h + 1) * P]
                        pe.matmul(o, DMb[w][:, b * NH1 + h, :], RB[w][:, b, h, :], start=True, stop=False)
                        pe.matmul(o, E2b[w][r, b, h, :], VR[r, h, :], start=False, stop=True)
                        o = VS[r, h, :]
                        pe.matmul(o, DMb[w][:, b * NH1 + h, P - 1:P], RB[w][:, b, h, :], start=True, stop=False)
                        mm = pe.matmul(o, E2b[w][r, b, h, P - 1:P], VR[r, h, :], start=False, stop=True)
                mm.then_inc(c_done, 1)

            def two_chunks(k, last=False):
                chunk_sums(2 * k + 1, 1, k)
                chunk_products(2 * k, 0)
                if not last:
                    chunk_sums(2 * k + 2, 0, k + 1)
                chunk_products(2 * k + 1, 1)
            chunk_sums(0, 0, 0)
            repeat(pe, TCH // 2 - 1, two_chunks)
            two_chunks(TCH // 2 - 1, True)
            pe.wait_ge(bnd_read, TCH)
            pe.wait_ge(y_out, TCH)
            pe.wait_ge(ok_ready, 1)
            pe.matmul(PS[0:1, 3, 0:1], okv[:, :], onesq[:, 0:1], start=True, stop=True).then_inc(cnt1_ready, 1)
            pe.wait_ge(flag_set, 1)
            with pe.If(pe.value_load(flag[:, :], min_val=0, max_val=1) > 0):
                def clip_mm(k):
                    pe.wait_ge(g_hc_done, k + 1)
                    for i in range(2):
                        after(pe, g_y_out, 2 * k + i)
                        for q in range(4):
                            t = 8 * i + 2 * q
                            mm = pe.matmul(PS[0:B, q, :], cst[:, 2 * P + 2:2 * P + 2 + B], g_hc[:, t:t + 2, :].rearrange("p t c -> p (t c)"), start=True, stop=True)
                        mm.then_inc(g_mm, 1)
                repeat(pe, S // GT, clip_mm)
                pe.wait_ge(g_y_out, 2 * S // GT)

            def gate(k):
                pe.wait_ge(yl_ready, k + 1)
                for i in range(4):
                    mm = pe.transpose(PS[:, 0, i * P:(i + 1) * P], wb[1].rearrange("p t (f c) -> p (t f) c", f=2)[:, i, :], ident[:, :])
                mm.then_inc(ylT_ready, 1)
                pe.wait_ge(ylT_out, k + 1)
                after(pe, s2_done, k)
                for t in range(2):
                    for f in range(2):
                        mm = pe.matmul(PS[:, 1, t * D:(t + 1) * D], ylT[:, (2 * t + f) * P:(2 * t + f + 1) * P], wout[:, f, :], start=(f == 0), stop=(f == 1))
                mm.then_inc(pr_ready, 1)
            repeat(pe, NT // 2, gate)

            pe.wait_ge(xn2T_out, NB)
            pe.wait_ge(s2_done, NT // 2)
            pe.matmul(PS[:, 2, 0:B], wp[:, 0:P], XNT.rearrange("p (b s) -> p b s", b=B)[:, :, S - 1], start=True, stop=True).then_inc(a1_ready, 1)
            pe.wait_ge(a1_out, 1)
            for b in range(B):
                o = PS[0:1, 2, b * E1:(b + 1) * E1]
                pe.matmul(o, hn[:, b:b + 1], wp[:, P + 1:P + 1 + E1], start=True, stop=False)
                mm = pe.matmul(o, ones1[:, 0:1], r1[:, 0:E1], start=False, stop=True)
            mm.then_inc(l1_ready, 1)
            pe.wait_ge(oh_ready, 1)
            pe.matmul(PS[:, 2, 0:B * E1], ones1[:, :], lg1[:, 3, :, :].rearrange("p b e -> p (b e)"), start=True, stop=True).then_inc(ohb_ready, 1)
            pe.wait_ge(sel1_done, 1)

            for b in range(B):
                def ff(k, b=b):
                    j = NB // B * b + k
                    xb = XNT[:, bass.ds(j * 512, 512)]
                    for f in range(2):
                        after(pe, fh_out, 2 * (j - 1) + f + 1)
                        pe.matmul(PS[:, 2 + f, :], SW1[b][:, f * P:(f + 1) * P], xb, start=True, stop=True).then_inc(fh_ready, 1)
                    pe.wait_ge(fh_out, 2 * j + 2)
                    for f in range(2):
                        mm = pe.matmul(PS[:, 4, :], SW1[b][:, F1 + f * P:F1 + (f + 1) * P], HH[f][:, :], start=(f == 0), stop=(f == 1))
                    mm.then_inc(rt_ready, 1)
                    pe.wait_ge(rt_out, j + 1)
                    after(pe, gin_ready, j)
                    for t in range(TB):
                        o = PS[:, 5, t * P:(t + 1) * P]
                        pe.matmul(o, SG[0][:, t * P:(t + 1) * P], wo1[:, :], start=True, stop=False)
                        mm = pe.matmul(o, ones1[:, :], r1[:, E1:E1 + D], start=False, stop=True)
                    mm.then_inc(fo_ready, 1)
                repeat(pe, NB // B, ff) if b == 0 else loop_only(pe, NB // B, ff)


def holt_constants():
    al, be = np.float64(ALPHA), np.float64(BETA)
    F = np.array([[1 - al, 1 - al], [be * (1 - al) - be, be * (1 - al) + 1 - be]])
    g = np.array([al, be * al])
    pw = [np.eye(2)]
    for _ in range(P):
        pw.append(F @ pw[-1])
    level = np.zeros((P, P))
    for t in range(P):
        for s in range(t + 1):
            level[s, t] = (pw[t - s] @ g)[0]
    end = np.stack([pw[P - 1 - s] @ g for s in range(P)])
    state = np.stack([pw[t + 1][0] for t in range(P)], axis=1)
    return level, end, state, pw[P].T


_OUTS = [((2, 2048, 128), 'float32')]


def layout(x):
    f = np.float32
    g = lambda n: np.asarray(x[n])

    def pair(name, transpose=True):
        m = np.zeros((P, P), f)
        m[:DH, :DH] = g(f"L0_attn_{name}1").T
        m[DH:, DH:] = g(f"L0_attn_{name}2").T
        return m

    cat = lambda *n: np.concatenate([g("L0_attn_" + i) for i in n])
    level, end, state, full = holt_constants()
    wi = g("L1_attn_in_proj_w")
    tri = np.triu(np.ones((P, P)))
    rowc = np.zeros((P, P + 2), f)
    rowc[0:2, 0:P], rowc[0:2, P:P + 2] = state, full
    d = {
        "x": g("L0_attn_x"),
        "ident": np.eye(P, dtype=f),
        "consts": np.concatenate([level, end, tri, np.repeat(np.eye(B), DS, axis=0)], axis=1).astype(f),
        "rowc": rowc,
        "wsq": np.stack([pair("wq"), pair("wk"), pair("wv"), pair("wo")], axis=1),
        "wff1": g("L0_attn_w_ff1").T,
        "wff2": g("L0_attn_w_ff2").T.reshape(DFF // P, P, D).transpose(1, 0, 2),
        "bcol": np.stack([cat("bq1", "bq2"), cat("bk1", "bk2")] + list(g("L0_attn_b_ff1").reshape(DFF // P, P)), axis=1),
        "brow": np.concatenate([cat("bv1", "bv2"), cat("bo1", "bo2"), g("L0_attn_b_ff2")])[None],
        "affine": np.stack([cat("g1", "g2"), cat("be1", "be2"), g("L0_attn_g_ff"), g("L0_attn_be_ff"),
                            g("L1_attn_ni_w"), g("L1_attn_ni_b"), g("L1_attn_no_w"), g("L1_attn_no_b")]),
        "win": np.concatenate([wi[:2 * DI + DS], wi[2 * DI + 2 * DS:], wi[2 * DI + DS:2 * DI + 2 * DS]]).T,
        "wout": g("L1_attn_out_proj_w").T.reshape(2, P, D).transpose(1, 0, 2),
        "alog": np.stack([g("L1_attn_A_log"), g("L1_attn_dt_bias")]),
        "sc_aff": np.stack([np.repeat(g("L1_attn_Dparam"), HP), g("L1_attn_ln_w"), g("L1_attn_ln_b")]),
        "ew1": np.concatenate([g("L1_ffn_W1").transpose(1, 0, 2), g("L1_ffn_W2").reshape(E1, 2, P, D).transpose(2, 0, 1, 3).reshape(P, E1, F1),
                               g("L1_ffn_b1").reshape(E1, 2, P).transpose(2, 0, 1), g("L1_ffn_b2").T[:, :, None]], axis=2),
        "wp": np.concatenate([g("L1_ffn_Wp1"), g("L1_ffn_bp1")[:, None], g("L1_ffn_Wp2")], axis=1),
        "wo1": g("L1_ffn_Wo"),
        "r1": np.concatenate([g("L1_ffn_bp2"), g("L1_ffn_bo")])[None],
        "io1": np.arange(E1, dtype=f)[None] - 64,
        "ones": np.ones((1, P), f),
        "onesq": np.ones((P, P), f),
        "wgT": g("L0_ffn_wg").T,
        "io": np.arange(E, dtype=f) - 64,
        "ltg": np.tril(np.ones((NG, NG), f), -1),
        "ew": np.concatenate([np.stack([g("L0_ffn_w1"), g("L0_ffn_w3"), g("L0_ffn_w2")], axis=2),
                              np.stack([g("L0_ffn_sw1"), g("L0_ffn_sw3"), g("L0_ffn_sw2")], axis=1)[None]]),
    }
    return {n: np.ascontiguousarray(v) for n, v in d.items()}


def kernel(**inputs):
    import concourse.bacc as _bacc
    from concourse.bass_utils import run_bass_kernel_spmd as _run

    nc = _bacc.Bacc("TRN2", target_bir_lowering=False, num_devices=1)
    arrays, args = {}, {}
    for name, v in layout(inputs).items():
        arrays[f"in_{name}_dram"] = v
        args[name] = nc.dram_tensor(f"in_{name}_dram", v.shape, mybir.dt.from_np(v.dtype), kind="ExternalInput").ap()
    out = nc.dram_tensor("out_0_dram", _OUTS[0][0], F32, kind="ExternalOutput").ap()
    build(nc, args, out)
    r = _run(nc, [arrays], core_ids=[0])
    return r.results[0]["out_0_dram"]
```

```python
from contextlib import ExitStack

import concourse.bass as bass
import numpy as np
from concourse import mybir

ALU = mybir.AluOpType
ACT = mybir.ActivationFunctionType
F32 = mybir.dt.float32
BF16 = mybir.dt.bfloat16
X_AX = mybir.AxisListType.X

P = 128
B, S, D = 2, 2048, 128
N = B * S
NT = N // P
NB = N // 512
TB = NT // NB
H, DK, DH = 8, 8, 64
G = 2 * H
UNITS = G * B
EPS = 1e-5
DI, DS, NH1, HP = 256, 64, 4, 64
E1, F1 = 8, 256
HMAX = 10.0
BOUND = 0.9 * HMAX * HMAX
GT = 16
ALPHA, BETA = 0.1, 0.1
KROWS = 9 * DK
TCH = S // P
STEPS = 2 * TCH
DFF = 512
TURN, TURNED = 7, 16
E, NG, KTOP, GTOP = 32, 8, 4, 4
CAP = int(1.25 * N * KTOP / E)
LN4, LN7, LN9 = NB, 3 * NB, 5 * NB


class Chain:

    def __init__(self, eng, sem):
        self.eng, self.sem, self.n, self.base = eng, sem, 0, 0

    def link(self, ins):
        ins.then_inc(self.sem, 1)
        self.n += 1
        self.eng.wait_ge(self.sem, self.base + self.n)


def repeat(eng, trips, body, chain=None, start=0):
    n0 = chain.n if chain else 0
    body(start)
    if trips > 1:
        per = chain.n - n0 if chain else 0
        with eng.Fori(start + 1, start + trips) as j:
            if chain and per:
                chain.base = (j - 1 - start) * per
            body(j)
        if chain and per:
            assert chain.n - n0 == 2 * per
            chain.base, chain.n = 0, n0 + trips * per


def loop_only(eng, start, end, body):
    with eng.Fori(start, end) as j:
        body(j)


def after(eng, sem, count):
    if not isinstance(count, int) or count > 0:
        eng.wait_ge(sem, count)


def layernorm_core(v, ch, src, cen, sq, mean, var, rstd, width, var_ready, std_ready, count):
    shape = list(src.shape)
    ch.link(v.tensor_reduce(mean, src, X_AX, ALU.add))
    ch.link(v.tensor_scalar(mean, mean, 1.0 / width, None, ALU.mult))
    ch.link(v.tensor_tensor(cen, src, mean.unsqueeze(2).broadcast_to(shape), ALU.subtract))
    ch.link(v.tensor_tensor(sq, cen, cen, ALU.mult))
    ch.link(v.tensor_reduce(var, sq, X_AX, ALU.add))
    v.tensor_scalar(var, var, 1.0 / width, EPS, ALU.mult, ALU.add).then_inc(var_ready, 1)
    v.wait_ge(std_ready, count)
    ch.link(v.reciprocal(rstd, rstd))


def build(nc, a, out):
    x_v = a["x"].rearrange("b (t p) d -> p (b t) d", p=P)
    out_v = out.rearrange("b (t p) d -> p (b t) d", p=P)

    with ExitStack() as ctx:
        def sb(name, shape, dt=F32):
            return ctx.enter_context(nc.sbuf_tensor(name, shape, dt))

        def sem(name):
            return ctx.enter_context(nc.semaphore(name))

        def dram(name, shape, dt=F32):
            return nc.dram_tensor(name, shape, dt, kind="Internal").ap()

        xn_d = dram("xn_d", (N, D))
        xct_d = dram("xct_d", (P, N))
        ql_d = dram("ql_d", (3, P, N), BF16)
        kl_d = dram("kl_d", (3, P, N), BF16)
        zs_d = dram("zs_d", (N, DI))
        xs_d = dram("xs_d", (N, DI))
        b_d = dram("b_d", (N, DS))
        bt_d = dram("bt_d", (DS, N))
        ct_d = dram("ct_d", (DS, N))
        lda_d = dram("lda_d", (N, NH1))
        y_d = dram("y_d", (N, DI))
        xe_d = dram("xe_d", (E * CAP, D))
        oe_d = dram("oe_d", (E * CAP + 1, D))
        o_d = dram("o_d", (2, G, 2 * DK, N))

        PS = ctx.enter_context(nc.psum_tensor("PS", [P, 7, 512], F32))
        PT = ctx.enter_context(nc.psum_tensor("PT", [P, 1024], BF16))

        PTF = PT[:, :].bitcast(F32)

        X = sb("X", [P, NT, D])
        ident = sb("ident", [P, P])
        identb = sb("identb", [P, P], BF16)
        cst = sb("cst", [P, a["consts"].shape[1]])
        rows = sb("rows", [P, a["rowc"].shape[1]])
        wsq = sb("wsq", [P, 4, P])
        wff1 = sb("wff1", [P, DFF])
        wff2 = sb("wff2", [P, DFF // P, D])
        bcol = sb("bcol", [P, a["bcol"].shape[1]])
        brow = sb("brow", [1, a["brow"].shape[1]])
        affine = sb("affine", [P, a["affine"].shape[0], P])
        ones1 = sb("ones1", [1, P])
        wgT = sb("wgT", [P, E])
        S0 = sb("S0", [P, NT, D])
        VP = sb("VP", [P, NT, P])

        XNT = sb("XNT", [P, N])
        YM = sb("YM", [P, NT, D])
        EW = [sb(f"EW{i}", [P, 3, P]) for i in range(4)]
        SG = [sb(f"SG{i}", [P, 512]) for i in range(2)]
        HH = [sb(f"HH{i}", [P, 512]) for i in range(2)]
        onesq = sb("onesq", [P, P])
        io = sb("io", [P, E])
        ltg = sb("ltg", [P, NG, NG])
        EK = sb("EK", [P, NT, KTOP])
        WK = sb("WK", [P, NT, KTOP])
        ROW = sb("ROW", [P, NT, KTOP])
        ROWI = sb("ROWI", [P, NT, KTOP], mybir.dt.uint32)
        zt = sb("zt", [P, 2 * D])
        rows_s = [sb(f"rows_s{i}", [P, KTOP], mybir.dt.uint32) for i in range(2)]
        wk_s = [sb(f"wk_s{i}", [P, KTOP]) for i in range(2)]
        xn_s = [sb(f"xn_s{i}", [P, D]) for i in range(2)]
        gs = sb("gs", [P, 3, NT])
        gmx = sb("gmx", [P, NT, NG])

        wa = [sb(f"wa{i}", [P, TB, P]) for i in range(6)]
        st = sb("st", [P, 3, 8])

        stacks = sb("stacks", [P, 8 * S], BF16)
        QS = [stacks[:, i * S:(i + 1) * S] for i in range(4)]
        KS = [stacks[:, (4 + i) * S:(5 + i) * S] for i in range(4)]
        VH = [sb(f"VH{i}", [P, TCH, 32]) for i in range(4)]
        probs = sb("probs", [P, 4 * 1024])
        PR = [probs[:, i * 1024:(i + 1) * 1024] for i in range(4)]
        gt = [stacks[:, i * S:(i + 1) * S].bitcast(F32).rearrange("p (t e) -> p t e", e=E) for i in range(6)]
        gcmp = [probs[:, i * 2048:(i + 1) * 2048].rearrange("p (t g q) -> p t g q", g=NG, q=NG) for i in range(2)]
        stack_f = stacks[:, :].bitcast(F32)
        part_ = lambda i: stack_f[:, i * CAP:(i + 1) * CAP]
        xe_in = [part_(i).rearrange("p (t d) -> p t d", d=D) for i in range(4)]
        xeT, sge, hhe = ([part_(4 + 2 * n + i) for i in range(2)] for n in range(3))
        oe_s = [part_(10 + i) for i in range(2)]
        GB = [stack_f[:, i * KTOP * D:(i + 1) * KTOP * D].rearrange("p (k d) -> p k d", d=D) for i in range(2)]
        XN2 = S0
        S2 = YM
        YS = stacks[:, :].bitcast(F32).rearrange("p (t c) -> p t c", c=DI)
        bs = [sb(f"bs{i}", [P, B, DS]) for i in range(2)]
        DT = sb("DT", [P, NT, NH1])
        dtt = sb("dtt", [P, 2, NT, NH1])
        alog = sb("alog", [P, 3, NH1])
        win = sb("win", [P, 2 * DI + DS + NH1 + DS])
        wout = sb("wout", [P, 2, D])
        sc_aff = sb("sc_aff", [P, 3, DI])
        lb, DE, DM, MM0 = (VP[:, 8 * i:8 * i + 8, :] for i in range(4))
        MM = [MM0, YM[:, 0:8, :]]
        heads = lambda t: t.rearrange("p (b h t) -> p b h t", b=B, h=NH1)
        ym_flat, head_cols = YM.rearrange("p t c -> p (t c)"), B * NH1 * P
        E2 = [heads(probs[0:DS, 0:head_cols]), heads(ym_flat[0:DS, 2560:2560 + head_cols])]
        CTD = [[probs[0:DS, 1024 + b * 512:1536 + b * 512].rearrange("p (h t) -> p h t", h=NH1) for b in range(B)],
               [wa[b][0:DS, :, :] for b in range(B)]]
        E2b = [heads(wa[2 + i].rearrange("p t c -> p (t c)")[0:DS, :].bitcast(BF16)) for i in range(2)]
        RB = [heads(probs[:, 2048 + i * 512:2560 + i * 512].bitcast(BF16)) for i in range(2)]
        DMb = [ym_flat[:, 1024 + i * 512:1536 + i * 512].bitcast(BF16).rearrange("p (i t) -> p i t", t=P) for i in range(2)]
        BD = [heads(t) for t in (probs[:, 3072:3584], ym_flat[:, 2048:2560])]
        ldc = sb("ldc", [P, B, NH1])
        nls = sb("nls", [P, B * NH1])
        HS = sb("HS", [DS, B, NH1, HP])
        hst2 = sb("hst2", [DS, B, NH1, HP])
        VR = sb("VR", [DS, NH1, P], BF16)
        VS = PTF.rearrange("p (h t) -> p h t", h=NH1)
        nmx2 = dtt[:, 0, :, :]
        MXV = sb("MXV", [P, B, TCH, 2 * NH1])
        FW1 = stacks[:, :].bitcast(F32)[:, 0:E1 * (2 * F1 + 3)].rearrange("p (e c) -> p e c", e=E1)
        SW1 = [sb(f"SW1_{b}", [P, 2 * F1 + 3]) for b in range(B)]
        wp = sb("wp", [P, P + 1 + E1])
        wo1 = sb("wo1", [P, D])
        r1 = sb("r1", [1, E1 + D])
        io1 = sb("io1", [1, E1])
        lg1 = sb("lg1", [1, 4, B, E1])
        s1_ = sb("s1_", [1, 2, B])
        hn = sb("hn", [P, B])
        oh = sb("oh", [P, B * E1])

        OE = SG
        mxp = sb("mxp", [P, TCH, 4])
        nmx = sb("nmx", [P, 2, TCH])
        spl = sb("spl", [P, P // TCH, TCH], BF16)
        mT = sb("mT", [3 * TCH, P], BF16)

        vp_flat = VP.rearrange("p t c -> p (t c)")
        wb = [vp_flat[:, i * 512:(i + 1) * 512].rearrange("p (t c) -> p t c", t=2) for i in range(3)]
        ylT = vp_flat[:, 1536:2048]
        hx = bs
        hst = [sb(f"hst_{i}", [2, B, DH]) for i in range(2)]
        hout = [HH[i][0:DH, 0:B * P].rearrange("p (b s) -> p b s", b=B) for i in range(2)]

        dve_chain, act_chain = sem("dve_chain"), sem("act_chain")
        ch = Chain(nc.vector, dve_chain)

        c_ld = sem("c_ld")
        ones_set = sem("ones_set")
        var_ready, std_ready = sem("var_ready"), sem("std_ready")
        xn_ready, xnT_ready, xnT_out = sem("xn_ready"), sem("xnT_ready"), sem("xnT_out")
        xn_st, xct_st, s0_ld = sem("xn_st"), sem("xct_st"), sem("s0_ld")
        hx_ld = [sem("hx_ld0"), sem("hx_ld1")]
        hst_ld, h_state, h_out = (sem(n) for n in ("hst_ld", "h_state", "h_out"))
        h_st = [sem("h_st0"), sem("h_st1")]
        xc_ld, qk_ready, v_ready, q_out, k_out, v_out, qs_ready, ks_ready = (
            sem(n) for n in ("xc_ld", "qk_ready", "v_ready", "q_out", "k_out", "v_out", "qs_ready", "ks_ready"))
        ql_st, kl_st = sem("ql_st"), sem("kl_st")
        qk_ld = [sem(f"qk_ld{i}") for i in range(4)]
        m_ld = [sem(f"m_ld{i}") for i in range(4)]
        vh_ready, mxs_ready, mx_done, spl_ready, mt_ready, mt_out = (
            sem(n) for n in ("vh_ready", "mxs_ready", "mx_done", "spl_ready", "mt_ready", "mt_out"))
        sc_ready, exp_done, pv_done, o_evac = (
            sem(n) for n in ("sc_ready", "exp_done", "pv_done", "o_evac"))
        oe_st = [sem("oe_st0"), sem("oe_st1")]
        at_ld, at_sum, r_ready, y_ready, yT_ready, yT_out, f_ready, f_out, ff_ready, at_free = (
            sem(n) for n in ("at_ld", "at_sum", "r_ready", "y_ready", "yT_ready", "yT_out",
                             "f_ready", "f_out", "ff_ready", "at_free"))
        sp_passed = sem("sp_passed")
        out_st = sem("out_st")
        clip_chain = sem("clip_chain")
        h_zero, h_level, h_carried, vh_set = sem("h_zero"), sem("h_level"), sem("h_carried"), sem("vh_set")
        GROUPS = UNITS // 4
        (xnn_ready, xnnT_ready, xnnT_out, bct_ready, bct_out, bct_st, zx_ready, zx_out,
         bd_ready, bd_out) = (sem(n) for n in ("xnn_ready", "xnnT_ready",
         "xnnT_out", "bct_ready", "bct_out", "bct_st", "zx_ready", "zx_out", "bd_ready", "bd_out"))
        zx_st = [sem("zx_st0"), sem("zx_st1")]
        b_st = [sem("b_st0"), sem("b_st1")]
        exp_in, exp_out, w1_ld = (sem(n) for n in ("exp_in", "exp_out", "w1_ld"))
        c_ld8 = [sem("c_ld8_0"), sem("c_ld8_1")]
        lb_set, la_ready, dif_done, d_done, el_done, dm_done, opb_ready, vr_out, ops_ready, c_done, y_out, hs_done = (
            sem(n) for n in ("lb_set", "la_ready", "dif_done", "d_done", "el_done", "dm_done", "opb_ready", "vr_out", "ops_ready", "c_done", "y_out", "hs_done"))
        bnd_read = sem("bnd_read")
        okv = sb("okv", [P, 1])
        flag = sb("flag", [1, 1], mybir.dt.int32)
        g_x = VP.rearrange("p t c -> p (t c)").rearrange("p (t c) -> p t c", c=DI)
        g_hc = probs.rearrange("p (t c) -> p t c", c=DI)
        g_y = YM.rearrange("p t c -> p (t c)")[0:B, :]
        g_b, g_c = HH[0][:, 0:GT], HH[0][:, GT:2 * GT]
        g_dec = HH[1][:, 0:GT * NH1].rearrange("p (t h) -> p t h", h=NH1)
        g_h = wa[5].rearrange("p t c -> p (t c)")[:, 0:DI].rearrange("p (h q) -> p h q", h=NH1)
        ok_ready, cnt1_ready, flag_set, lda_st, g_ld, g_dec_done, g_hc_done, g_mm, g_y_out, g_st = (
            sem(n) for n in ("ok_ready", "cnt1_ready", "flag_set", "lda_st", "g_ld", "g_dec_done", "g_hc_done", "g_mm", "g_y_out",
                             "g_st"))
        z_ld, fw_ld = sem("z_ld"), sem("fw_ld")
        yl_ready, pr_ready, s2_done = (
            sem(n) for n in ("yl_ready", "pr_ready", "s2_done"))
        a1_ready, a1_out, l1_ready, oh_ready, ohb_ready, sel1_done = (
            sem(n) for n in ("a1_ready", "a1_out", "l1_ready", "oh_ready", "ohb_ready", "sel1_done"))
        fh_ready, fh_out, rt_ready, rt_out, fo_ready, gin_ready, g_ready, fin_ready = (
            sem(n) for n in ("fh_ready", "fh_out", "rt_ready", "rt_out", "fo_ready", "gin_ready", "g_ready", "fin_ready"))
        TRI = cst[:, P + 2:2 * P + 2]

        def aff1(i):
            return affine[:, 4 + i, :].unsqueeze(1).broadcast_to([P, TB, P])
        lg_ready, lg_out, sel_done, cnt_ready, rows_done = (
            sem(n) for n in ("lg_ready", "lg_out", "sel_done", "cnt_ready", "rows_done"))
        ew_ld = [sem(f"ew_ld{i}") for i in range(4)]
        mh_ready, sg_done, hh_done, mo_ready, ym_done, g_done, x1_done = (
            sem(n) for n in ("mh_ready", "sg_done", "hh_done", "mo_ready", "ym_done", "g_done", "x1_done"))
        zero_set, zero_st, staged = sem("zero_set"), sem("zero_st"), sem("staged")
        sc_st = [sem("sc_st0"), sem("sc_st1")]
        xt_ready, xt_out, oe_out = sem("xt_ready"), sem("xt_out"), sem("oe_out")
        oes_st = [sem("oes_st0"), sem("oes_st1")]
        ga_ld = [sem("ga_ld0"), sem("ga_ld1")]
        pool_chain, y_sum = sem("pool_chain"), sem("y_sum")
        FH = PR
        CONSTS = [(ident[:, :], "ident"), (cst[:, :], "consts"), (rows[:, :], "rowc"),
                  (wff1[:, :], "wff1"), (bcol[:, :], "bcol"), (brow[:, :], "brow"), (wsq[:, :, :], "wsq"),
                  (wff2[:, :, :], "wff2"), (ones1[:, :], "ones"),
                  (onesq[:, :], "onesq"), (wgT[:, :], "wgT")]
        CONSTS1 = [(win[:, :], "win"), (wout[:, :, :], "wout"), (wp[:, :], "wp"), (wo1[:, :], "wo1"),
                   (r1[:, :], "r1"), (io1[:, :], "io1")]
        NCONST1 = len(CONSTS1) + 2
        NCONST = len(CONSTS) + 4

        def f_(t):
            return t.rearrange("p t c -> p (t c)")

        def aff(i):
            return affine[:, i, :].unsqueeze(1).broadcast_to([P, TB, P])

        block = ctx.enter_context(nc.Block())

        def load_expert(sp, hold, e, w, shared=False):
            hold(mo_ready, e - 3)
            sp.dma_start(EW[w][:, :, :], a["ew"][bass.ds(e, 1)].rearrange("o p m c -> (o p) m c")).then_inc(ew_ld[w], 16)
            if not shared:
                xe = xe_d[bass.ds(e * CAP, CAP), :].rearrange("(t p) d -> p t d", p=P)
                sp.dma_start(xe_in[w], xe).then_inc(ew_ld[w], 16)

        @block.sync
        def _(sp):
            def hold(sem_, count):
                after(sp, sem_, count)
                if not isinstance(count, int):
                    sp.sem_inc(sp_passed, 1)

            sp.dma_start(X[:, :, :], x_v).then_inc(c_ld, 16)
            for dst, src in CONSTS:
                sp.dma_start(dst, a[src]).then_inc(c_ld, 16)
            sp.dma_start(io[:, :], a["io"].partition_broadcast(P)).then_inc(c_ld, 16)
            sp.dma_start(ltg[:, :, :], a["ltg"].partition_broadcast(P)).then_inc(c_ld, 16)
            sp.dma_start(affine[:, :, :], a["affine"].partition_broadcast(P)).then_inc(c_ld, 16)

            def store_xn(j):
                hold(xn_ready, j + 1)
                sp.dma_start(xn_d.rearrange("(t p) d -> p t d", p=P)[:, bass.ds(j * TB, TB), :], wa[1][:, :, :]).then_inc(xn_st, 16)
                hold(xnT_out, j + 1)
                sp.dma_start(xct_d[0:DH, bass.ds(j * 512, 512)], XNT[0:DH, bass.ds(j * 512, 512)]).then_inc(xct_st, 16)
            repeat(sp, NB, store_xn)

            hold(xn_st, 16 * NB)
            hold(xct_st, 16 * NB)
            hold(h_zero, 1)
            xnb = xn_d.rearrange("(b s) d -> s b d", b=B)
            sp.dma_start(hst[0][0:1, :, :], xnb[0:1, :, 0:DH]).then_inc(hst_ld, 16)

            def holt_tiles(j):
                for w in range(2):
                    t = 2 * j + w
                    hold(h_level, t - 1)
                    sp.dma_start(hx[w][:, :, :], xnb[bass.ds(t * P, P), :, 0:DH]).then_inc(hx_ld[w], 16)
                for w in range(2):
                    t = 2 * j + w
                    hold(h_out, t + 1)
                    sp.dma_start(xct_d.rearrange("d (b s) -> d b s", b=B)[DH:P, :, bass.ds(t * P, P)],
                                 hout[w][:, :, :]).then_inc(h_st[w], 16)
            repeat(sp, TCH // 2, holt_tiles)
            sp.dma_start(S0[:, :, :], xn_d.rearrange("(t p) d -> p t d", p=P)).then_inc(s0_ld, 16)
            for w in range(2):
                hold(h_st[w], 16 * (TCH // 2))

            def qkv_block(j):
                hold(v_ready, j)
                sp.dma_start(f_(wa[0]), xct_d[:, bass.ds(j * 512, 512)]).then_inc(xc_ld, 16)
                for parts, src, ready, stored in ((ql_d, QS, qs_ready, ql_st), (kl_d, KS, ks_ready, kl_st)):
                    hold(ready, j + 1)
                    for lv in range(3):
                        sp.dma_start(parts[lv, :, bass.ds(j * 512, 512)], src[lv][:, 0:512]).then_inc(stored, 16)
            repeat(sp, NB, qkv_block)
            hold(ql_st, 48 * NB)
            hold(kl_st, 48 * NB)
            hold(ones_set, 8)

            def load_unit(u, g, b, w):
                hold(pv_done, TCH * (u - 3))
                for r in range(3):
                    q_src = ql_d[r, bass.ds(g * DK, DK), b * S:(b + 1) * S].unsqueeze(0).broadcast_to([3, DK, S])
                    sp.dma_start(QS[w][24 * r:24 * r + 24, :], q_src).then_inc(qk_ld[w], 16)
                    k_src = kl_d[:, bass.ds(g * DK, DK), b * S:(b + 1) * S]
                    sp.dma_start(KS[w][24 * r:24 * r + 24, :], k_src).then_inc(qk_ld[w], 16)

            def store_half(u, g, b, half):
                hold(o_evac, 2 * u + half + 1)
                for jg in range(4):
                    col = b * S + half * 1024 + (jg % 2) * 512
                    sp.dma_start(o_d[jg // 2, bass.ds(g, 1), :, col:col + 512],
                                 OE[half][32 * jg:32 * jg + 16, :]).then_inc(oe_st[half], 16)

            for u in range(4):
                load_unit(u, u // 2, u % 2, u)

            def load_max(u, w):
                hold(mt_out, u + 1)
                sp.dma_start(QS[w][KROWS:KROWS + 3, :], mT[:, :]).then_inc(m_ld[w], 16)

            load_max(0, 0)
            hold(zero_set, 1)
            sp.dma_start(oe_d[E * CAP:E * CAP + 1, :], zt[0:1, 0:D]).then_inc(zero_st, 16)
            xe_z = xe_d.rearrange("(n p r) d -> p n (r d)", p=P, r=2)
            zn = E * CAP // (2 * P) // (UNITS // 2)

            def group(k, last=False, clear=False):
                for w in range(4):
                    if clear:
                        sp.dma_start(xe_z[:, bass.ds(zn * (4 * k + w), zn), :], zt[:, :].unsqueeze(1).broadcast_to([P, zn, 2 * D])).then_inc(zero_st, 16)
                    u, g = 4 * k + w, 2 * k + w // 2
                    if not (last and w == 3):
                        load_max(u + 1, (w + 1) % 4)
                    store_half(u, g, w % 2, 0)
                    store_half(u, g, w % 2, 1)
                    if not last:
                        load_unit(u + 4, g + 2, w % 2, w)
            repeat(sp, GROUPS // 2, lambda k: group(k, clear=True))
            loop_only(sp, GROUPS // 2, GROUPS - 1, group)
            group(GROUPS - 1, True)

            hold(sc_ready, STEPS * UNITS)
            for w in range(2):
                hold(sc_st[w], 64 * NT // 2)
            for w in range(4):
                load_expert(sp, hold, w, w)

            def experts(k, last=False):
                for w in range(4):
                    e = 4 * k + w
                    hold(oe_out, e + 1)
                    sp.dma_start(oe_d[bass.ds(e * CAP, CAP), :].rearrange("(t p) d -> p t d", p=P),
                                 oe_s[w % 2].rearrange("p (t d) -> p t d", d=D)).then_inc(oes_st[w % 2], 16)
                    if not last:
                        load_expert(sp, hold, e + 4, w)
            repeat(sp, E // 4 - 1, experts)
            experts(E // 4 - 1, True)
            load_expert(sp, hold, E, 0, True)
            for half in range(2):
                hold(oe_st[half], 64 * UNITS)

            def attn_block(j):
                hold(at_free, j)
                c = bass.ds(j * 512, 512)
                for i in range(4):
                    sp.dma_start(f_(wa[i]), o_d[i % 2, :, (i // 2) * DK:(i // 2 + 1) * DK, c]).then_inc(at_ld, 16)
                sp.dma_start(f_(wa[4]), xct_d[:, c]).then_inc(at_ld, 16)
            repeat(sp, NB, attn_block)
            hold(at_free, NB)
            for dst, src in CONSTS1:
                sp.dma_start(dst, a[src]).then_inc(w1_ld, 16)
            sp.dma_start(alog[:, 0:2, :], a["alog"].partition_broadcast(P)).then_inc(w1_ld, 16)
            sp.dma_start(sc_aff[:, :, :], a["sc_aff"].partition_broadcast(P)).then_inc(w1_ld, 16)

            def store_proj(j):
                hold(bct_out, 2 * j + 2)
                sp.dma_start(bt_d[:, bass.ds(j * 512, 512)], HH[0][0:DS, :]).then_inc(bct_st, 16)
                sp.dma_start(ct_d[:, bass.ds(j * 512, 512)], HH[1][0:DS, :]).then_inc(bct_st, 16)
                for t in range(TB):
                    tok = bass.ds((TB * j + t) * P, P)
                    hold(zx_out, 2 * (TB * j + t) + 2)
                    sp.dma_start(zs_d[tok, :], SG[t % 2][:, 0:DI]).then_inc(zx_st[t % 2], 16)
                    sp.dma_start(xs_d[tok, :], SG[t % 2][:, DI:2 * DI]).then_inc(zx_st[t % 2], 16)
                    hold(bd_out, TB * j + t + 1)
                    sp.dma_start(b_d[tok, :], bs[t % 2][:, 0, :]).then_inc(b_st[t % 2], 16)
            repeat(sp, NB, store_proj)
            hold(bct_st, 32 * NB)
            for w in range(2):
                hold(zx_st[w], 32 * NT // 2)
                hold(b_st[w], 16 * NT // 2)

            def load_chunk(k):
                for w in range(2):
                    c = 2 * k + w
                    hold(c_done, c - 1)
                    tok = bass.ds(c * P, P)
                    bview = lambda d: d.rearrange("(b s) n -> s b n", b=B)[tok]
                    tview = lambda d: d.rearrange("n (b s) -> n b s", b=B)[:, :, tok]
                    sp.dma_start(SG[w].rearrange("p (b n) -> p b n", b=B), bview(xs_d)).then_inc(c_ld8[w], 16)
                    sp.dma_start(bs[w][:, :, :], bview(b_d)).then_inc(c_ld8[w], 16)
                    sp.dma_start(HH[w][0:DS, 0:256].rearrange("p (b s) -> p b s", b=B), tview(bt_d)).then_inc(c_ld8[w], 16)
                    sp.dma_start(HH[w][0:DS, 256:512].rearrange("p (b s) -> p b s", b=B), tview(ct_d)).then_inc(c_ld8[w], 16)
            repeat(sp, TCH // 2, load_chunk)
            hold(hs_done, TCH)

            hold(flag_set, 1)
            with sp.If(sp.value_load(flag[:, :], min_val=0, max_val=1) > 0):
                sp.dma_start(lda_d.rearrange("(t p) h -> p t h", p=P), DT[:, :, :]).then_inc(lda_st, 16)
                hold(lda_st, 16)

                def clip_io(k):
                    hold(g_hc_done, k)
                    hold(g_mm, 2 * k)
                    for b in range(B):
                        tok = bass.ds(k * GT + b * S, GT)
                        rows_ = slice(b * DS, (b + 1) * DS)
                        sp.dma_start(g_x[rows_], xs_d[tok, :].partition_broadcast(DS)).then_inc(g_ld, 16)
                        sp.dma_start(g_b[rows_], bt_d[:, tok]).then_inc(g_ld, 16)
                        sp.dma_start(g_c[rows_], ct_d[:, tok]).then_inc(g_ld, 16)
                        sp.dma_start(g_dec[rows_], lda_d[tok, :].partition_broadcast(DS)).then_inc(g_ld, 16)
                    hold(g_y_out, 2 * k + 2)
                    for b in range(B):
                        sp.dma_start(y_d[bass.ds(k * GT + b * S, GT), :].rearrange("t c -> (t c)").unsqueeze(0), g_y[b:b + 1, :]).then_inc(g_st, 16)
                repeat(sp, S // GT, clip_io)
                hold(g_st, 16 * B * S // GT)
                sp.dma_start(YS, y_d.rearrange("(t p) c -> p t c", p=P)).then_inc(g_st, 16)
                hold(g_st, 16 * B * S // GT + 16)

            def load_gate(k):
                hold(yl_ready, k)
                tiles = bass.ds(2 * k, 2)
                sp.dma_start(SG[0].rearrange("p (t c) -> p t c", t=2), xs_d.rearrange("(t p) c -> p t c", p=P)[:, tiles, :]).then_inc(z_ld, 16)
                sp.dma_start(SG[1].rearrange("p (t c) -> p t c", t=2), zs_d.rearrange("(t p) c -> p t c", p=P)[:, tiles, :]).then_inc(z_ld, 16)
            repeat(sp, NT // 2, load_gate)
            hold(s2_done, NT // 2)
            sp.dma_start(FW1, a["ew1"]).then_inc(fw_ld, 16)
            def store_out(j):
                hold(fin_ready, j + 1)
                sp.dma_start(out_v[:, bass.ds(TB * j, TB), :], X[:, bass.ds(TB * j, TB), :]).then_inc(out_st, 16)
            repeat(sp, NB, store_out)
            hold(out_st, 16 * NB)

        @block.vector
        def _(v):
            link = ch.link
            link(v.memset(spl[:, :, :], 0.0))
            v.memset(hst[0][:, :, :], 0.0).then_inc(h_zero, 1)
            v.wait_ge(c_ld, 16 * NCONST)
            link(v.tensor_copy(identb[:, :], ident[:, :]))

            def ln_x(j):
                after(v, xnT_ready, j)
                layernorm_core(v, ch, X[:, bass.ds(j * TB, TB), :], wa[0][:, :, :], wa[3][:, :, :], st[:, 0, 0:TB], st[:, 1, 0:TB],
                               st[:, 2, 0:TB], D, var_ready, std_ready, j + 1)
                after(v, xn_st, 16 * j)
                v.tensor_tensor(wa[1][:, :, :], wa[0][:, :, :], st[:, 2, 0:TB].unsqueeze(2).broadcast_to([P, TB, P]), ALU.mult).then_inc(xn_ready, 1)
                v.wait_ge(xn_ready, j + 1)
            repeat(v, NB, ln_x, ch)

            v.wait_ge(lg_out, 1)
            L, SC, M, T1, T2, SEL = (t[:, :, :] for t in gt)
            tok = lambda col: col.unsqueeze(2).broadcast_to([P, NT, E])
            exps = io[:, :].unsqueeze(1).broadcast_to([P, NT, E])
            s0, s1 = gs[:, 0, :], gs[:, 1, :]
            link(v.tensor_reduce(s0, L, X_AX, ALU.max))
            v.tensor_tensor(L, L, tok(s0), ALU.subtract).then_inc(exp_in, 1)
            v.wait_ge(exp_out, 1)
            link(v.tensor_reduce(s0, SC, X_AX, ALU.add))
            link(v.reciprocal(s0, s0))
            link(v.tensor_tensor(SC, SC, tok(s0), ALU.mult))
            GM = gmx[:, :, :]
            link(v.tensor_reduce(GM.rearrange("p t g -> p (t g)"), SC.rearrange("p t (g q) -> p (t g) q", g=NG), X_AX, ALU.max))
            other = GM.unsqueeze(2).broadcast_to([P, NT, NG, NG])
            own = GM.unsqueeze(3).broadcast_to([P, NT, NG, NG])
            c0, c1 = gcmp[0][:, :, :, :], gcmp[1][:, :, :, :]
            link(v.tensor_tensor(c0, other, own, ALU.is_gt))
            link(v.tensor_tensor(c1, other, own, ALU.is_equal))
            flat = lambda c: c.rearrange("p t g q -> p t (g q)")
            link(v.tensor_tensor(flat(c1), flat(c1), ltg.rearrange("p g q -> p (g q)").unsqueeze(1).broadcast_to([P, NT, NG * NG]), ALU.mult))
            link(v.tensor_tensor(flat(c0), flat(c0), flat(c1), ALU.add))
            link(v.tensor_reduce(GM.rearrange("p t g -> p (t g)"), c0.rearrange("p t g q -> p (t g) q"), X_AX, ALU.add))
            link(v.tensor_scalar(GM, GM, GTOP - 0.5, None, ALU.is_lt))
            keep = GM.rearrange("p t g -> p (t g)").unsqueeze(2).broadcast_to([P, NT * NG, E // NG])
            g4 = lambda t: t.rearrange("p t (g q) -> p (t g) q", g=NG)
            link(v.tensor_tensor(g4(M), g4(SC), keep, ALU.mult))
            link(v.tensor_scalar(g4(T1), keep, 2.0, -2.0, ALU.mult, ALU.add))
            link(v.tensor_tensor(M, M, T1, ALU.add))
            link(v.memset(SEL, 0.0))
            for k in range(KTOP):
                ek, wk = (t[:, :, k:k + 1].broadcast_to([P, NT, E]) for t in (EK, WK))
                link(v.tensor_reduce(WK[:, :, k:k + 1], M.unsqueeze(2), X_AX, ALU.max))
                link(v.tensor_tensor(T1, M, wk, ALU.is_equal))
                link(v.tensor_tensor(T1, T1, exps, ALU.mult))
                link(v.tensor_reduce(EK[:, :, k:k + 1], T1.unsqueeze(2), X_AX, ALU.min))
                link(v.tensor_tensor(T2, exps, ek, ALU.is_equal))
                link(v.tensor_tensor(SEL, SEL, T2, ALU.add))
                link(v.scalar_tensor_tensor(T2.rearrange("p t e -> p (t e)"), T2.rearrange("p t e -> p (t e)"), -4.0, M.rearrange("p t e -> p (t e)"), ALU.mult, ALU.add))
                link(v.tensor_copy(M, T2))
            v.sem_inc(sel_done, 1)
            wsum = s0.unsqueeze(2).broadcast_to([P, NT, KTOP])
            link(v.tensor_reduce(s0, WK[:, :, :], X_AX, ALU.add))
            link(v.tensor_scalar(s0, s0, 1e-9, None, ALU.add))
            link(v.reciprocal(s0, s0))
            link(v.tensor_tensor(WK[:, :, :], WK[:, :, :], wsum, ALU.mult))
            v.wait_ge(cnt_ready, 1)
            bank = lambda i: PS[:, i:i + 2, :].rearrange("p a (t e) -> p (a t) e", e=E)
            link(v.tensor_copy(T1, bank(2)))
            src, dst = T1, T2
            step = 1
            while step < NT:
                link(v.tensor_copy(dst[:, 0:step, :], src[:, 0:step, :]))
                link(v.tensor_tensor(dst[:, step:NT, :], src[:, step:NT, :], src[:, 0:NT - step, :], ALU.add))
                src, dst, step = dst, src, 2 * step
            link(v.tensor_copy(M, bank(0)))
            link(v.tensor_tensor(M[:, 1:NT, :], M[:, 1:NT, :], src[:, 0:NT - 1, :], ALU.add))
            for k in range(KTOP):
                link(v.tensor_tensor(T1, exps, EK[:, :, k:k + 1].broadcast_to([P, NT, E]), ALU.is_equal))
                link(v.tensor_tensor(T1, T1, M, ALU.mult))
                link(v.tensor_reduce(ROW[:, :, k:k + 1], T1.unsqueeze(2), X_AX, ALU.add))
            flat_k = lambda t: t.rearrange("p t k -> p (t k)")
            keep_k, row, ek = SEL[:, :, 0:KTOP], ROW[:, :, :], EK[:, :, :]
            link(v.tensor_scalar(keep_k, row, CAP + 0.5, None, ALU.is_lt))
            link(v.tensor_tensor(WK[:, :, :], WK[:, :, :], keep_k, ALU.mult))
            link(v.scalar_tensor_tensor(flat_k(ROW), flat_k(EK), float(CAP), flat_k(ROW), ALU.mult, ALU.add))
            link(v.tensor_scalar(row, row, float(64 * CAP - 1 - E * CAP), None, ALU.add))
            link(v.tensor_tensor(row, row, keep_k, ALU.mult))
            link(v.tensor_scalar(row, row, float(E * CAP), None, ALU.add))
            v.tensor_copy(ROWI[:, :, :], row).then_inc(rows_done, 1)

            def split_qk(j):
                for full, evacuated, parts, ready, stored in ((wa[1], q_out, QS, qs_ready, ql_st), (wa[2], k_out, KS, ks_ready, kl_st)):
                    f = f_(full)
                    v.wait_ge(evacuated, j + 1)
                    after(v, stored, 48 * j)
                    link(v.tensor_copy(parts[0][:, 0:512], f))
                    link(v.tensor_tensor(f, f, parts[0][:, 0:512], ALU.subtract))
                    link(v.tensor_copy(parts[1][:, 0:512], f))
                    link(v.tensor_tensor(f, f, parts[1][:, 0:512], ALU.subtract))
                    v.tensor_copy(parts[2][:, 0:512], f).then_inc(ready, 1)
            repeat(v, NB, split_qk, ch)

            def write_rows(uu, slot, trip):
                v.wait_ge(mt_ready, uu + 1)
                if slot > 0:
                    v.wait_ge(m_ld[slot - 1], 16 * (trip + 1))
                else:
                    after(v, m_ld[3], 16 * trip)
                v.tensor_copy(mT[:, :], PT[0:3 * TCH, 0:P]).then_inc(mt_out, 1)

            def unit_max(uu, slot, trip):
                for n in range(4 * TCH):
                    v.wait_ge(mxs_ready, 4 * TCH * uu + n + 1)
                    v.tensor_reduce(mxp[:, n // 4, n % 4:n % 4 + 1], PS[:, 5 + n % 2, :], X_AX, ALU.max).then_inc(mx_done, 1)
                    if n == TURNED - 1 and not (slot == 0 and isinstance(uu, int)):
                        write_rows(uu - 1, (slot - 1) % 4, trip - (slot == 0))
                v.wait_ge(mx_done, 4 * TCH * (uu + 1))
                link(v.tensor_reduce(nmx[:, 0, :], mxp[:, :, :], X_AX, ALU.max, negate=True))
                if not (slot == 0 and isinstance(uu, int)):
                    v.wait_ge(mt_ready, uu)
                link(v.tensor_copy(spl[:, 0, :], nmx[:, 0, :]))
                link(v.tensor_tensor(nmx[:, 1, :], nmx[:, 0, :], spl[:, 0, :], ALU.subtract))
                link(v.tensor_copy(spl[:, 1, :], nmx[:, 1, :]))
                link(v.tensor_tensor(nmx[:, 0, :], nmx[:, 1, :], spl[:, 1, :], ALU.subtract))
                v.tensor_copy(spl[:, 2, :], nmx[:, 0, :]).then_inc(spl_ready, 1)

            def group_max(k):
                for w in range(4):
                    unit_max(4 * k + w, w, k)
            repeat(v, GROUPS, group_max, ch)
            write_rows(UNITS - 1, 3, GROUPS - 1)

            def expert_h(e, w):
                v.wait_ge(sg_done, e + 1)
                after(v, mo_ready, e - 1)
                halves = lambda t: t.rearrange("p (h c) -> p h c", h=2)
                v.tensor_tensor(halves(hhe[w % 2]), halves(sge[w % 2]), PS[:, 4:6, 0:CAP // 2], ALU.mult).then_inc(hh_done, 1)

            def expert_out(e, w, uses):
                v.wait_ge(mo_ready, e + 1)
                after(v, oes_st[w % 2], 16 * uses)
                v.tensor_copy(oe_s[w % 2][:, 0:512], PS[:, 6, :])
                v.tensor_copy(oe_s[w % 2][:, 512:CAP], PTF[:, 0:CAP - 512]).then_inc(oe_out, 1)

            def experts(k):
                for w in range(4):
                    expert_h(4 * k + w, w)
                    if not (w == 0 and isinstance(k, int)):
                        expert_out(4 * k + w - 1, (w + 3) % 4, 2 * k + (w + 3) // 2 - 2)
            repeat(v, E // 4, experts)
            expert_out(E - 1, 3, E // 2 - 1)

            def finish_attn(j):
                f = [f_(w_) for w_ in wa]
                v.wait_ge(at_ld, 80 * (j + 1))
                link(v.tensor_tensor(f[0], f[0], f[1], ALU.add))
                link(v.tensor_tensor(f[2], f[2], f[3], ALU.add))
                link(v.reciprocal(f[2], f[2]))
                v.tensor_tensor(f[0], f[0], f[2], ALU.mult).then_inc(at_sum, 1)
                v.wait_ge(r_ready, j + 1)
                half = PS[:, 0, :].rearrange("p (t d) -> p t d", d=DH)
                w8 = [wa[i].rearrange("p t (m d) -> p (t m) d", d=DH) for i in range(6)]
                layernorm_core(v, ch, half, w8[1], w8[2], st[:, 0, :], st[:, 1, :], st[:, 2, :], DH, var_ready, std_ready, LN4 + 2 * j + 1)
                link(v.tensor_tensor(w8[1], w8[1], st[:, 2, :].unsqueeze(2).broadcast_to([P, 2 * TB, DH]), ALU.mult))
                link(v.tensor_tensor(wa[1][:, :, :], wa[1][:, :, :], aff(0), ALU.mult))
                v.tensor_tensor(wa[1][:, :, :], wa[1][:, :, :], aff(1), ALU.add).then_inc(y_ready, 1)
                v.wait_ge(ff_ready, j + 1)
                z = PS[:, 0, :].rearrange("p (t d) -> p t d", d=D)
                layernorm_core(v, ch, z, wa[1][:, :, :], wa[2][:, :, :], st[:, 0, 0:TB], st[:, 1, 0:TB], st[:, 2, 0:TB], D, var_ready, std_ready, LN4 + 2 * j + 2)
                link(v.tensor_tensor(wa[1][:, :, :], wa[1][:, :, :], st[:, 2, 0:TB].unsqueeze(2).broadcast_to([P, TB, P]), ALU.mult))
                link(v.tensor_tensor(wa[1][:, :, :], wa[1][:, :, :], aff(2), ALU.mult))
                v.tensor_tensor(S0[:, bass.ds(j * TB, TB), :], wa[1][:, :, :], aff(3), ALU.add).then_inc(at_free, 1)
            repeat(v, NB, finish_attn, ch)

            def shared_out(j, w):
                v.wait_ge(mo_ready, E + j + 1)
                v.wait_ge(y_sum, TB * j + TB)
                v.tensor_tensor(YM[:, bass.ds(TB * j, TB), :], PS[:, 4 + w, :].rearrange("p (t d) -> p t d", d=D),
                                YM[:, bass.ds(TB * j, TB), :], ALU.add).then_inc(ym_done, 1)

            def shared(k):
                for w in range(2):
                    j = 2 * k + w
                    v.wait_ge(sg_done, E + j + 1)
                    after(v, mo_ready, E + j - 1)
                    v.tensor_tensor(HH[w][:, :], SG[w][:, :], PS[:, 2 + w, :], ALU.mult).then_inc(hh_done, 1)
                    if not (w == 0 and isinstance(k, int)):
                        shared_out(j - 1, 1 - w)
            repeat(v, NB // 2, shared)
            shared_out(NB - 1, 1)
            v.wait_ge(g_done, 1)
            link(v.tensor_tensor(YM[:, :, :], YM[:, :, :], S0[:, :, :], ALU.mult))
            v.tensor_tensor(X[:, :, :], X[:, :, :], YM[:, :, :], ALU.add).then_inc(x1_done, 1)

            v.wait_ge(w1_ld, 16 * NCONST1)
            v.wait_ge(x1_done, 1)
            bc = lambda: st[:, 2, 0:TB].unsqueeze(2).broadcast_to([P, TB, P])

            def ln_x1(j):
                after(v, xnT_ready, NB + j)
                layernorm_core(v, ch, X[:, bass.ds(j * TB, TB), :], wa[0][:, :, :], wa[2][:, :, :], st[:, 0, 0:TB], st[:, 1, 0:TB],
                               st[:, 2, 0:TB], D, var_ready, std_ready, LN7 + 2 * j + 1)
                v.tensor_tensor(wa[1][:, :, :], wa[0][:, :, :], bc(), ALU.mult).then_inc(xn_ready, 1)
                v.wait_ge(xn_ready, NB + j + 1)
                link(v.tensor_copy(XN2[:, bass.ds(j * TB, TB), :], wa[1][:, :, :]))
                layernorm_core(v, ch, wa[1][:, :, :], wa[0][:, :, :], wa[2][:, :, :], st[:, 0, 0:TB], st[:, 1, 0:TB],
                               st[:, 2, 0:TB], D, var_ready, std_ready, LN7 + 2 * j + 2)
                link(v.tensor_tensor(wa[0][:, :, :], wa[0][:, :, :], bc(), ALU.mult))
                link(v.tensor_tensor(wa[0][:, :, :], wa[0][:, :, :], aff1(0), ALU.mult))
                after(v, xnnT_ready, j)
                v.tensor_tensor(wa[4][:, :, :], wa[0][:, :, :], aff1(1), ALU.add).then_inc(xnn_ready, 1)
                for t in range(TB):
                    v.wait_ge(bd_ready, TB * j + t + 1)
                    after(v, b_st[t % 2], 16 * (2 * j + t // 2))
                    link(v.tensor_copy(bs[t % 2][:, 0, :], PS[:, 6, 0:DS]))
                    v.tensor_copy(DT[:, bass.ds(TB * j + t, 1), :], PS[:, 6, DS:DS + NH1].unsqueeze(1)).then_inc(bd_out, 1)
            repeat(v, NB, ln_x1, ch)
            v.wait_ge(bd_out, NT)
            t4 = lambda i: alog[:, i, :].unsqueeze(1).broadcast_to([P, NT, NH1])
            d0, d1, d2 = DT[:, :, :], dtt[:, 0, :, :], dtt[:, 1, :, :]
            link(v.tensor_tensor(d0, d0, t4(1), ALU.add))
            link(v.tensor_scalar(d1, d0, -1.0, None, ALU.mult))
            v.tensor_tensor(d1, d1, d0, ALU.min).then_inc(exp_in, 1)
            v.wait_ge(exp_out, 2)
            link(v.tensor_scalar(d0, d0, 0.0, None, ALU.max))
            link(v.tensor_tensor(d0, d0, d2, ALU.add))
            link(v.tensor_scalar(d0, d0, 0.001, 0.1, ALU.max, ALU.min))
            link(v.tensor_tensor(d0, d0, t4(2), ALU.mult))
            link(v.tensor_scalar(d0, d0, -1.0, float(np.log(0.99)), ALU.mult, ALU.min))

            link(v.memset(HS[:, :, :, :], 0.0))
            link(v.memset(VR[:, :, :], 0.0))
            ldt = DT[:, :, :].rearrange("p (b c) h -> p b c h", b=B)
            hf = lambda t: t.rearrange("p b h n -> p (b h) n")

            def spread_decays(c):
                after(v, la_ready, c)
                link(v.tensor_copy(ldc[:, :, :].unsqueeze(2), ldt[:, :, bass.ds(c, 1), :]))
                v.tensor_copy(lb, ldc.rearrange("p b h -> p (b h)").unsqueeze(2).broadcast_to([P, B * NH1, P])).then_inc(lb_set, 1)

            def chunk_operands(c, w, trip, last=False):
                v.wait_ge(la_ready, c + 1)
                link(v.tensor_copy(nls[:, :], PS[:, 2, 0:B * NH1]))
                for b in range(B):
                    for h in range(NH1):
                        i = b * NH1 + h
                        ins = v.tensor_scalar(DE[:, i, :], PS[:, b, h * P:(h + 1) * P], nls[:, i:i + 1], 0.0, ALU.subtract, ALU.min)
                ins.then_inc(dif_done, 1)
                if not last:
                    spread_decays(c + 1)
                v.wait_ge(c_ld8[w], 64 * (trip + 1))
                x4 = SG[w].rearrange("p (b h n) -> p b h n", b=B, h=NH1)
                v.tensor_tensor(RB[w][:, :, :, 0:HP], x4, x4, ALU.mult)
                for b in range(B):
                    bb = bs[w][:, b, :].unsqueeze(1).broadcast_to([P, NH1, DS])
                    v.tensor_tensor(RB[w][:, b, :, HP:P], bb, bb, ALU.mult)
                v.wait_ge(d_done, c + 1)
                v.tensor_tensor(DM, DE, TRI.unsqueeze(1).broadcast_to([P, B * NH1, P]), ALU.mult).then_inc(dm_done, 1)
                for b in range(B):
                    bb = bs[w][:, b, :].unsqueeze(1).broadcast_to([P, NH1, DS])
                    v.tensor_tensor(BD[w][:, b, :, :], DE[:, b * NH1:(b + 1) * NH1, P - 1:P].broadcast_to([P, NH1, DS]), bb, ALU.mult)
                v.wait_ge(dm_done, c + 1)
                for b in range(B):
                    gg = PS[:, 2, P + b * P:2 * P + b * P].unsqueeze(1).broadcast_to([P, NH1, P])
                    v.tensor_tensor(MM[w][:, b * NH1:(b + 1) * NH1, :], DM[:, b * NH1:(b + 1) * NH1, :], gg, ALU.mult)
                v.wait_ge(el_done, c + 1)
                for b in range(B):
                    cc = HH[w][0:DS, 256 + b * P:256 + (b + 1) * P].unsqueeze(1).broadcast_to([DS, NH1, P])
                    ins = v.tensor_tensor(CTD[w][b], E2[w][:, b, :, :], cc, ALU.mult)
                ins.then_inc(ops_ready, 1)

            def chunk_state(c, w):
                link(v.tensor_tensor(hf(hst2[:, :, :, :]), hf(HS[:, :, :, :]), hf(E2[w])[:, :, P - 1:P].broadcast_to([DS, B * NH1, HP]), ALU.mult))
                v.wait_ge(c_done, c + 1)
                v.tensor_tensor(hf(HS[:, :, :, :]), hf(hst2[:, :, :, :]), PS[0:DS, 4, :].rearrange("p (i n) -> p i n", n=HP), ALU.add).then_inc(hs_done, 1)
                for b in range(B):
                    ins = v.tensor_reduce(MXV[:, b, bass.ds(c, 1), :], PS[:, 5 + b, :].rearrange("p (i n) -> p i n", n=HP).unsqueeze(1), X_AX, ALU.max)
                ins.then_inc(bnd_read, 1)
                v.wait_ge(hs_done, c + 1)

            def two_chunks(k, last=False):
                chunk_operands(2 * k + 1, 1, k, last)
                chunk_state(2 * k, 0)
                if not last:
                    chunk_operands(2 * k + 2, 0, k + 1)
                chunk_state(2 * k + 1, 1)
            spread_decays(0)
            chunk_operands(0, 0, 0)
            repeat(v, TCH // 2 - 1, two_chunks, ch)
            two_chunks(TCH // 2 - 1, True)
            v.wait_ge(bnd_read, TCH)

            mv = MXV.rearrange("p b c (h k) -> p (b c) h k", k=2)
            mp_ = nmx2[:, :, :]
            link(v.tensor_tensor(mp_, mv[:, :, :, 0], mv[:, :, :, 1], ALU.mult))
            link(v.tensor_reduce(okv[:, :], mp_.rearrange("p t h -> p (t h)"), X_AX, ALU.max))
            v.tensor_scalar(okv[:, :], okv[:, :], BOUND, None, ALU.is_lt).then_inc(ok_ready, 1)
            v.wait_ge(cnt1_ready, 1)
            v.tensor_scalar(flag[:, :], PS[0:1, 3, 0:1], P - 0.5, None, ALU.is_lt).then_inc(flag_set, 1)
            v.wait_ge(flag_set, 1)
            with v.If(v.value_load(flag[:, :], min_val=0, max_val=1) > 0):
                cchain = Chain(v, clip_chain)
                cchain.link(v.memset(g_h, 0.0))

                def clip_steps(k):
                    v.wait_ge(g_ld, 8 * 16 * (k + 1))
                    v.wait_ge(g_dec_done, k + 1)
                    after(v, g_mm, 2 * k)
                    for t in range(GT):
                        cchain.link(v.tensor_tensor(g_h, g_h, g_dec[:, t, :].unsqueeze(2).broadcast_to([P, NH1, HP]), ALU.mult))
                        hflat = g_h.rearrange("p h q -> p (h q)")
                        cchain.link(v.scalar_tensor_tensor(hflat, g_x[:, t, :], g_b[:, t:t + 1], hflat, ALU.mult, ALU.add))
                        cchain.link(v.tensor_scalar(hflat, hflat, HMAX, -HMAX, ALU.min, ALU.max))
                        ins = v.tensor_scalar(g_hc[:, t, :], hflat, g_c[:, t:t + 1], None, ALU.mult)
                        if t == GT - 1:
                            ins.then_inc(g_hc_done, 1)
                            v.wait_ge(g_hc_done, k + 1)
                        else:
                            cchain.link(ins)
                repeat(v, S // GT, clip_steps, cchain)
                v.wait_ge(g_st, 16 * B * S // GT + 16)

            def gate(k):
                v.wait_ge(z_ld, 32 * (k + 1))
                y2 = wb[0][:, :, :]
                chan = lambda i: sc_aff[:, i, :].unsqueeze(1).broadcast_to([P, 2, DI])
                g2 = lambda t: t.rearrange("p (t c) -> p t c", t=2)
                link(v.tensor_tensor(y2, g2(SG[0]), chan(0), ALU.mult))
                link(v.tensor_tensor(y2, y2, YS[:, bass.ds(2 * k, 2), :], ALU.add))
                link(v.tensor_tensor(y2, y2, g2(SG[1]), ALU.mult))
                layernorm_core(v, ch, y2, wb[1][:, :, :], wb[2][:, :, :], st[:, 0, 0:2], st[:, 1, 0:2], st[:, 2, 0:2], DI, var_ready, std_ready, LN9 + 2 * k + 1)
                link(v.tensor_tensor(wb[1][:, :, :], wb[1][:, :, :], st[:, 2, 0:2].unsqueeze(2).broadcast_to([P, 2, DI]), ALU.mult))
                link(v.tensor_tensor(wb[1][:, :, :], wb[1][:, :, :], chan(1), ALU.mult))
                v.tensor_tensor(wb[1][:, :, :], wb[1][:, :, :], chan(2), ALU.add).then_inc(yl_ready, 1)
                v.wait_ge(pr_ready, k + 1)
                o = wa[5][:, 0:2, :]
                link(v.tensor_scalar(o, PS[:, 1, 0:2 * D].rearrange("p (t d) -> p t d", t=2), HMAX, -HMAX, ALU.min, ALU.max))
                layernorm_core(v, ch, o, wa[5][:, 2:4, :], wa[3][:, 0:2, :], st[:, 0, 0:2], st[:, 1, 0:2], st[:, 2, 0:2], D, var_ready, std_ready, LN9 + 2 * k + 2)
                o = wa[5][:, 2:4, :]
                link(v.tensor_tensor(o, o, st[:, 2, 0:2].unsqueeze(2).broadcast_to([P, 2, D]), ALU.mult))
                link(v.tensor_tensor(o, o, affine[:, 6, :].unsqueeze(1).broadcast_to([P, 2, D]), ALU.mult))
                v.tensor_tensor(S2[:, bass.ds(2 * k, 2), :], o, affine[:, 7, :].unsqueeze(1).broadcast_to([P, 2, D]), ALU.add).then_inc(s2_done, 1)
                v.wait_ge(s2_done, k + 1)
            repeat(v, NT // 2, gate, ch)

            v.wait_ge(l1_ready, 1)
            q0, q1, q2, q3 = (lg1[:, i, :, :] for i in range(4))
            r_, n_ = s1_[:, 0, :], s1_[:, 1, :]
            b_ = lambda t: t.unsqueeze(2).broadcast_to([1, B, E1])
            link(v.tensor_copy(q0, PS[0:1, 2, 0:B * E1].rearrange("p (b e) -> p b e", b=B)))
            link(v.tensor_reduce(r_, q0, X_AX, ALU.max))
            v.tensor_tensor(q0, q0, b_(r_), ALU.subtract).then_inc(exp_in, 1)
            v.wait_ge(exp_out, 3)
            link(v.tensor_reduce(r_, q1, X_AX, ALU.add))
            link(v.reciprocal(r_, r_))
            link(v.tensor_tensor(q1, q1, b_(r_), ALU.mult))
            link(v.tensor_reduce(r_, q1, X_AX, ALU.max))
            link(v.tensor_tensor(q2, q1, b_(r_), ALU.is_equal))
            ex = io1[:, :].unsqueeze(1).broadcast_to([1, B, E1])
            link(v.tensor_tensor(q2, q2, ex, ALU.mult))
            link(v.tensor_reduce(n_, q2, X_AX, ALU.min))
            v.tensor_tensor(q3, ex, b_(n_), ALU.is_equal).then_inc(oh_ready, 1)
            v.wait_ge(ohb_ready, 1)
            link(v.tensor_copy(oh[:, :], PS[:, 2, 0:B * E1]))
            v.wait_ge(fw_ld, 16)
            for b in range(B):
                link(v.tensor_scalar(SW1[b][:, :], FW1[:, 0, :], oh[:, b * E1:b * E1 + 1], None, ALU.mult))
                for e in range(1, E1):
                    link(v.scalar_tensor_tensor(SW1[b][:, :], FW1[:, e, :], oh[:, b * E1 + e:b * E1 + e + 1], SW1[b][:, :], ALU.mult, ALU.add))
            v.tensor_copy(oh[:, :], oh[:, :]).then_inc(sel1_done, 1)

            def finish(j):
                v.wait_ge(fo_ready, j + 1)
                after(v, fin_ready, j)
                v.scalar_tensor_tensor(f_(wa[0]), PS[:, 5, :], 0.3, XN2[:, bass.ds(TB * j, TB), :].rearrange("p t d -> p (t d)"), ALU.mult, ALU.add).then_inc(gin_ready, 1)
                v.wait_ge(g_ready, j + 1)
                link(v.tensor_tensor(wa[1][:, :, :], wa[1][:, :, :], S2[:, bass.ds(TB * j, TB), :], ALU.mult))
                xb = X[:, bass.ds(TB * j, TB), :]
                v.tensor_tensor(xb, xb, wa[1][:, :, :], ALU.add).then_inc(fin_ready, 1)
            repeat(v, NB, finish, ch)
            v.wait_ge(fin_ready, NB)

        @block.scalar
        def _(act):
            act.wait_ge(c_ld, 16 * NCONST)

            def ln_x(j):
                act.wait_ge(var_ready, j + 1)
                act.activation(st[:, 2, 0:TB], st[:, 1, 0:TB], ACT.Sqrt).then_inc(std_ready, 1)
                act.wait_ge(xnT_ready, j + 1)
                act.activation(XNT[:, bass.ds(j * 512, 512)], PS[:, 0, :], ACT.Copy).then_inc(xnT_out, 1)
            repeat(act, NB, ln_x)

            act.wait_ge(lg_ready, 1)
            act.activation(gt[0].rearrange("p t e -> p (t e)"), PS[:, 0:2, :].rearrange("p a c -> p (a c)"), ACT.Copy).then_inc(lg_out, 1)
            act.wait_ge(exp_in, 1)
            act.activation(gt[1][:, :, :], gt[0][:, :, :], ACT.Exp).then_inc(exp_out, 1)

            def levels(j):
                for w in range(2):
                    act.wait_ge(h_state, 2 * j + w + 1)
                    act.activation(hst[1 - w].rearrange("p b d -> p (b d)"), PS[0:2, 4, 0:P], ACT.Copy).then_inc(h_carried, 1)
                    act.wait_ge(h_level, 2 * j + w + 1)
                    after(act, h_st[w], 16 * j)
                    act.activation(hout[w].rearrange("p b s -> p (b s)"), PS[0:DH, 5 + w, 0:B * P], ACT.Copy).then_inc(h_out, 1)
            repeat(act, TCH // 2, levels)

            def qkv_out(j):
                act.wait_ge(qk_ready, j + 1)
                after(act, qs_ready, j)
                act.activation(f_(wa[1]), PS[:, 4, :], ACT.Identity, bias=bcol[:, 0:1]).then_inc(q_out, 1)
                after(act, ks_ready, j)
                act.activation(f_(wa[2]), PS[:, 5, :], ACT.Identity, bias=bcol[:, 1:2]).then_inc(k_out, 1)
                act.wait_ge(v_ready, j + 1)
                act.activation(VP[:, bass.ds(j * TB, TB), :], PS[:, 6, :].rearrange("p (t c) -> p t c", c=P), ACT.Copy).then_inc(v_out, 1)
            repeat(act, NB, qkv_out)

            def evac(u, trip_halves, half):
                act.wait_ge(pv_done, TCH * u + TCH // 2 * (half + 1))
                after(act, oe_st[half], 64 * u)
                act.activation(OE[half][:, :], PS[:, 4, :], ACT.Copy).then_inc(o_evac, 1)

            def unit_exp(u):
                for i in range(STEPS):
                    T = STEPS * u + i
                    act.wait_ge(sc_ready, T + 1)
                    if i % 2 == 0:
                        after(act, pv_done, TCH * u + i // 2 - 1)
                    act.activation(PR[i % 4][:, :], PS[:, 2 * (i % 2):2 * (i % 2) + 2, :].rearrange("p a c -> p (a c)"), ACT.Exp,
                                   scale=float(1.0 / np.sqrt(np.float32(DK)))).then_inc(exp_done, 1)
                    if i == TCH + 1:
                        evac(u, 0, 0)
                evac(u, 0, 1)

            def group_exp(k):
                for w in range(4):
                    unit_exp(4 * k + w)
            repeat(act, GROUPS, group_exp)

            def turned(e, w):
                act.wait_ge(xt_ready, e + 1)
                after(act, mh_ready, e - 1)
                act.activation(xeT[w % 2], PS[:, 0:2, :].rearrange("p a c -> p (a c)")[:, 0:CAP], ACT.Copy).then_inc(xt_out, 1)

            def experts(k, last=False):
                for w in range(4):
                    e = 4 * k + w
                    if not (last and w == 3):
                        turned(e + 1, w + 1)
                    act.wait_ge(mh_ready, e + 1)
                    after(act, hh_done, e - 1)
                    act.activation(sge[w % 2].rearrange("p (h c) -> p h c", h=2), PS[:, 2:4, 0:CAP // 2], ACT.Silu).then_inc(sg_done, 1)
            turned(0, 0)
            repeat(act, E // 4 - 1, experts)
            experts(E // 4 - 1, True)

            def finish_attn(j):
                act.wait_ge(var_ready, LN4 + 2 * j + 1)
                act.activation(st[:, 2, :], st[:, 1, :], ACT.Sqrt).then_inc(std_ready, 1)
                act.wait_ge(yT_ready, j + 1)
                act.activation(f_(wa[3]), PS[:, 1, :], ACT.Copy).then_inc(yT_out, 1)
                for f in range(DFF // P):
                    act.wait_ge(f_ready, 4 * j + f + 1)
                    act.activation(FH[f][:, 0:512], PS[:, 2 + f, :], ACT.Relu, bias=bcol[:, 2 + f:3 + f]).then_inc(f_out, 1)
                act.wait_ge(var_ready, LN4 + 2 * j + 2)
                act.activation(st[:, 2, 0:TB], st[:, 1, 0:TB], ACT.Sqrt).then_inc(std_ready, 1)
            repeat(act, NB, finish_attn)

            for half in range(2):
                act.wait_ge(oe_st[half], 64 * UNITS)

            def shared(k):
                for w in range(2):
                    act.wait_ge(mh_ready, E + 2 * k + w + 1)
                    act.wait_ge(hh_done, E + 2 * k + w - 1)
                    act.activation(SG[w][:, :], PS[:, w, :], ACT.Silu).then_inc(sg_done, 1)
            repeat(act, NB // 2, shared)
            act.wait_ge(ym_done, NB)
            act.activation(YM[:, :, :], YM[:, :, :], ACT.Silu).then_inc(g_done, 1)

            act.wait_ge(w1_ld, 16 * NCONST1)

            def proj(j):
                for i in range(2):
                    act.wait_ge(var_ready, LN7 + 2 * j + i + 1)
                    act.activation(st[:, 2, 0:TB], st[:, 1, 0:TB], ACT.Sqrt).then_inc(std_ready, 1)
                    if i == 0:
                        act.wait_ge(xnT_ready, NB + j + 1)
                        act.activation(XNT[:, bass.ds(j * 512, 512)], PS[:, 0, :], ACT.Copy).then_inc(xnT_out, 1)
                act.wait_ge(xnnT_ready, j + 1)
                after(act, bd_ready, TB * j)
                act.activation(f_(wa[3]), PS[:, 1, :], ACT.Copy).then_inc(xnnT_out, 1)
                act.wait_ge(bct_ready, j + 1)
                after(act, bct_st, 32 * j)
                act.activation(HH[0][0:DS, :], PS[0:DS, 4, :], ACT.Copy).then_inc(bct_out, 1)
                act.activation(HH[1][0:DS, :], PS[0:DS, 5, :], ACT.Copy).then_inc(bct_out, 1)
                for t in range(TB):
                    act.wait_ge(zx_ready, TB * j + t + 1)
                    after(act, zx_st[t % 2], 32 * (2 * j + t // 2))
                    act.activation(SG[t % 2][:, 0:DI], PS[:, 2 + t % 2, 0:DI], ACT.Silu).then_inc(zx_out, 1)
                    act.activation(SG[t % 2][:, DI:2 * DI], PS[:, 2 + t % 2, DI:2 * DI], ACT.Copy).then_inc(zx_out, 1)
            repeat(act, NB, proj)
            act.wait_ge(exp_in, 2)
            act.activation(alog[:, 2, :], alog[:, 0, :], ACT.Exp)
            act.activation(dtt[:, 1, :, :], dtt[:, 0, :, :], ACT.Exp).then_inc(act_chain, 1)
            act.wait_ge(act_chain, 1)
            act.activation(dtt[:, 1, :, :], dtt[:, 1, :, :], ACT.Ln, bias=1.0).then_inc(exp_out, 1)

            def chunk_exps(c, w):
                act.wait_ge(dif_done, c + 1)
                act.activation(DE, DE, ACT.Exp).then_inc(d_done, 1)
                after(act, hs_done, c - 1)
                sums = PS[0:DS, 0:2, :].rearrange("p b c -> p (b c)")
                act.activation(E2[w].rearrange("p b h t -> p (b h t)"), sums, ACT.Exp).then_inc(el_done, 1)
                act.activation(E2b[w].rearrange("p b h t -> p (b h t)"), sums, ACT.Exp)
                act.wait_ge(dm_done, c + 1)
                act.activation(DMb[w], DM, ACT.Copy).then_inc(opb_ready, 1)

            def chunk_out(c):
                act.wait_ge(c_done, c + 1)
                for b in range(B):
                    act.activation(VR[32 * b:32 * b + 1, :, :], VS[32 * b:32 * b + 1, :, :], ACT.Copy).then_inc(vr_out, 1)
                act.activation(YS.rearrange("p (b c) n -> p b c n", b=B)[:, :, bass.ds(c, 1), :],
                               PS[:, 3, :].rearrange("p (b n) -> p b n", b=B).unsqueeze(2), ACT.Copy).then_inc(y_out, 1)

            def two_chunks(k, last=False):
                chunk_exps(2 * k + 1, 1)
                chunk_out(2 * k)
                if not last:
                    chunk_exps(2 * k + 2, 0)
                chunk_out(2 * k + 1)
            chunk_exps(0, 0)
            repeat(act, TCH // 2 - 1, two_chunks)
            two_chunks(TCH // 2 - 1, True)
            act.wait_ge(flag_set, 1)
            with act.If(act.value_load(flag[:, :], min_val=0, max_val=1) > 0):
                def clip_out(k):
                    act.wait_ge(g_ld, 8 * 16 * (k + 1))
                    act.activation(HH[1][:, 0:GT * NH1], HH[1][:, 0:GT * NH1], ACT.Exp).then_inc(g_dec_done, 1)
                    for i in range(2):
                        act.wait_ge(g_mm, 2 * k + i + 1)
                        if i == 0:
                            after(act, g_st, 16 * B * k)
                        act.activation(g_y[:, i * 2048:(i + 1) * 2048], PS[0:B, 0:4, :].rearrange("p a c -> p (a c)"), ACT.Copy).then_inc(g_y_out, 1)
                repeat(act, S // GT, clip_out)

            def gate(k):
                act.wait_ge(var_ready, LN9 + 2 * k + 1)
                act.activation(st[:, 2, 0:2], st[:, 1, 0:2], ACT.Sqrt).then_inc(std_ready, 1)
                act.wait_ge(yT_ready, NB + k + 1)
                act.activation(ylT[:, :], PS[:, 0, :], ACT.Copy).then_inc(yT_out, 1)
                act.wait_ge(var_ready, LN9 + 2 * k + 2)
                act.activation(st[:, 2, 0:2], st[:, 1, 0:2], ACT.Sqrt).then_inc(std_ready, 1)
            repeat(act, NT // 2, gate)

            act.wait_ge(a1_ready, 1)
            act.activation(hn[:, :], PS[:, 2, 0:B], ACT.Gelu, bias=wp[:, P:P + 1]).then_inc(a1_out, 1)
            act.wait_ge(exp_in, 3)
            act.activation(lg1[:, 1, :, :], lg1[:, 0, :, :], ACT.Exp).then_inc(exp_out, 1)
            act.wait_ge(sel1_done, 1)

            for b in range(B):
                def ff(k, b=b):
                    j = NB // B * b + k
                    for f in range(2):
                        act.wait_ge(fh_ready, 2 * j + f + 1)
                        act.activation(HH[f][:, :], PS[:, 2 + f, :], ACT.Gelu, bias=SW1[b][:, 2 * F1 + f:2 * F1 + f + 1]).then_inc(fh_out, 1)
                    act.wait_ge(rt_ready, j + 1)
                    act.activation(SG[0][:, :], PS[:, 4, :], ACT.Identity, bias=SW1[b][:, 2 * F1 + 2:2 * F1 + 3]).then_inc(rt_out, 1)
                    act.wait_ge(gin_ready, j + 1)
                    after(act, fin_ready, j)
                    act.activation(f_(wa[1]), f_(wa[0]), ACT.Silu).then_inc(g_ready, 1)
                repeat(act, NB // B, ff) if b == 0 else loop_only(act, 0, NB // B, ff)

        @block.gpsimd
        def _(pool):
            for i in range(4):
                pool.memset(VH[i][:, :, :], 1.0).then_inc(vh_set, 1)
            pool.wait_ge(ql_st, 48 * NB)
            pool.wait_ge(kl_st, 48 * NB)
            pool.wait_ge(vh_set, 4)
            for i in range(4):
                pool.memset(QS[i][64:96, :], 1.0).then_inc(ones_set, 1)
                pool.memset(KS[i][64:96, :], 1.0).then_inc(ones_set, 1)
            pool.wait_ge(ones_set, 8)
            pool.wait_ge(v_out, NB)
            pool.memset(zt[:, :], 0.0).then_inc(zero_set, 1)

            def stage_rows(t, i, count, src, dst):
                pool.tensor_copy(rows_s[i][:, :].unsqueeze(1), ROWI[:, bass.ds(t, 1), :]).then_inc(staged, 1)
                pool.tensor_copy(dst, src).then_inc(staged, 1)
                pool.wait_ge(staged, count)
                pool.sem_inc(sp_passed, 1)

            def prepare(k, scatter=False):
                for w in range(4):
                    u, g = 4 * k + w, 2 * k + w // 2
                    after(pool, pv_done, TCH * (u - 3))
                    pool.tensor_copy(VH[w][:, :, 0:DK], VP[:, (w % 2) * TCH:(w % 2 + 1) * TCH, bass.ds(g * DK, DK)]).then_inc(vh_ready, 1)
                    if scatter:
                        uses = 4 * (k - GROUPS // 2) + w
                        for i in range(2):
                            t = 2 * uses + i
                            after(pool, sc_st[i], 64 * uses)
                            stage_rows(t, i, 2 * t + 2, S0[:, bass.ds(t, 1), :], xn_s[i][:, :].unsqueeze(1))
                            for n in range(KTOP):
                                pool.indirect_dma_start(xe_d, bass.IndirectOffsetOnAxis(rows_s[i][:, n:n + 1], 0), xn_s[i][:, :], None,
                                                        bounds_check=E * CAP - 1, oob_is_err=False).then_inc(sc_st[i], 16)
            repeat(pool, GROUPS // 2, prepare)
            pool.wait_ge(rows_done, 1)
            pool.wait_ge(s0_ld, 16)
            pool.wait_ge(zero_st, 16 * (UNITS // 2 + 1))
            repeat(pool, GROUPS // 2, lambda k: prepare(k, True), start=GROUPS // 2)

            for i in range(2):
                pool.wait_ge(sc_st[i], 64 * NT // 2)
                pool.wait_ge(oes_st[i], 16 * E // 2)
            pool_links = Chain(pool, pool_chain)

            def gather(k):
                for i in range(2):
                    t = 2 * k + i
                    stage_rows(t, i, 2 * NT + 2 * t + 2, WK[:, bass.ds(t, 1), :], wk_s[i][:, :].unsqueeze(1))
                    for n in range(KTOP):
                        pool.indirect_dma_start(GB[i][:, n, :], None, oe_d, bass.IndirectOffsetOnAxis(rows_s[i][:, n:n + 1], 0),
                                                bounds_check=E * CAP, oob_is_err=False).then_inc(ga_ld[i], 16)
                for i in range(2):
                    pool.wait_ge(ga_ld[i], 64 * (k + 1))
                    pool_links.link(pool.tensor_tensor(GB[i], GB[i], wk_s[i][:, :].unsqueeze(2).broadcast_to([P, KTOP, D]), ALU.mult))
                    pool_links.link(pool.tensor_tensor(GB[i][:, 0:2, :], GB[i][:, 0:2, :], GB[i][:, 2:4, :], ALU.add))
                    pool.tensor_tensor(YM[:, bass.ds(2 * k + i, 1), :], GB[i][:, 0:1, :], GB[i][:, 1:2, :], ALU.add).then_inc(y_sum, 1)
                pool.wait_ge(y_sum, 2 * k + 2)
            repeat(pool, NT // 2, gather, pool_links)

        @block.tensor
        def _(pe):
            pe.wait_ge(c_ld, 16 * NCONST)

            def turn(j):
                pe.wait_ge(xn_ready, j + 1)
                after(pe, xnT_out, j)
                for t in range(TB):
                    mm = pe.transpose(PS[:, 0, t * P:(t + 1) * P], wa[1][:, t, :], ident[:, :])
                mm.then_inc(xnT_ready, 1)
            repeat(pe, NB, turn)
            pe.wait_ge(xnT_out, NB)
            for t in range(NT):
                mm = pe.matmul(PS[:, t // 16, (t % 16) * E:(t % 16 + 1) * E], XNT[:, t * P:(t + 1) * P], wgT[:, :], start=True, stop=True)
            mm.then_inc(lg_ready, 1)

            def holt(j):
                for w in range(2):
                    t = 2 * j + w
                    pe.wait_ge(hx_ld[w], 16 * (j + 1))
                    if w or not isinstance(j, int):
                        pe.wait_ge(h_carried, t)
                    else:
                        pe.wait_ge(hst_ld, 16)
                    o = PS[0:2, 4, 0:P]
                    pe.matmul(o, cst[:, P:P + 2], hx[w].rearrange("p b d -> p (b d)"), start=True, stop=False)
                    pe.matmul(o, rows[0:2, P:P + 2], hst[w].rearrange("p b d -> p (b d)"), start=False, stop=True).then_inc(h_state, 1)
                    after(pe, h_out, t - 1)
                    for b in range(B):
                        o = PS[0:DH, 5 + w, b * P:(b + 1) * P]
                        pe.matmul(o, hx[w][:, b, :], cst[:, 0:P], start=True, stop=False)
                        mm = pe.matmul(o, hst[w][:, b, :], rows[0:2, 0:P], start=False, stop=True)
                    mm.then_inc(h_level, 1)
            repeat(pe, TCH // 2, holt)
            pe.wait_ge(sel_done, 1)
            pe.wait_ge(lg_out, 1)
            for h in range(2):
                sel = gt[5][:, h * 16:(h + 1) * 16, :].rearrange("p t e -> p (t e)")
                pe.matmul(PS[:, h, :], cst[:, P + 2:2 * P + 2], sel, start=True, stop=True)
                mm = pe.matmul(PS[:, 2 + h, :], onesq[:, :], sel, start=True, stop=True)
            mm.then_inc(cnt_ready, 1)
            pe.wait_ge(h_out, TCH)

            def qkv(j):
                pe.wait_ge(xc_ld, 16 * (j + 1))
                after(pe, k_out, j)
                pe.matmul(PS[:, 4, :], wsq[:, 0, :], f_(wa[0]), start=True, stop=True)
                pe.matmul(PS[:, 5, :], wsq[:, 1, :], f_(wa[0]), start=True, stop=True).then_inc(qk_ready, 1)
                after(pe, v_out, j)
                for t in range(TB):
                    o = PS[:, 6, t * P:(t + 1) * P]
                    pe.matmul(o, wa[0][:, t, :], wsq[:, 2, :], start=True, stop=False)
                    mm = pe.matmul(o, ones1[:, :], brow[:, 0:P], start=False, stop=True)
                mm.then_inc(v_ready, 1)
            repeat(pe, NB, qkv)

            def max_scores(uu, n, w):
                after(pe, mx_done, 4 * TCH * uu + n - 1)
                pe.matmul(PS[:, 5 + n % 2, :], QS[w][0:KROWS, (n // 4) * P:(n // 4 + 1) * P], KS[w][0:KROWS, (n % 4) * 512:(n % 4 + 1) * 512],
                          start=True, stop=True).then_inc(mxs_ready, 1)

            def turn_max(uu):
                pe.wait_ge(spl_ready, uu + 1)
                after(pe, mt_out, uu)
                pe.transpose(PT[:, 0:P], spl.rearrange("p l c -> p (l c)"), identb[:, :]).then_inc(mt_ready, 1)

            def weigh(u, pair, w):
                pe.wait_ge(exp_done, STEPS * u + 2 * pair + 2)
                if pair % (TCH // 2) == 0:
                    after(pe, o_evac, 2 * u + pair // (TCH // 2))
                for odd in range(2):
                    i = 2 * pair + odd
                    kt = i % TCH
                    for qb in range(2):
                        jg = 2 * odd + qb
                        mm = pe.matmul(PS[32 * jg:32 * jg + 32, 4, :], VH[w][:, kt, :], PR[i % 4][:, qb * 512:(qb + 1) * 512],
                                       start=(kt < 2), stop=(kt >= TCH - 2))
                mm.then_inc(pv_done, 1)

            def unit(u, w, trip, last, final):
                nw = (w + 2) % 4
                pe.wait_ge(m_ld[w], 16 * (trip + 1))
                if not last:
                    pe.wait_ge(qk_ld[nw], 96 * (trip + 1 + (w >= 2)))
                n = 0
                for i in range(STEPS):
                    kt, qh = i % TCH, i // TCH
                    after(pe, exp_done, STEPS * u + i - 1)
                    for qb in range(2):
                        q0 = qh * 1024 + qb * 512
                        mm = pe.matmul(PS[:, 2 * (i % 2) + qb, :], KS[w][0:KROWS + 3, kt * P:(kt + 1) * P], QS[w][0:KROWS + 3, q0:q0 + 512],
                                       start=True, stop=True)
                    mm.then_inc(sc_ready, 1)
                    if not last:
                        max_scores(u + 2, n, nw)
                        n += 1
                    if i == 1:
                        pe.wait_ge(vh_ready, u + 1)
                    if i % 2 and i >= 3:
                        weigh(u, (i - 3) // 2, w)
                    if i % 2 and not last:
                        for _ in range(2):
                            max_scores(u + 2, n, nw)
                            n += 1
                    if i == TURN and not final:
                        turn_max(u + 1)
                weigh(u, TCH - 1, w)

            pe.wait_ge(v_out, NB)
            pe.wait_ge(rows_done, 1)
            for u in range(2):
                pe.wait_ge(qk_ld[u], 96)
                for n in range(4 * TCH):
                    max_scores(u, n, u)
                    if u == 1 and n == TURNED - 1:
                        turn_max(0)

            def group(k, last=False):
                for w in range(4):
                    unit(4 * k + w, w, k, last and w >= 2, last and w == 3)
            repeat(pe, GROUPS - 1, group)
            group(GROUPS - 1, True)

            pe.wait_ge(o_evac, 2 * UNITS)
            pe.wait_ge(exp_done, STEPS * UNITS)
            pe.wait_ge(mx_done, 4 * TCH * UNITS)
            pe.wait_ge(mt_out, UNITS)

            def turn_tokens(e, w, trip):
                pe.wait_ge(ew_ld[w], 32 * (trip + 1))
                after(pe, xt_out, e)
                for t in range(CAP // P):
                    mm = pe.transpose(PS[:, t // TB, (t % TB) * P:(t % TB + 1) * P], xe_in[w][:, t, :], ident[:, :])
                mm.then_inc(xt_ready, 1)

            def expert_out(e, w):
                pe.wait_ge(hh_done, e + 1)
                after(pe, oe_out, e)
                for t in range(CAP // P):
                    o = PS[:, 6, t * P:(t + 1) * P] if t < TB else PTF[:, 0:P]
                    mm = pe.matmul(o, hhe[w % 2][:, t * P:(t + 1) * P], EW[w][:, 2, :], start=True, stop=True)
                mm.then_inc(mo_ready, 1)

            def experts(k, last=False):
                for w in range(4):
                    e = 4 * k + w
                    if not (last and w == 3):
                        turn_tokens(e + 1, (w + 1) % 4, k + (w == 3))
                    pe.wait_ge(xt_out, e + 1)
                    after(pe, hh_done, e)
                    for m in range(2):
                        for h in range(2):
                            mm = pe.matmul(PS[:, 2 + 2 * m + h, 0:CAP // 2], EW[w][:, m, :], xeT[w % 2][:, h * CAP // 2:(h + 1) * CAP // 2], start=True, stop=True)
                    mm.then_inc(mh_ready, 1)
                    if w or last or not isinstance(k, int):
                        expert_out(e - 1, (w + 3) % 4)
            turn_tokens(0, 0, 0)
            repeat(pe, E // 4 - 1, experts)
            experts(E // 4 - 1, True)
            expert_out(E - 1, 3)

            pe.wait_ge(hh_done, E)

            def finish_attn(j):
                pe.wait_ge(at_sum, j + 1)
                for t in range(TB):
                    o = PS[:, 0, t * P:(t + 1) * P]
                    pe.matmul(o, wa[0][:, t, :], wsq[:, 3, :], start=True, stop=False)
                    pe.matmul(o, wa[4][:, t, :], ident[:, :], start=False, stop=False)
                    mm = pe.matmul(o, ones1[:, :], brow[:, P:2 * P], start=False, stop=True)
                mm.then_inc(r_ready, 1)
                pe.wait_ge(y_ready, j + 1)
                for t in range(TB):
                    mm = pe.transpose(PS[:, 1, t * P:(t + 1) * P], wa[1][:, t, :], ident[:, :])
                mm.then_inc(yT_ready, 1)
                pe.wait_ge(yT_out, j + 1)
                for f in range(DFF // P):
                    after(pe, f_out, 4 * (j - 1) + f + 1)
                    pe.matmul(PS[:, 2 + f, :], wff1[:, f * P:(f + 1) * P], f_(wa[3]), start=True, stop=True).then_inc(f_ready, 1)
                pe.wait_ge(f_out, 4 * (j + 1))
                for t in range(TB):
                    o = PS[:, 0, t * P:(t + 1) * P]
                    for f in range(DFF // P):
                        pe.matmul(o, FH[f][:, t * P:(t + 1) * P], wff2[:, f, :], start=(f == 0), stop=False)
                    pe.matmul(o, wa[3][:, t, :], ident[:, :], start=False, stop=False)
                    mm = pe.matmul(o, ones1[:, :], brow[:, 2 * P:3 * P], start=False, stop=True)
                mm.then_inc(ff_ready, 1)
            repeat(pe, NB, finish_attn)

            pe.wait_ge(at_free, NB)
            pe.wait_ge(ew_ld[0], 32 * (E // 4) + 16)

            def shared_project(j, w):
                pe.wait_ge(hh_done, E + j + 1)
                after(pe, ym_done, j - 1)
                for t in range(TB):
                    mm = pe.matmul(PS[:, 4 + w, t * P:(t + 1) * P], HH[w][:, t * P:(t + 1) * P], EW[0][:, 2, :], start=True, stop=True)
                mm.then_inc(mo_ready, 1)

            def shared(k):
                for w in range(2):
                    j = 2 * k + w
                    pe.wait_ge(hh_done, E + j - 1)
                    pe.matmul(PS[:, w, :], EW[0][:, 0, :], XNT[:, bass.ds(j * 512, 512)], start=True, stop=True)
                    pe.matmul(PS[:, 2 + w, :], EW[0][:, 1, :], XNT[:, bass.ds(j * 512, 512)], start=True, stop=True).then_inc(mh_ready, 1)
                    if not (w == 0 and isinstance(k, int)):
                        shared_project(j - 1, 1 - w)
            repeat(pe, NB // 2, shared)
            shared_project(NB - 1, 1)

            pe.wait_ge(w1_ld, 16 * NCONST1)
            pe.wait_ge(ym_done, NB)

            def proj(j):
                pe.wait_ge(xn_ready, NB + j + 1)
                after(pe, xnT_out, NB + j)
                for t in range(TB):
                    mm = pe.transpose(PS[:, 0, t * P:(t + 1) * P], wa[1][:, t, :], ident[:, :])
                mm.then_inc(xnT_ready, 1)
                pe.wait_ge(xnn_ready, j + 1)
                after(pe, xnnT_out, j)
                for t in range(TB):
                    mm = pe.transpose(PS[:, 1, t * P:(t + 1) * P], wa[4][:, t, :], ident[:, :])
                mm.then_inc(xnnT_ready, 1)
                pe.wait_ge(xnnT_out, j + 1)
                after(pe, bct_out, 2 * j)
                ob, oc = 2 * DI, 2 * DI + DS + NH1
                pe.matmul(PS[0:DS, 4, :], win[:, ob:ob + DS], f_(wa[3]), start=True, stop=True)
                pe.matmul(PS[0:DS, 5, :], win[:, oc:oc + DS], f_(wa[3]), start=True, stop=True).then_inc(bct_ready, 1)
                for t in range(TB):
                    after(pe, zx_out, 2 * (TB * j + t - 1))
                    pe.matmul(PS[:, 2 + t % 2, :], wa[3][:, t, :], win[:, 0:2 * DI], start=True, stop=True).then_inc(zx_ready, 1)
                    after(pe, bd_out, TB * j + t)
                    pe.matmul(PS[:, 6, 0:DS + NH1], wa[3][:, t, :], win[:, ob:oc], start=True, stop=True).then_inc(bd_ready, 1)
            repeat(pe, NB, proj)
            pe.wait_ge(zx_out, 2 * NT)
            pe.wait_ge(bd_out, NT)

            def chunk_sums(c, w, trip):
                pe.wait_ge(lb_set, c + 1)
                after(pe, ops_ready, c)
                after(pe, opb_ready, c)
                for b in range(B):
                    for h in range(NH1):
                        pe.matmul(PS[:, b, h * P:(h + 1) * P], lb[:, b * NH1 + h, :], TRI, start=True, stop=True)
                pe.matmul(PS[:, 2, 0:B * NH1], TRI, ldc.rearrange("p b h -> p (b h)"), start=True, stop=True)
                pe.wait_ge(c_ld8[w], 64 * (trip + 1))
                for b in range(B):
                    mm = pe.matmul(PS[:, 2, P + b * P:2 * P + b * P], HH[w][0:DS, b * P:(b + 1) * P], HH[w][0:DS, 256 + b * P:256 + (b + 1) * P],
                                   start=True, stop=True)
                mm.then_inc(la_ready, 1)

            def chunk_products(c, w):
                pe.wait_ge(ops_ready, c + 1)
                after(pe, hs_done, c)
                after(pe, y_out, c)
                for b in range(B):
                    for h in range(NH1):
                        i, n = b * NH1 + h, (b * NH1 + h) * HP
                        x = SG[w][:, n:n + HP]
                        pe.matmul(PS[:, 3, n:n + HP], MM[w][:, i, :], x, start=True, stop=False)
                        pe.matmul(PS[:, 3, n:n + HP], CTD[w][b][:, h, :], HS[:, b, h, :], start=False, stop=True)
                        pe.matmul(PS[0:DS, 4, n:n + HP], BD[w][:, b, h, :], x, start=True, stop=True)
                pe.wait_ge(opb_ready, c + 1)
                after(pe, vr_out, 2 * c)
                after(pe, bnd_read, c)
                for b in range(B):
                    r = slice(32 * b, 32 * b + 1)
                    for h in range(NH1):
                        o = PS[:, 5 + b, h * P:(h + 1) * P]
                        pe.matmul(o, DMb[w][:, b * NH1 + h, :], RB[w][:, b, h, :], start=True, stop=False)
                        pe.matmul(o, E2b[w][r, b, h, :], VR[r, h, :], start=False, stop=True)
                        o = VS[r, h, :]
                        pe.matmul(o, DMb[w][:, b * NH1 + h, P - 1:P], RB[w][:, b, h, :], start=True, stop=False)
                        mm = pe.matmul(o, E2b[w][r, b, h, P - 1:P], VR[r, h, :], start=False, stop=True)
                mm.then_inc(c_done, 1)

            def two_chunks(k, last=False):
                chunk_sums(2 * k + 1, 1, k)
                chunk_products(2 * k, 0)
                if not last:
                    chunk_sums(2 * k + 2, 0, k + 1)
                chunk_products(2 * k + 1, 1)
            chunk_sums(0, 0, 0)
            repeat(pe, TCH // 2 - 1, two_chunks)
            two_chunks(TCH // 2 - 1, True)
            pe.wait_ge(bnd_read, TCH)
            pe.wait_ge(y_out, TCH)
            pe.wait_ge(ok_ready, 1)
            pe.matmul(PS[0:1, 3, 0:1], okv[:, :], onesq[:, 0:1], start=True, stop=True).then_inc(cnt1_ready, 1)
            pe.wait_ge(flag_set, 1)
            with pe.If(pe.value_load(flag[:, :], min_val=0, max_val=1) > 0):
                def clip_mm(k):
                    pe.wait_ge(g_hc_done, k + 1)
                    for i in range(2):
                        after(pe, g_y_out, 2 * k + i)
                        for q in range(4):
                            t = 8 * i + 2 * q
                            mm = pe.matmul(PS[0:B, q, :], cst[:, 2 * P + 2:2 * P + 2 + B], g_hc[:, t:t + 2, :].rearrange("p t c -> p (t c)"), start=True, stop=True)
                        mm.then_inc(g_mm, 1)
                repeat(pe, S // GT, clip_mm)
                pe.wait_ge(g_y_out, 2 * S // GT)

            def gate(k):
                pe.wait_ge(yl_ready, k + 1)
                for i in range(4):
                    mm = pe.transpose(PS[:, 0, i * P:(i + 1) * P], wb[1].rearrange("p t (f c) -> p (t f) c", f=2)[:, i, :], ident[:, :])
                mm.then_inc(yT_ready, 1)
                pe.wait_ge(yT_out, NB + k + 1)
                after(pe, s2_done, k)
                for t in range(2):
                    for f in range(2):
                        mm = pe.matmul(PS[:, 1, t * D:(t + 1) * D], ylT[:, (2 * t + f) * P:(2 * t + f + 1) * P], wout[:, f, :], start=(f == 0), stop=(f == 1))
                mm.then_inc(pr_ready, 1)
            repeat(pe, NT // 2, gate)

            pe.wait_ge(xnT_out, NB + NB)
            pe.wait_ge(s2_done, NT // 2)
            pe.matmul(PS[:, 2, 0:B], wp[:, 0:P], XNT.rearrange("p (b s) -> p b s", b=B)[:, :, S - 1], start=True, stop=True).then_inc(a1_ready, 1)
            pe.wait_ge(a1_out, 1)
            for b in range(B):
                o = PS[0:1, 2, b * E1:(b + 1) * E1]
                pe.matmul(o, hn[:, b:b + 1], wp[:, P + 1:P + 1 + E1], start=True, stop=False)
                mm = pe.matmul(o, ones1[:, 0:1], r1[:, 0:E1], start=False, stop=True)
            mm.then_inc(l1_ready, 1)
            pe.wait_ge(oh_ready, 1)
            pe.matmul(PS[:, 2, 0:B * E1], ones1[:, :], lg1[:, 3, :, :].rearrange("p b e -> p (b e)"), start=True, stop=True).then_inc(ohb_ready, 1)
            pe.wait_ge(sel1_done, 1)

            for b in range(B):
                def ff(k, b=b):
                    j = NB // B * b + k
                    xb = XNT[:, bass.ds(j * 512, 512)]
                    for f in range(2):
                        after(pe, fh_out, 2 * (j - 1) + f + 1)
                        pe.matmul(PS[:, 2 + f, :], SW1[b][:, f * P:(f + 1) * P], xb, start=True, stop=True).then_inc(fh_ready, 1)
                    pe.wait_ge(fh_out, 2 * j + 2)
                    for f in range(2):
                        mm = pe.matmul(PS[:, 4, :], SW1[b][:, F1 + f * P:F1 + (f + 1) * P], HH[f][:, :], start=(f == 0), stop=(f == 1))
                    mm.then_inc(rt_ready, 1)
                    pe.wait_ge(rt_out, j + 1)
                    after(pe, gin_ready, j)
                    for t in range(TB):
                        o = PS[:, 5, t * P:(t + 1) * P]
                        pe.matmul(o, SG[0][:, t * P:(t + 1) * P], wo1[:, :], start=True, stop=False)
                        mm = pe.matmul(o, ones1[:, :], r1[:, E1:E1 + D], start=False, stop=True)
                    mm.then_inc(fo_ready, 1)
                repeat(pe, NB // B, ff) if b == 0 else loop_only(pe, 0, NB // B, ff)


def holt_constants():
    al, be = np.float64(ALPHA), np.float64(BETA)
    F = np.array([[1 - al, 1 - al], [be * (1 - al) - be, be * (1 - al) + 1 - be]])
    g = np.array([al, be * al])
    pw = [np.eye(2)]
    for _ in range(P):
        pw.append(F @ pw[-1])
    level = np.zeros((P, P))
    for t in range(P):
        for s in range(t + 1):
            level[s, t] = (pw[t - s] @ g)[0]
    end = np.stack([pw[P - 1 - s] @ g for s in range(P)])
    state = np.stack([pw[t + 1][0] for t in range(P)], axis=1)
    return level, end, state, pw[P].T


_OUTS = [((2, 2048, 128), 'float32')]


def layout(x):
    f = np.float32
    g = lambda n: np.asarray(x[n])

    def pair(name, transpose=True):
        m = np.zeros((P, P), f)
        m[:DH, :DH] = g(f"L0_attn_{name}1").T
        m[DH:, DH:] = g(f"L0_attn_{name}2").T
        return m

    cat = lambda *n: np.concatenate([g("L0_attn_" + i) for i in n])
    level, end, state, full = holt_constants()
    wi = g("L1_attn_in_proj_w")
    tri = np.triu(np.ones((P, P)))
    rowc = np.zeros((P, P + 2), f)
    rowc[0:2, 0:P], rowc[0:2, P:P + 2] = state, full
    d = {
        "x": g("L0_attn_x"),
        "ident": np.eye(P, dtype=f),
        "consts": np.concatenate([level, end, tri, np.repeat(np.eye(B), DS, axis=0)], axis=1).astype(f),
        "rowc": rowc,
        "wsq": np.stack([pair("wq"), pair("wk"), pair("wv"), pair("wo")], axis=1),
        "wff1": g("L0_attn_w_ff1").T,
        "wff2": g("L0_attn_w_ff2").T.reshape(DFF // P, P, D).transpose(1, 0, 2),
        "bcol": np.stack([cat("bq1", "bq2"), cat("bk1", "bk2")] + list(g("L0_attn_b_ff1").reshape(DFF // P, P)), axis=1),
        "brow": np.concatenate([cat("bv1", "bv2"), cat("bo1", "bo2"), g("L0_attn_b_ff2")])[None],
        "affine": np.stack([cat("g1", "g2"), cat("be1", "be2"), g("L0_attn_g_ff"), g("L0_attn_be_ff"),
                            g("L1_attn_ni_w"), g("L1_attn_ni_b"), g("L1_attn_no_w"), g("L1_attn_no_b")]),
        "win": np.concatenate([wi[:2 * DI + DS], wi[2 * DI + 2 * DS:], wi[2 * DI + DS:2 * DI + 2 * DS]]).T,
        "wout": g("L1_attn_out_proj_w").T.reshape(2, P, D).transpose(1, 0, 2),
        "alog": np.stack([g("L1_attn_A_log"), g("L1_attn_dt_bias")]),
        "sc_aff": np.stack([np.repeat(g("L1_attn_Dparam"), HP), g("L1_attn_ln_w"), g("L1_attn_ln_b")]),
        "ew1": np.concatenate([g("L1_ffn_W1").transpose(1, 0, 2), g("L1_ffn_W2").reshape(E1, 2, P, D).transpose(2, 0, 1, 3).reshape(P, E1, F1),
                               g("L1_ffn_b1").reshape(E1, 2, P).transpose(2, 0, 1), g("L1_ffn_b2").T[:, :, None]], axis=2),
        "wp": np.concatenate([g("L1_ffn_Wp1"), g("L1_ffn_bp1")[:, None], g("L1_ffn_Wp2")], axis=1),
        "wo1": g("L1_ffn_Wo"),
        "r1": np.concatenate([g("L1_ffn_bp2"), g("L1_ffn_bo")])[None],
        "io1": np.arange(E1, dtype=f)[None] - 64,
        "ones": np.ones((1, P), f),
        "onesq": np.ones((P, P), f),
        "wgT": g("L0_ffn_wg").T,
        "io": np.arange(E, dtype=f) - 64,
        "ltg": np.tril(np.ones((NG, NG), f), -1),
        "ew": np.concatenate([np.stack([g("L0_ffn_w1"), g("L0_ffn_w3"), g("L0_ffn_w2")], axis=2),
                              np.stack([g("L0_ffn_sw1"), g("L0_ffn_sw3"), g("L0_ffn_sw2")], axis=1)[None]]),
    }
    return {n: np.ascontiguousarray(v) for n, v in d.items()}


def kernel(**inputs):
    import concourse.bacc as _bacc
    from concourse.bass_utils import run_bass_kernel_spmd as _run

    nc = _bacc.Bacc("TRN2", target_bir_lowering=False, num_devices=1)
    arrays, args = {}, {}
    for name, v in layout(inputs).items():
        arrays[f"in_{name}_dram"] = v
        args[name] = nc.dram_tensor(f"in_{name}_dram", v.shape, mybir.dt.from_np(v.dtype), kind="ExternalInput").ap()
    out = nc.dram_tensor("out_0_dram", _OUTS[0][0], F32, kind="ExternalOutput").ap()
    build(nc, args, out)
    r = _run(nc, [arrays], core_ids=[0])
    return r.results[0]["out_0_dram"]
```

```python
from contextlib import ExitStack

import concourse.bass as bass
import numpy as np
from concourse import mybir

ALU = mybir.AluOpType
ACT = mybir.ActivationFunctionType
F32 = mybir.dt.float32
BF16 = mybir.dt.bfloat16
X_AX = mybir.AxisListType.X

P = 128
B, S, D = 2, 2048, 128
N = B * S
NT = N // P
NB = N // 512
TB = NT // NB
H, DK, DH = 8, 8, 64
G = 2 * H
UNITS = G * B
EPS = 1e-5
DI, DS, NH1, HP = 256, 64, 4, 64
E1, F1 = 8, 256
HMAX = 10.0
BOUND = 0.9 * HMAX * HMAX
GT = 16
ALPHA, BETA = 0.1, 0.1
KROWS = 9 * DK
TCH = S // P
STEPS = 2 * TCH
DFF = 512
TURN, TURNED = 7, 16
E, NG, KTOP, GTOP = 32, 8, 4, 4
CAP = int(1.25 * N * KTOP / E)
LN4, LN7, LN9 = NB, 3 * NB, 5 * NB


class Chain:

    def __init__(self, eng, sem):
        self.eng, self.sem, self.n, self.base = eng, sem, 0, 0

    def link(self, ins):
        ins.then_inc(self.sem, 1)
        self.n += 1
        self.eng.wait_ge(self.sem, self.base + self.n)


def repeat(eng, trips, body, chain=None, start=0):
    n0 = chain.n if chain else 0
    body(start)
    if trips > 1:
        per = chain.n - n0 if chain else 0
        with eng.Fori(start + 1, start + trips) as j:
            if chain and per:
                chain.base = (j - 1 - start) * per
            body(j)
        if chain and per:
            assert chain.n - n0 == 2 * per
            chain.base, chain.n = 0, n0 + trips * per


def loop_only(eng, start, end, body, chain=None, per=0):
    n0 = chain.n if chain else 0
    with eng.Fori(start, end) as j:
        if chain:
            chain.base = (j - start) * per
        body(j)
    if chain:
        assert chain.n - n0 == per
        chain.base, chain.n = 0, n0 + (end - start) * per


def after(eng, sem, count):
    if not isinstance(count, int) or count > 0:
        eng.wait_ge(sem, count)


def layernorm_core(v, ch, src, cen, sq, mean, var, rstd, width, var_ready, std_ready, count):
    shape = list(src.shape)
    ch.link(v.tensor_reduce(mean, src, X_AX, ALU.add))
    ch.link(v.tensor_scalar(mean, mean, 1.0 / width, None, ALU.mult))
    ch.link(v.tensor_tensor(cen, src, mean.unsqueeze(2).broadcast_to(shape), ALU.subtract))
    ch.link(v.tensor_tensor(sq, cen, cen, ALU.mult))
    ch.link(v.tensor_reduce(var, sq, X_AX, ALU.add))
    v.tensor_scalar(var, var, 1.0 / width, EPS, ALU.mult, ALU.add).then_inc(var_ready, 1)
    v.wait_ge(std_ready, count)
    ch.link(v.reciprocal(rstd, rstd))


def statistics(v, ch, src, bns, mv, tiles, var_ready, passed):
    for t in range(tiles):
        ins = v.bn_stats(bns[:, t, :], src(t))
    ch.link(ins)
    v.sem_inc(passed, 1)
    for t in range(tiles):
        ins = v.bn_aggr(mv[:, t, :], bns[:, t, :])
    ch.link(ins)
    v.tensor_scalar(mv[:, 0:tiles, 1:2], mv[:, 0:tiles, 1:2], EPS, None, ALU.add).then_inc(var_ready, 1)


def standardise(v, ch, dst, src, mv, tiles, std_ready, count):
    v.wait_ge(std_ready, count)
    ch.link(v.reciprocal(mv[:, 0:tiles, 1:2], mv[:, 0:tiles, 1:2]))
    for t in range(tiles):
        ins = v.tensor_scalar(dst(t), src(t), mv[:, t, 0:1], mv[:, t, 1:2], ALU.subtract, ALU.mult)
    return ins


def build(nc, a, out):
    x_v = a["x"].rearrange("b (t p) d -> p (b t) d", p=P)
    out_v = out.rearrange("b (t p) d -> p (b t) d", p=P)

    with ExitStack() as ctx:
        def sb(name, shape, dt=F32):
            return ctx.enter_context(nc.sbuf_tensor(name, shape, dt))

        def sem(name):
            return ctx.enter_context(nc.semaphore(name))

        def dram(name, shape, dt=F32):
            return nc.dram_tensor(name, shape, dt, kind="Internal").ap()

        xn_d = dram("xn_d", (N, D))
        xct_d = dram("xct_d", (P, N))
        ql_d = dram("ql_d", (3, P, N), BF16)
        kl_d = dram("kl_d", (3, P, N), BF16)
        zs_d = dram("zs_d", (N, DI))
        xs_d = dram("xs_d", (N, DI))
        b_d = dram("b_d", (N, DS))
        bt_d = dram("bt_d", (DS, N))
        ct_d = dram("ct_d", (DS, N))
        lda_d = dram("lda_d", (N, NH1))
        y_d = dram("y_d", (N, DI))
        xe_d = dram("xe_d", (E * CAP, D))
        oe_d = dram("oe_d", (E * CAP + 1, D))
        o_d = dram("o_d", (2, G, 2 * DK, N))

        PS = ctx.enter_context(nc.psum_tensor("PS", [P, 7, 512], F32))
        PT = ctx.enter_context(nc.psum_tensor("PT", [P, 1024], BF16))

        PTF = PT[:, :].bitcast(F32)

        X = sb("X", [P, NT, D])
        ident = sb("ident", [P, P])
        identb = sb("identb", [P, P], BF16)
        cst = sb("cst", [P, a["consts"].shape[1]])
        rows = sb("rows", [P, a["rowc"].shape[1]])
        wsq = sb("wsq", [P, 4, P])
        wff1 = sb("wff1", [P, DFF])
        wff2 = sb("wff2", [P, DFF // P, D])
        bcol = sb("bcol", [P, a["bcol"].shape[1]])
        brow = sb("brow", [1, a["brow"].shape[1]])
        affine = sb("affine", [P, a["affine"].shape[0], P])
        ones1 = sb("ones1", [1, P])
        wgT = sb("wgT", [P, E])
        S0 = sb("S0", [P, NT, D])
        VP = sb("VP", [P, NT, P])

        XNT = sb("XNT", [P, N])
        YM = sb("YM", [P, NT, D])
        EW = [sb(f"EW{i}", [P, 3, P]) for i in range(4)]
        SG = [sb(f"SG{i}", [P, 512]) for i in range(2)]
        HH = [sb(f"HH{i}", [P, 512]) for i in range(2)]
        onesq = sb("onesq", [P, P])
        io = sb("io", [P, E])
        ltg = sb("ltg", [P, NG, NG])
        EK = sb("EK", [P, NT, KTOP])
        WK = sb("WK", [P, NT, KTOP])
        ROW = sb("ROW", [P, NT, KTOP])
        ROWI = sb("ROWI", [P, NT, KTOP], mybir.dt.uint32)
        zt = sb("zt", [P, 2 * D])
        rows_s = [sb(f"rows_s{i}", [P, KTOP], mybir.dt.uint32) for i in range(2)]
        wk_s = [sb(f"wk_s{i}", [P, KTOP]) for i in range(2)]
        xn_s = [sb(f"xn_s{i}", [P, D]) for i in range(2)]
        gs = sb("gs", [P, 1, NT])
        gmx = sb("gmx", [P, NT, NG])

        wa = [sb(f"wa{i}", [P, TB, P]) for i in range(6)]
        st = sb("st", [P, 3, 8])
        bns = sb("bns", [P, TB, 6])
        mv = [sb(f"mv{i}", [P, TB, 2]) for i in range(2)]

        stacks = sb("stacks", [P, 8 * S], BF16)
        QS = [stacks[:, i * S:(i + 1) * S] for i in range(4)]
        KS = [stacks[:, (4 + i) * S:(5 + i) * S] for i in range(4)]
        VH = [sb(f"VH{i}", [P, TCH, 32]) for i in range(4)]
        probs = sb("probs", [P, 4 * 1024])
        PR = [probs[:, i * 1024:(i + 1) * 1024] for i in range(4)]
        gt = [stacks[:, i * S:(i + 1) * S].bitcast(F32).rearrange("p (t e) -> p t e", e=E) for i in range(6)]
        gcmp = [probs[:, i * 2048:(i + 1) * 2048].rearrange("p (t g q) -> p t g q", g=NG, q=NG) for i in range(2)]
        stack_f = stacks[:, :].bitcast(F32)
        part_ = lambda i: stack_f[:, i * CAP:(i + 1) * CAP]
        xe_in = [part_(i).rearrange("p (t d) -> p t d", d=D) for i in range(4)]
        xeT, sge, hhe = ([part_(4 + 2 * n + i) for i in range(2)] for n in range(3))
        oe_s = [part_(10 + i) for i in range(2)]
        GB = [stack_f[:, i * KTOP * D:(i + 1) * KTOP * D].rearrange("p (k d) -> p k d", d=D) for i in range(2)]
        AT = [[stack_f[:, 1024 + (5 * i + n) * 512:1536 + (5 * i + n) * 512] for n in range(5)] for i in range(2)]
        XN2 = S0
        S2 = YM
        YS = stacks[:, :].bitcast(F32).rearrange("p (t c) -> p t c", c=DI)
        bs = [sb(f"bs{i}", [P, B, DS]) for i in range(2)]
        DT = sb("DT", [P, NT, NH1])
        dtt = sb("dtt", [P, 2, NT, NH1])
        alog = sb("alog", [P, 3, NH1])
        win = sb("win", [P, 2 * DI + DS + NH1 + DS])
        wout = sb("wout", [P, 2, D])
        sc_aff = sb("sc_aff", [P, 3, DI])
        lb, DE, DM, MM0 = (VP[:, 8 * i:8 * i + 8, :] for i in range(4))
        MM = [MM0, YM[:, 0:8, :]]
        heads = lambda t: t.rearrange("p (b h t) -> p b h t", b=B, h=NH1)
        ym_flat, head_cols = YM.rearrange("p t c -> p (t c)"), B * NH1 * P
        E2 = [heads(probs[0:DS, 0:head_cols]), heads(ym_flat[0:DS, 2560:2560 + head_cols])]
        CTD = [[probs[0:DS, 1024 + b * 512:1536 + b * 512].rearrange("p (h t) -> p h t", h=NH1) for b in range(B)],
               [wa[b][0:DS, :, :] for b in range(B)]]
        E2b = [heads(wa[2 + i].rearrange("p t c -> p (t c)")[0:DS, :].bitcast(BF16)) for i in range(2)]
        RB = [heads(probs[:, 2048 + i * 512:2560 + i * 512].bitcast(BF16)) for i in range(2)]
        DMb = [ym_flat[:, 1024 + i * 512:1536 + i * 512].bitcast(BF16).rearrange("p (i t) -> p i t", t=P) for i in range(2)]
        BD = [heads(t) for t in (probs[:, 3072:3584], ym_flat[:, 2048:2560])]
        ldc = sb("ldc", [P, B, NH1])
        nls = sb("nls", [P, B * NH1])
        HS = sb("HS", [DS, B, NH1, HP])
        hst2 = sb("hst2", [DS, B, NH1, HP])
        VR = sb("VR", [DS, NH1, P], BF16)
        VS = PTF.rearrange("p (h t) -> p h t", h=NH1)
        nmx2 = dtt[:, 0, :, :]
        MXV = sb("MXV", [P, B, TCH, 2 * NH1])
        FWC, E1P = 2 * F1 + 3, 7
        fw_p = probs[:, 0:E1P * FWC].rearrange("p (e c) -> p e c", e=E1P)
        fw_v = VP.rearrange("p t c -> p (t c)")[:, 2048:2048 + FWC].unsqueeze(1)
        FW1 = [fw_p[:, e, :] if e < E1P else fw_v[:, 0, :] for e in range(E1)]
        SW1 = [sb(f"SW1_{b}", [P, 2 * F1 + 3]) for b in range(B)]
        wp = sb("wp", [P, P + 1 + E1])
        wo1 = sb("wo1", [P, D])
        r1 = sb("r1", [1, E1 + D])
        io1 = sb("io1", [1, E1])
        lg1 = sb("lg1", [1, 4, B, E1])
        s1_ = sb("s1_", [1, 2, B])
        hn = sb("hn", [P, B])
        oh = sb("oh", [P, B * E1])

        OE = SG
        mxp = sb("mxp", [P, TCH, 4])
        nmx = sb("nmx", [P, 2, TCH])
        spl = sb("spl", [P, P // TCH, TCH], BF16)
        mT = sb("mT", [3 * TCH, P], BF16)

        vp_flat = VP.rearrange("p t c -> p (t c)")
        wb = [vp_flat[:, i * 512:(i + 1) * 512].rearrange("p (t c) -> p t c", t=2) for i in range(3)]
        ylT = vp_flat[:, 1536:2048]
        hx = bs
        hst = [sb(f"hst_{i}", [2, B, DH]) for i in range(2)]
        hout = [HH[i][0:DH, 0:B * P].rearrange("p (b s) -> p b s", b=B) for i in range(2)]

        dve_chain, act_chain = sem("dve_chain"), sem("act_chain")
        ch = Chain(nc.vector, dve_chain)

        c_ld = sem("c_ld")
        ones_set = sem("ones_set")
        var_ready, std_ready = sem("var_ready"), sem("std_ready")
        xn_ready, xnT_ready, xnT_out = sem("xn_ready"), sem("xnT_ready"), sem("xnT_out")
        xn_st, xct_st, s0_ld = sem("xn_st"), sem("xct_st"), sem("s0_ld")
        hx_ld = [sem("hx_ld0"), sem("hx_ld1")]
        hst_ld, h_state, h_out = (sem(n) for n in ("hst_ld", "h_state", "h_out"))
        h_st = [sem("h_st0"), sem("h_st1")]
        xc_ld = [sem("xc_ld0"), sem("xc_ld1")]
        qk_ready, v_ready, q_out, k_out, v_out, qs_ready, ks_ready = (
            sem(n) for n in ("qk_ready", "v_ready", "q_out", "k_out", "v_out", "qs_ready", "ks_ready"))
        ql_st, kl_st = sem("ql_st"), sem("kl_st")
        qk_ld = [sem(f"qk_ld{i}") for i in range(4)]
        m_ld = [sem(f"m_ld{i}") for i in range(4)]
        vh_ready, mxs_ready, mx_done, spl_ready, mt_ready, mt_out = (
            sem(n) for n in ("vh_ready", "mxs_ready", "mx_done", "spl_ready", "mt_ready", "mt_out"))
        sc_ready, exp_done, pv_done, o_evac = (
            sem(n) for n in ("sc_ready", "exp_done", "pv_done", "o_evac"))
        oe_st = [sem("oe_st0"), sem("oe_st1")]
        at_ld = [sem("at_ld0"), sem("at_ld1")]
        at_sum, r_ready, y_ready, yT_ready, yT_out, f_ready, f_out, ff_ready, at_free = (
            sem(n) for n in ("at_sum", "r_ready", "y_ready", "yT_ready", "yT_out",
                             "f_ready", "f_out", "ff_ready", "at_free"))
        passed = sem("passed")
        out_st = sem("out_st")
        clip_chain = sem("clip_chain")
        h_zero, h_level, h_carried, vh_set = sem("h_zero"), sem("h_level"), sem("h_carried"), sem("vh_set")
        GROUPS = UNITS // 4
        (xnn_ready, xnnT_ready, xnnT_out, bct_ready, bct_out, bct_st, zx_ready, zx_out,
         bd_ready, bd_out) = (sem(n) for n in ("xnn_ready", "xnnT_ready",
         "xnnT_out", "bct_ready", "bct_out", "bct_st", "zx_ready", "zx_out", "bd_ready", "bd_out"))
        zx_st = [sem("zx_st0"), sem("zx_st1")]
        b_st = [sem("b_st0"), sem("b_st1")]
        exp_in, exp_out, w1_ld = (sem(n) for n in ("exp_in", "exp_out", "w1_ld"))
        c_ld8 = [sem("c_ld8_0"), sem("c_ld8_1")]
        lb_set, la_ready, dif_done, d_done, el_done, dm_done, opb_ready, vr_out, ops_ready, c_done, y_out, hs_done = (
            sem(n) for n in ("lb_set", "la_ready", "dif_done", "d_done", "el_done", "dm_done", "opb_ready", "vr_out", "ops_ready", "c_done", "y_out", "hs_done"))
        bnd_read = sem("bnd_read")
        okv = sb("okv", [P, 1])
        flag = sb("flag", [1, 1], mybir.dt.int32)
        g_x = VP.rearrange("p t c -> p (t c)").rearrange("p (t c) -> p t c", c=DI)
        g_hc = probs.rearrange("p (t c) -> p t c", c=DI)
        g_y = YM.rearrange("p t c -> p (t c)")[0:B, :]
        g_b, g_c = HH[0][:, 0:GT], HH[0][:, GT:2 * GT]
        g_dec = HH[1][:, 0:GT * NH1].rearrange("p (t h) -> p t h", h=NH1)
        g_h = wa[5].rearrange("p t c -> p (t c)")[:, 0:DI].rearrange("p (h q) -> p h q", h=NH1)
        ok_ready, cnt1_ready, flag_set, lda_st, g_ld, g_dec_done, g_hc_done, g_mm, g_y_out, g_st = (
            sem(n) for n in ("ok_ready", "cnt1_ready", "flag_set", "lda_st", "g_ld", "g_dec_done", "g_hc_done", "g_mm", "g_y_out",
                             "g_st"))
        z_ld, fw_ld = sem("z_ld"), sem("fw_ld")
        yl_ready, pr_ready, s2_done = (
            sem(n) for n in ("yl_ready", "pr_ready", "s2_done"))
        a1_ready, a1_out, l1_ready, oh_ready, ohb_ready, sel1_done = (
            sem(n) for n in ("a1_ready", "a1_out", "l1_ready", "oh_ready", "ohb_ready", "sel1_done"))
        fh_ready, fh_out, rt_ready, rt_out, fo_ready, gin_ready, g_ready, fin_ready = (
            sem(n) for n in ("fh_ready", "fh_out", "rt_ready", "rt_out", "fo_ready", "gin_ready", "g_ready", "fin_ready"))
        TRI = cst[:, P + 2:2 * P + 2]

        def aff1(i):
            return affine[:, 4 + i, :].unsqueeze(1).broadcast_to([P, TB, P])
        lg_ready, lg_out, sel_done, rows_done = (
           
            sem(n) for n in ("lg_ready", "lg_out", "sel_done", "rows_done"))
        ew_ld = [sem(f"ew_ld{i}") for i in range(4)]
        mh_ready, sg_done, hh_done, mo_ready, ym_done, g_done, x1_done = (
            sem(n) for n in ("mh_ready", "sg_done", "hh_done", "mo_ready", "ym_done", "g_done", "x1_done"))
        zero_st, staged = sem("zero_st"), sem("staged")
        sc_st = [sem("sc_st0"), sem("sc_st1")]
        xt_ready, xt_out, oe_out = sem("xt_ready"), sem("xt_out"), sem("oe_out")
        oes_st = [sem("oes_st0"), sem("oes_st1")]
        ga_ld = [sem("ga_ld0"), sem("ga_ld1")]
        pool_chain, y_sum = sem("pool_chain"), sem("y_sum")
        FH = PR
        XC, QF, KF = ([wa[n], wa[n + 3]] for n in range(3))
        MXB = [PS[:, 5, :], PS[:, 6, :], PTF]
        TURN_N = TURNED - 1
        assert TURN_N % 3 == 0
        RES = [PS[:, 0, :], PS[:, 6, :]]
        CONSTS = [(ident[:, :], "ident"), (cst[:, :], "consts"), (rows[:, :], "rowc"),
                  (wff1[:, :], "wff1"), (bcol[:, :], "bcol"), (brow[:, :], "brow"), (wsq[:, :, :], "wsq"),
                  (wff2[:, :, :], "wff2"), (ones1[:, :], "ones"),
                  (onesq[:, :], "onesq"), (wgT[:, :], "wgT")]
        CONSTS1 = [(win[:, :], "win"), (wout[:, :, :], "wout"), (wp[:, :], "wp"), (wo1[:, :], "wo1"),
                   (r1[:, :], "r1"), (io1[:, :], "io1")]
        NCONST1 = len(CONSTS1) + 2
        NCONST = len(CONSTS) + 4

        def f_(t):
            return t.rearrange("p t c -> p (t c)")

        def aff(i):
            return affine[:, i, :].unsqueeze(1).broadcast_to([P, TB, P])

        block = ctx.enter_context(nc.Block())

        def load_expert(sp, hold, e, w, shared=False):
            hold(mo_ready, e - 3)
            sp.dma_start(EW[w][:, :, :], a["ew"][bass.ds(e, 1)].rearrange("o p m c -> (o p) m c")).then_inc(ew_ld[w], 16)
            if not shared:
                xe = xe_d[bass.ds(e * CAP, CAP), :].rearrange("(t p) d -> p t d", p=P)
                sp.dma_start(xe_in[w], xe).then_inc(ew_ld[w], 16)

        @block.sync
        def _(sp):
            def hold(sem_, count):
                after(sp, sem_, count)
                if not isinstance(count, int):
                    sp.sem_inc(passed, 1)

            sp.dma_start(X[:, :, :], x_v).then_inc(c_ld, 16)
            for dst, src in CONSTS:
                sp.dma_start(dst, a[src]).then_inc(c_ld, 16)
            sp.dma_start(io[:, :], a["io"].partition_broadcast(P)).then_inc(c_ld, 16)
            sp.dma_start(ltg[:, :, :], a["ltg"].partition_broadcast(P)).then_inc(c_ld, 16)
            sp.dma_start(affine[:, :, :], a["affine"].partition_broadcast(P)).then_inc(c_ld, 16)

            def store_xn(j):
                hold(xn_ready, j + 1)
                sp.dma_start(xn_d.rearrange("(t p) d -> p t d", p=P)[:, bass.ds(j * TB, TB), :], wa[1][:, :, :]).then_inc(xn_st, 16)
                hold(xnT_out, j + 1)
                sp.dma_start(xct_d[0:DH, bass.ds(j * 512, 512)], XNT[0:DH, bass.ds(j * 512, 512)]).then_inc(xct_st, 16)
            repeat(sp, NB, store_xn)

            hold(xn_st, 16 * NB)
            hold(xct_st, 16 * NB)
            hold(h_zero, 1)
            xnb = xn_d.rearrange("(b s) d -> s b d", b=B)
            sp.dma_start(hst[0][0:1, :, :], xnb[0:1, :, 0:DH]).then_inc(hst_ld, 16)

            def holt_tiles(j):
                for w in range(2):
                    t = 2 * j + w
                    hold(h_level, t - 1)
                    sp.dma_start(hx[w][:, :, :], xnb[bass.ds(t * P, P), :, 0:DH]).then_inc(hx_ld[w], 16)
                for w in range(2):
                    t = 2 * j + w
                    hold(h_out, t + 1)
                    sp.dma_start(xct_d.rearrange("d (b s) -> d b s", b=B)[DH:P, :, bass.ds(t * P, P)],
                                 hout[w][:, :, :]).then_inc(h_st[w], 16)
            repeat(sp, TCH // 2, holt_tiles)
            sp.dma_start(S0[:, :, :], xn_d.rearrange("(t p) d -> p t d", p=P)).then_inc(s0_ld, 16)
            for w in range(2):
                hold(h_st[w], 16 * (TCH // 2))

            def load_block(j, w):
                hold(v_ready, j - 1)
                sp.dma_start(f_(XC[w]), xct_d[:, bass.ds(j * 512, 512)]).then_inc(xc_ld[w], 16)

            def qkv_blocks(k, last=False):
                for w in range(2):
                    j = 2 * k + w
                    for parts, src, ready, stored in ((ql_d, QS, qs_ready, ql_st), (kl_d, KS, ks_ready, kl_st)):
                        hold(ready, j + 1)
                        for lv in range(3):
                            sp.dma_start(parts[lv, :, bass.ds(j * 512, 512)], src[lv][:, 0:512]).then_inc(stored, 16)
                    if not last:
                        load_block(j + 2, w)
            load_block(0, 0)
            load_block(1, 1)
            repeat(sp, NB // 2 - 1, qkv_blocks)
            qkv_blocks(NB // 2 - 1, True)
            hold(ql_st, 48 * NB)
            hold(kl_st, 48 * NB)

            def load_unit(u, g, b, w):
                hold(pv_done, TCH * (u - 3))
                for r in range(3):
                    q_src = ql_d[r, bass.ds(g * DK, DK), b * S:(b + 1) * S].unsqueeze(0).broadcast_to([3, DK, S])
                    sp.dma_start(QS[w][24 * r:24 * r + 24, :], q_src).then_inc(qk_ld[w], 16)
                    k_src = kl_d[:, bass.ds(g * DK, DK), b * S:(b + 1) * S]
                    sp.dma_start(KS[w][24 * r:24 * r + 24, :], k_src).then_inc(qk_ld[w], 16)

            def store_half(u, g, b, half):
                hold(o_evac, 2 * u + half + 1)
                for jg in range(4):
                    col = b * S + half * 1024 + (jg % 2) * 512
                    sp.dma_start(o_d[jg // 2, bass.ds(g, 1), :, col:col + 512],
                                 OE[half][32 * jg:32 * jg + 16, :]).then_inc(oe_st[half], 16)

            for u in range(4):
                hold(ones_set, 2 * u + 2)
                load_unit(u, u // 2, u % 2, u)

            def load_max(u, w):
                hold(mt_out, u + 1)
                sp.dma_start(QS[w][KROWS:KROWS + 3, :], mT[:, :]).then_inc(m_ld[w], 16)

            load_max(0, 0)
            hold(ones_set, 9)
            sp.dma_start(oe_d[E * CAP:E * CAP + 1, :], zt[0:1, 0:D]).then_inc(zero_st, 16)
            xe_z = xe_d.rearrange("(n p r) d -> p n (r d)", p=P, r=2)
            zn = E * CAP // (2 * P) // (UNITS // 2)

            def group(k, last=False, clear=False):
                for w in range(4):
                    if clear:
                        sp.dma_start(xe_z[:, bass.ds(zn * (4 * k + w), zn), :], zt[:, :].unsqueeze(1).broadcast_to([P, zn, 2 * D])).then_inc(zero_st, 16)
                    u, g = 4 * k + w, 2 * k + w // 2
                    if not (last and w == 3):
                        load_max(u + 1, (w + 1) % 4)
                    store_half(u, g, w % 2, 0)
                    store_half(u, g, w % 2, 1)
                    if not last:
                        load_unit(u + 4, g + 2, w % 2, w)
            repeat(sp, GROUPS // 2, lambda k: group(k, clear=True))
            loop_only(sp, GROUPS // 2, GROUPS - 1, group)
            group(GROUPS - 1, True)

            hold(sc_ready, STEPS * UNITS)
            for w in range(2):
                hold(sc_st[w], 64 * NT // 2)
            for w in range(4):
                load_expert(sp, hold, w, w)

            def experts(k, last=False):
                for w in range(4):
                    e = 4 * k + w
                    hold(oe_out, e + 1)
                    sp.dma_start(oe_d[bass.ds(e * CAP, CAP), :].rearrange("(t p) d -> p t d", p=P),
                                 oe_s[w % 2].rearrange("p (t d) -> p t d", d=D)).then_inc(oes_st[w % 2], 16)
                    if not last:
                        load_expert(sp, hold, e + 4, w)
            repeat(sp, E // 4 - 1, experts)
            experts(E // 4 - 1, True)
            load_expert(sp, hold, E, 0, True)
            for half in range(2):
                hold(oe_st[half], 64 * UNITS)

            def attn_blocks(k):
                for w in range(2):
                    j = 2 * k + w
                    hold(r_ready, j - 1)
                    c = bass.ds(j * 512, 512)
                    for i in range(4):
                        sp.dma_start(AT[w][i], o_d[i % 2, :, (i // 2) * DK:(i // 2 + 1) * DK, c]).then_inc(at_ld[w], 16)
                    sp.dma_start(AT[w][4], xct_d[:, c]).then_inc(at_ld[w], 16)
            hold(oes_st[0], 16 * E // 2)
            hold(oes_st[1], 16 * E // 2)
            repeat(sp, NB // 2, attn_blocks)
            hold(at_free, NB)
            for dst, src in CONSTS1:
                sp.dma_start(dst, a[src]).then_inc(w1_ld, 16)
            sp.dma_start(alog[:, 0:2, :], a["alog"].partition_broadcast(P)).then_inc(w1_ld, 16)
            sp.dma_start(sc_aff[:, :, :], a["sc_aff"].partition_broadcast(P)).then_inc(w1_ld, 16)

            def store_proj(j):
                hold(bd_out, j + 1)
                for i in range(2):
                    sp.dma_start(b_d[bass.ds((TB * j + 2 * i) * P, 2 * P), :].rearrange("(t p) n -> p t n", p=P), bs[i][:, :, :]).then_inc(b_st[i], 16)
                hold(bct_out, 2 * j + 2)
                sp.dma_start(bt_d[:, bass.ds(j * 512, 512)], HH[0][0:DS, :]).then_inc(bct_st, 16)
                sp.dma_start(ct_d[:, bass.ds(j * 512, 512)], HH[1][0:DS, :]).then_inc(bct_st, 16)
                for t in range(TB):
                    tok = bass.ds((TB * j + t) * P, P)
                    hold(zx_out, 2 * (TB * j + t) + 2)
                    sp.dma_start(zs_d[tok, :], SG[t % 2][:, 0:DI]).then_inc(zx_st[t % 2], 16)
                    sp.dma_start(xs_d[tok, :], SG[t % 2][:, DI:2 * DI]).then_inc(zx_st[t % 2], 16)
            repeat(sp, NB, store_proj)
            hold(bct_st, 32 * NB)
            for w in range(2):
                hold(zx_st[w], 32 * NT // 2)
                hold(b_st[w], 16 * NB)

            def load_chunk(k):
                for w in range(2):
                    c = 2 * k + w
                    hold(c_done, c - 1)
                    tok = bass.ds(c * P, P)
                    bview = lambda d: d.rearrange("(b s) n -> s b n", b=B)[tok]
                    tview = lambda d: d.rearrange("n (b s) -> n b s", b=B)[:, :, tok]
                    sp.dma_start(SG[w].rearrange("p (b n) -> p b n", b=B), bview(xs_d)).then_inc(c_ld8[w], 16)
                    sp.dma_start(bs[w][:, :, :], bview(b_d)).then_inc(c_ld8[w], 16)
                    sp.dma_start(HH[w][0:DS, 0:256].rearrange("p (b s) -> p b s", b=B), tview(bt_d)).then_inc(c_ld8[w], 16)
                    sp.dma_start(HH[w][0:DS, 256:512].rearrange("p (b s) -> p b s", b=B), tview(ct_d)).then_inc(c_ld8[w], 16)
            repeat(sp, TCH // 2, load_chunk)
            hold(hs_done, TCH)

            hold(flag_set, 1)
            with sp.If(sp.value_load(flag[:, :], min_val=0, max_val=1) > 0):
                sp.dma_start(lda_d.rearrange("(t p) h -> p t h", p=P), DT[:, :, :]).then_inc(lda_st, 16)
                hold(lda_st, 16)

                def clip_io(k):
                    hold(g_hc_done, k)
                    hold(g_mm, 2 * k)
                    for b in range(B):
                        tok = bass.ds(k * GT + b * S, GT)
                        rows_ = slice(b * DS, (b + 1) * DS)
                        sp.dma_start(g_x[rows_], xs_d[tok, :].partition_broadcast(DS)).then_inc(g_ld, 16)
                        sp.dma_start(g_b[rows_], bt_d[:, tok]).then_inc(g_ld, 16)
                        sp.dma_start(g_c[rows_], ct_d[:, tok]).then_inc(g_ld, 16)
                        sp.dma_start(g_dec[rows_], lda_d[tok, :].partition_broadcast(DS)).then_inc(g_ld, 16)
                    hold(g_y_out, 2 * k + 2)
                    for b in range(B):
                        sp.dma_start(y_d[bass.ds(k * GT + b * S, GT), :].rearrange("t c -> (t c)").unsqueeze(0), g_y[b:b + 1, :]).then_inc(g_st, 16)
                repeat(sp, S // GT, clip_io)
                hold(g_st, 16 * B * S // GT)
                sp.dma_start(YS, y_d.rearrange("(t p) c -> p t c", p=P)).then_inc(g_st, 16)
                hold(g_st, 16 * B * S // GT + 16)

            sp.dma_start(fw_p, a["ew1"][:, 0:E1P, :]).then_inc(fw_ld, 16)
            sp.dma_start(fw_v, a["ew1"][:, E1P:E1, :]).then_inc(fw_ld, 16)

            def load_gate(k):
                hold(var_ready, LN9 + 2 * k - 1 if not isinstance(k, int) else 0)
                tiles = bass.ds(2 * k, 2)
                sp.dma_start(SG[0].rearrange("p (t c) -> p t c", t=2), xs_d.rearrange("(t p) c -> p t c", p=P)[:, tiles, :]).then_inc(z_ld, 16)
                sp.dma_start(SG[1].rearrange("p (t c) -> p t c", t=2), zs_d.rearrange("(t p) c -> p t c", p=P)[:, tiles, :]).then_inc(z_ld, 16)
            repeat(sp, NT // 2, load_gate)
            def store_out(j):
                hold(fin_ready, j + 1)
                sp.dma_start(out_v[:, bass.ds(TB * j, TB), :], X[:, bass.ds(TB * j, TB), :]).then_inc(out_st, 16)
            repeat(sp, NB, store_out)
            hold(out_st, 16 * NB)

        @block.vector
        def _(v):
            link = ch.link
            link(v.memset(spl[:, :, :], 0.0))
            v.memset(hst[0][:, :, :], 0.0).then_inc(h_zero, 1)
            v.wait_ge(c_ld, 16 * NCONST)
            link(v.tensor_copy(identb[:, :], ident[:, :]))

            def tile_x(j):
                return lambda t: X[:, bass.ds(j * TB + t, 1), :].rearrange("p o d -> p (o d)")

            def stats_x(j, w):
                statistics(v, ch, tile_x(j), bns, mv[w], TB, var_ready, passed)

            def norm_x(j, w):
                after(v, xnT_ready, j)
                after(v, xn_st, 16 * j)
                standardise(v, ch, lambda t: wa[1][:, t, :], tile_x(j), mv[w], TB, std_ready, j + 1).then_inc(xn_ready, 1)

            def ln_x(k, last=False):
                for w in range(2):
                    if not (last and w == 1):
                        stats_x(2 * k + w + 1, 1 - w)
                    norm_x(2 * k + w, w)
            stats_x(0, 0)
            repeat(v, NB // 2 - 1, ln_x, ch)
            ln_x(NB // 2 - 1, True)

            v.wait_ge(lg_out, 1)
            L, SC, M, T1, T2, SEL = (t[:, :, :] for t in gt)
            tok = lambda col: col.unsqueeze(2).broadcast_to([P, NT, E])
            exps = io[:, :].unsqueeze(1).broadcast_to([P, NT, E])
            s0 = gs[:, 0, :]
            link(v.tensor_reduce(s0, L, X_AX, ALU.max))
            v.tensor_tensor(L, L, tok(s0), ALU.subtract).then_inc(exp_in, 1)
            v.wait_ge(exp_out, 1)
            link(v.tensor_reduce(s0, SC, X_AX, ALU.add))
            link(v.reciprocal(s0, s0))
            link(v.tensor_tensor(SC, SC, tok(s0), ALU.mult))
            GM = gmx[:, :, :]
            link(v.tensor_reduce(GM.rearrange("p t g -> p (t g)"), SC.rearrange("p t (g q) -> p (t g) q", g=NG), X_AX, ALU.max))
            other = GM.unsqueeze(2).broadcast_to([P, NT, NG, NG])
            own = GM.unsqueeze(3).broadcast_to([P, NT, NG, NG])
            c0, c1 = gcmp[0][:, :, :, :], gcmp[1][:, :, :, :]
            link(v.tensor_tensor(c0, other, own, ALU.is_gt))
            link(v.tensor_tensor(c1, other, own, ALU.is_equal))
            flat = lambda c: c.rearrange("p t g q -> p t (g q)")
            link(v.tensor_tensor(flat(c1), flat(c1), ltg.rearrange("p g q -> p (g q)").unsqueeze(1).broadcast_to([P, NT, NG * NG]), ALU.mult))
            link(v.tensor_tensor(flat(c0), flat(c0), flat(c1), ALU.add))
            link(v.tensor_reduce(GM.rearrange("p t g -> p (t g)"), c0.rearrange("p t g q -> p (t g) q"), X_AX, ALU.add))
            link(v.tensor_scalar(GM, GM, GTOP - 0.5, None, ALU.is_lt))
            keep = GM.rearrange("p t g -> p (t g)").unsqueeze(2).broadcast_to([P, NT * NG, E // NG])
            g4 = lambda t: t.rearrange("p t (g q) -> p (t g) q", g=NG)
            link(v.tensor_tensor(g4(M), g4(SC), keep, ALU.mult))
            link(v.tensor_scalar(g4(T1), keep, 2.0, -2.0, ALU.mult, ALU.add))
            link(v.tensor_tensor(M, M, T1, ALU.add))
            link(v.memset(SEL, 0.0))
            for k in range(KTOP):
                ek, wk = (t[:, :, k:k + 1].broadcast_to([P, NT, E]) for t in (EK, WK))
                link(v.tensor_reduce(WK[:, :, k:k + 1], M.unsqueeze(2), X_AX, ALU.max))
                link(v.tensor_tensor(T1, M, wk, ALU.is_equal))
                link(v.tensor_tensor(T1, T1, exps, ALU.mult))
                link(v.tensor_reduce(EK[:, :, k:k + 1], T1.unsqueeze(2), X_AX, ALU.min))
                link(v.tensor_tensor(T2, exps, ek, ALU.is_equal))
                link(v.tensor_tensor(SEL, SEL, T2, ALU.add))
                link(v.scalar_tensor_tensor(T2.rearrange("p t e -> p (t e)"), T2.rearrange("p t e -> p (t e)"), -4.0, M.rearrange("p t e -> p (t e)"), ALU.mult, ALU.add))
                link(v.tensor_copy(M, T2))
            v.sem_inc(sel_done, 1)
            wsum = s0.unsqueeze(2).broadcast_to([P, NT, KTOP])
            link(v.tensor_reduce(s0, WK[:, :, :], X_AX, ALU.add))
            link(v.tensor_scalar(s0, s0, 1e-9, None, ALU.add))
            link(v.reciprocal(s0, s0))
            link(v.tensor_tensor(WK[:, :, :], WK[:, :, :], wsum, ALU.mult))
            v.wait_ge(lg_ready, 2)
            bank = lambda i: PS[:, i:i + 2, :].rearrange("p a (t e) -> p (a t) e", e=E)
            link(v.tensor_copy(T1, bank(2)))
            src, dst = T1, T2
            step = 1
            while step < NT:
                link(v.tensor_copy(dst[:, 0:step, :], src[:, 0:step, :]))
                link(v.tensor_tensor(dst[:, step:NT, :], src[:, step:NT, :], src[:, 0:NT - step, :], ALU.add))
                src, dst, step = dst, src, 2 * step
            link(v.tensor_copy(M, bank(0)))
            link(v.tensor_tensor(M[:, 1:NT, :], M[:, 1:NT, :], src[:, 0:NT - 1, :], ALU.add))
            for k in range(KTOP):
                link(v.tensor_tensor(T1, exps, EK[:, :, k:k + 1].broadcast_to([P, NT, E]), ALU.is_equal))
                link(v.tensor_tensor(T1, T1, M, ALU.mult))
                link(v.tensor_reduce(ROW[:, :, k:k + 1], T1.unsqueeze(2), X_AX, ALU.add))
            flat_k = lambda t: t.rearrange("p t k -> p (t k)")
            keep_k, row, ek = SEL[:, :, 0:KTOP], ROW[:, :, :], EK[:, :, :]
            link(v.tensor_scalar(keep_k, row, CAP + 0.5, None, ALU.is_lt))
            link(v.tensor_tensor(WK[:, :, :], WK[:, :, :], keep_k, ALU.mult))
            link(v.scalar_tensor_tensor(flat_k(ROW), flat_k(EK), float(CAP), flat_k(ROW), ALU.mult, ALU.add))
            link(v.tensor_scalar(row, row, float(64 * CAP - 1 - E * CAP), None, ALU.add))
            link(v.tensor_tensor(row, row, keep_k, ALU.mult))
            link(v.tensor_scalar(row, row, float(E * CAP), None, ALU.add))
            v.tensor_copy(ROWI[:, :, :], row).then_inc(rows_done, 1)

            def split_qk(k):
                for w in range(2):
                    j = 2 * k + w
                    for full, evacuated, parts, ready, stored in ((QF[w], q_out, QS, qs_ready, ql_st), (KF[w], k_out, KS, ks_ready, kl_st)):
                        f = f_(full)
                        v.wait_ge(evacuated, j + 1)
                        after(v, stored, 48 * j)
                        link(v.tensor_copy(parts[0][:, 0:512], f))
                        link(v.tensor_tensor(f, f, parts[0][:, 0:512], ALU.subtract))
                        link(v.tensor_copy(parts[1][:, 0:512], f))
                        link(v.tensor_tensor(f, f, parts[1][:, 0:512], ALU.subtract))
                        v.tensor_copy(parts[2][:, 0:512], f).then_inc(ready, 1)
            repeat(v, NB // 2, split_qk, ch)

            def write_rows(uu, slot, trip):
                v.wait_ge(mt_ready, uu + 1)
                if slot > 0:
                    v.wait_ge(m_ld[slot - 1], 16 * (trip + 1))
                else:
                    after(v, m_ld[3], 16 * trip)
                v.tensor_copy(mT[:, :], PT[0:3 * TCH, 0:P]).then_inc(mt_out, 1)

            def unit_max(uu, slot, trip):
                for n in range(4 * TCH):
                    v.wait_ge(mxs_ready, 4 * TCH * uu + n + 1)
                    v.tensor_reduce(mxp[:, n // 4, n % 4:n % 4 + 1], MXB[n % 3], X_AX, ALU.max).then_inc(mx_done, 1)
                    if n == TURNED - 1 and not (slot == 0 and isinstance(uu, int)):
                        write_rows(uu - 1, (slot - 1) % 4, trip - (slot == 0))
                v.wait_ge(mx_done, 4 * TCH * (uu + 1))
                link(v.tensor_reduce(nmx[:, 0, :], mxp[:, :, :], X_AX, ALU.max, negate=True))
                if not (slot == 0 and isinstance(uu, int)):
                    v.wait_ge(mt_ready, uu)
                link(v.tensor_copy(spl[:, 0, :], nmx[:, 0, :]))
                link(v.tensor_tensor(nmx[:, 1, :], nmx[:, 0, :], spl[:, 0, :], ALU.subtract))
                link(v.tensor_copy(spl[:, 1, :], nmx[:, 1, :]))
                link(v.tensor_tensor(nmx[:, 0, :], nmx[:, 1, :], spl[:, 1, :], ALU.subtract))
                v.tensor_copy(spl[:, 2, :], nmx[:, 0, :]).then_inc(spl_ready, 1)

            def group_max(k):
                for w in range(4):
                    unit_max(4 * k + w, w, k)
            repeat(v, GROUPS, group_max, ch)
            write_rows(UNITS - 1, 3, GROUPS - 1)

            def expert_h(e, w):
                v.wait_ge(sg_done, e + 1)
                after(v, mo_ready, e - 1)
                halves = lambda t: t.rearrange("p (h c) -> p h c", h=2)
                v.tensor_tensor(halves(hhe[w % 2]), halves(sge[w % 2]), PS[:, 4:6, 0:CAP // 2], ALU.mult).then_inc(hh_done, 1)

            def expert_out(e, w, uses):
                v.wait_ge(mo_ready, e + 1)
                after(v, oes_st[w % 2], 16 * uses)
                v.tensor_copy(oe_s[w % 2][:, 0:512], PS[:, 6, :])
                v.tensor_copy(oe_s[w % 2][:, 512:CAP], PTF[:, 0:CAP - 512]).then_inc(oe_out, 1)

            def experts(k):
                for w in range(4):
                    expert_h(4 * k + w, w)
                    if not (w == 0 and isinstance(k, int)):
                        expert_out(4 * k + w - 1, (w + 3) % 4, 2 * k + (w + 3) // 2 - 2)
            repeat(v, E // 4, experts)
            expert_out(E - 1, 3, E // 2 - 1)

            def normalise(w, trip):
                f = AT[w]
                v.wait_ge(at_ld[w], 80 * (trip + 1))
                v.tensor_tensor(f[0], f[0], f[1], ALU.add)
                link(v.tensor_tensor(f[2], f[2], f[3], ALU.add))
                link(v.reciprocal(f[2], f[2]))
                v.tensor_tensor(f[0], f[0], f[2], ALU.mult).then_inc(at_sum, 1)

            def ln_half(j, w, count):
                v.wait_ge(r_ready, j + 1)
                half = RES[w].rearrange("p (t d) -> p t d", d=DH)
                w8 = [wa[i].rearrange("p t (m d) -> p (t m) d", d=DH) for i in range(2)]
                layernorm_core(v, ch, half, w8[0], w8[1], st[:, 0, :], st[:, 1, :], st[:, 2, :], DH, var_ready, std_ready, count)
                link(v.tensor_tensor(w8[0], w8[0], st[:, 2, :].unsqueeze(2).broadcast_to([P, 2 * TB, DH]), ALU.mult))
                link(v.tensor_tensor(wa[0][:, :, :], wa[0][:, :, :], aff(0), ALU.mult))
                after(v, yT_ready, j)
                v.tensor_tensor(wa[2][:, :, :], wa[0][:, :, :], aff(1), ALU.add).then_inc(y_ready, 1)
                v.wait_ge(y_ready, j + 1)

            def ln_ff(j, last=False):
                v.wait_ge(ff_ready, j + 1)
                z = PTF.rearrange("p (t d) -> p t d", d=D)
                layernorm_core(v, ch, z, wa[0][:, :, :], wa[1][:, :, :], st[:, 0, 0:TB], st[:, 1, 0:TB], st[:, 2, 0:TB], D, var_ready, std_ready, LN4 + 2 * j + 3 - last)
                link(v.tensor_tensor(wa[0][:, :, :], wa[0][:, :, :], st[:, 2, 0:TB].unsqueeze(2).broadcast_to([P, TB, P]), ALU.mult))
                link(v.tensor_tensor(wa[0][:, :, :], wa[0][:, :, :], aff(2), ALU.mult))
                v.tensor_tensor(S0[:, bass.ds(j * TB, TB), :], wa[0][:, :, :], aff(3), ALU.add).then_inc(at_free, 1)
                v.wait_ge(at_free, j + 1)

            def finish_attn(k, last=False):
                for w in range(2):
                    j = 2 * k + w
                    if not last:
                        normalise(w, k + 1)
                    if not (last and w == 1):
                        ln_half(j + 1, 1 - w, LN4 + 2 * j + 2)
                    ln_ff(j, last and w == 1)
            normalise(0, 0)
            normalise(1, 0)
            ln_half(0, 0, LN4 + 1)
            repeat(v, NB // 2 - 1, finish_attn, ch)
            finish_attn(NB // 2 - 1, True)

            def shared_out(j, w):
                v.wait_ge(mo_ready, E + j + 1)
                v.wait_ge(y_sum, TB * j + TB)
                v.tensor_tensor(YM[:, bass.ds(TB * j, TB), :], PS[:, 4 + w, :].rearrange("p (t d) -> p t d", d=D),
                                YM[:, bass.ds(TB * j, TB), :], ALU.add).then_inc(ym_done, 1)

            def shared(k):
                for w in range(2):
                    j = 2 * k + w
                    v.wait_ge(sg_done, E + j + 1)
                    after(v, mo_ready, E + j - 1)
                    v.tensor_tensor(HH[w][:, :], SG[w][:, :], PS[:, 2 + w, :], ALU.mult).then_inc(hh_done, 1)
                    if not (w == 0 and isinstance(k, int)):
                        shared_out(j - 1, 1 - w)
            repeat(v, NB // 2, shared)
            shared_out(NB - 1, 1)
            v.wait_ge(g_done, 1)
            link(v.tensor_tensor(YM[:, :, :], YM[:, :, :], S0[:, :, :], ALU.mult))
            v.tensor_tensor(X[:, :, :], X[:, :, :], YM[:, :, :], ALU.add).then_inc(x1_done, 1)

            v.wait_ge(w1_ld, 16 * NCONST1)
            v.wait_ge(x1_done, 1)
            def ln_x1(j):
                first, second, xn1, out1 = wa[0], wa[2], wa[1], wa[4]
                x1 = X[:, bass.ds(j * TB, TB), :]
                statistics(v, ch, lambda t: X[:, bass.ds(j * TB + t, 1), :].rearrange("p o d -> p (o d)"), bns, mv[0], TB, var_ready, passed)
                after(v, xnT_out, NB + j)
                v.wait_ge(std_ready, LN7 + 2 * j + 1)
                link(v.reciprocal(mv[0][:, :, 1:2], mv[0][:, :, 1:2]))
                link(v.tensor_tensor(first[:, :, :], x1, mv[0][:, :, 0:1].broadcast_to([P, TB, P]), ALU.subtract))
                v.tensor_tensor(xn1[:, :, :], first[:, :, :], mv[0][:, :, 1:2].broadcast_to([P, TB, P]), ALU.mult).then_inc(xn_ready, 1)
                v.wait_ge(xn_ready, NB + j + 1)
                statistics(v, ch, lambda t: xn1[:, t, :], bns, mv[1], TB, var_ready, passed)
                link(standardise(v, ch, lambda t: second[:, t, :], lambda t: xn1[:, t, :], mv[1], TB, std_ready, LN7 + 2 * j + 2))
                link(v.tensor_tensor(second[:, :, :], second[:, :, :], aff1(0), ALU.mult))
                after(v, xnnT_ready, j)
                v.tensor_tensor(out1[:, :, :], second[:, :, :], aff1(1), ALU.add).then_inc(xnn_ready, 1)

            def b_dt_out(j):
                v.wait_ge(bd_ready, j + 1)
                tiles = PS[:, 6, 0:TB * (DS + NH1)].rearrange("p (t c) -> p t c", t=TB)
                for i in range(2):
                    after(v, b_st[i], 16 * j)
                    v.tensor_copy(bs[i][:, :, :], tiles[:, 2 * i:2 * i + 2, 0:DS])
                v.tensor_copy(DT[:, bass.ds(TB * j, TB), :], tiles[:, :, DS:DS + NH1]).then_inc(bd_out, 1)

            def block(j):
                ln_x1(j + 1)
                b_dt_out(j)
            ln_x1(0)
            repeat(v, NB - 1, block, ch)
            b_dt_out(NB - 1)
            v.wait_ge(bd_out, NB)
            t4 = lambda i: alog[:, i, :].unsqueeze(1).broadcast_to([P, NT, NH1])
            d0, d1, d2 = DT[:, :, :], dtt[:, 0, :, :], dtt[:, 1, :, :]
            link(v.tensor_tensor(d0, d0, t4(1), ALU.add))
            link(v.tensor_scalar(d1, d0, -1.0, None, ALU.mult))
            v.tensor_tensor(d1, d1, d0, ALU.min).then_inc(exp_in, 1)
            v.wait_ge(exp_out, 2)
            link(v.tensor_scalar(d0, d0, 0.0, None, ALU.max))
            link(v.tensor_tensor(d0, d0, d2, ALU.add))
            link(v.tensor_scalar(d0, d0, 0.001, 0.1, ALU.max, ALU.min))
            link(v.tensor_tensor(d0, d0, t4(2), ALU.mult))
            link(v.tensor_scalar(d0, d0, -1.0, float(np.log(0.99)), ALU.mult, ALU.min))

            link(v.memset(HS[:, :, :, :], 0.0))
            link(v.memset(VR[:, :, :], 0.0))
            ldt = DT[:, :, :].rearrange("p (b c) h -> p b c h", b=B)
            hf = lambda t: t.rearrange("p b h n -> p (b h) n")

            def spread_decays(c):
                after(v, la_ready, c)
                link(v.tensor_copy(ldc[:, :, :].unsqueeze(2), ldt[:, :, bass.ds(c, 1), :]))
                v.tensor_copy(lb, ldc.rearrange("p b h -> p (b h)").unsqueeze(2).broadcast_to([P, B * NH1, P])).then_inc(lb_set, 1)

            def chunk_operands(c, w, trip, last=False):
                v.wait_ge(la_ready, c + 1)
                link(v.tensor_copy(nls[:, :], PS[:, 2, 0:B * NH1]))
                for b in range(B):
                    for h in range(NH1):
                        i = b * NH1 + h
                        ins = v.tensor_scalar(DE[:, i, :], PS[:, b, h * P:(h + 1) * P], nls[:, i:i + 1], 0.0, ALU.subtract, ALU.min)
                ins.then_inc(dif_done, 1)
                if not last:
                    spread_decays(c + 1)
                v.wait_ge(c_ld8[w], 64 * (trip + 1))
                x4 = SG[w].rearrange("p (b h n) -> p b h n", b=B, h=NH1)
                v.tensor_tensor(RB[w][:, :, :, 0:HP], x4, x4, ALU.mult)
                for b in range(B):
                    bb = bs[w][:, b, :].unsqueeze(1).broadcast_to([P, NH1, DS])
                    v.tensor_tensor(RB[w][:, b, :, HP:P], bb, bb, ALU.mult)
                v.wait_ge(d_done, c + 1)
                v.tensor_tensor(DM, DE, TRI.unsqueeze(1).broadcast_to([P, B * NH1, P]), ALU.mult).then_inc(dm_done, 1)
                for b in range(B):
                    bb = bs[w][:, b, :].unsqueeze(1).broadcast_to([P, NH1, DS])
                    v.tensor_tensor(BD[w][:, b, :, :], DE[:, b * NH1:(b + 1) * NH1, P - 1:P].broadcast_to([P, NH1, DS]), bb, ALU.mult)
                v.wait_ge(dm_done, c + 1)
                for b in range(B):
                    gg = PS[:, 2, P + b * P:2 * P + b * P].unsqueeze(1).broadcast_to([P, NH1, P])
                    v.tensor_tensor(MM[w][:, b * NH1:(b + 1) * NH1, :], DM[:, b * NH1:(b + 1) * NH1, :], gg, ALU.mult)
                v.wait_ge(el_done, c + 1)
                for b in range(B):
                    cc = HH[w][0:DS, 256 + b * P:256 + (b + 1) * P].unsqueeze(1).broadcast_to([DS, NH1, P])
                    ins = v.tensor_tensor(CTD[w][b], E2[w][:, b, :, :], cc, ALU.mult)
                ins.then_inc(ops_ready, 1)

            def chunk_state(c, w):
                link(v.tensor_tensor(hf(hst2[:, :, :, :]), hf(HS[:, :, :, :]), hf(E2[w])[:, :, P - 1:P].broadcast_to([DS, B * NH1, HP]), ALU.mult))
                v.wait_ge(c_done, c + 1)
                v.tensor_tensor(hf(HS[:, :, :, :]), hf(hst2[:, :, :, :]), PS[0:DS, 4, :].rearrange("p (i n) -> p i n", n=HP), ALU.add).then_inc(hs_done, 1)
                for b in range(B):
                    ins = v.tensor_reduce(MXV[:, b, bass.ds(c, 1), :], PS[:, 5 + b, :].rearrange("p (i n) -> p i n", n=HP).unsqueeze(1), X_AX, ALU.max)
                ins.then_inc(bnd_read, 1)
                v.wait_ge(hs_done, c + 1)

            def two_chunks(k, last=False):
                chunk_operands(2 * k + 1, 1, k, last)
                chunk_state(2 * k, 0)
                if not last:
                    chunk_operands(2 * k + 2, 0, k + 1)
                chunk_state(2 * k + 1, 1)
            spread_decays(0)
            chunk_operands(0, 0, 0)
            repeat(v, TCH // 2 - 1, two_chunks, ch)
            two_chunks(TCH // 2 - 1, True)
            v.wait_ge(bnd_read, TCH)

            mxk = MXV.rearrange("p b c (h k) -> p (b c) h k", k=2)
            mp_ = nmx2[:, :, :]
            link(v.tensor_tensor(mp_, mxk[:, :, :, 0], mxk[:, :, :, 1], ALU.mult))
            link(v.tensor_reduce(okv[:, :], mp_.rearrange("p t h -> p (t h)"), X_AX, ALU.max))
            v.tensor_scalar(okv[:, :], okv[:, :], BOUND, None, ALU.is_lt).then_inc(ok_ready, 1)
            v.wait_ge(cnt1_ready, 1)
            v.tensor_scalar(flag[:, :], PS[0:1, 3, 0:1], P - 0.5, None, ALU.is_lt).then_inc(flag_set, 1)
            v.wait_ge(flag_set, 1)
            with v.If(v.value_load(flag[:, :], min_val=0, max_val=1) > 0):
                cchain = Chain(v, clip_chain)
                cchain.link(v.memset(g_h, 0.0))

                def clip_steps(k):
                    v.wait_ge(g_ld, 8 * 16 * (k + 1))
                    v.wait_ge(g_dec_done, k + 1)
                    after(v, g_mm, 2 * k)
                    for t in range(GT):
                        cchain.link(v.tensor_tensor(g_h, g_h, g_dec[:, t, :].unsqueeze(2).broadcast_to([P, NH1, HP]), ALU.mult))
                        hflat = g_h.rearrange("p h q -> p (h q)")
                        cchain.link(v.scalar_tensor_tensor(hflat, g_x[:, t, :], g_b[:, t:t + 1], hflat, ALU.mult, ALU.add))
                        cchain.link(v.tensor_scalar(hflat, hflat, HMAX, -HMAX, ALU.min, ALU.max))
                        ins = v.tensor_scalar(g_hc[:, t, :], hflat, g_c[:, t:t + 1], None, ALU.mult)
                        if t == GT - 1:
                            ins.then_inc(g_hc_done, 1)
                            v.wait_ge(g_hc_done, k + 1)
                        else:
                            cchain.link(ins)
                repeat(v, S // GT, clip_steps, cchain)
                v.wait_ge(g_st, 16 * B * S // GT + 16)

            v.wait_ge(l1_ready, 1)
            q0, q1, q2, q3 = (lg1[:, i, :, :] for i in range(4))
            r_, n_ = s1_[:, 0, :], s1_[:, 1, :]
            b_ = lambda t: t.unsqueeze(2).broadcast_to([1, B, E1])
            link(v.tensor_copy(q0, PS[0:1, 2, 0:B * E1].rearrange("p (b e) -> p b e", b=B)))
            link(v.tensor_reduce(r_, q0, X_AX, ALU.max))
            v.tensor_tensor(q0, q0, b_(r_), ALU.subtract).then_inc(exp_in, 1)
            v.wait_ge(exp_out, 3)
            link(v.tensor_reduce(r_, q1, X_AX, ALU.add))
            link(v.reciprocal(r_, r_))
            link(v.tensor_tensor(q1, q1, b_(r_), ALU.mult))
            link(v.tensor_reduce(r_, q1, X_AX, ALU.max))
            link(v.tensor_tensor(q2, q1, b_(r_), ALU.is_equal))
            ex = io1[:, :].unsqueeze(1).broadcast_to([1, B, E1])
            link(v.tensor_tensor(q2, q2, ex, ALU.mult))
            link(v.tensor_reduce(n_, q2, X_AX, ALU.min))
            v.tensor_tensor(q3, ex, b_(n_), ALU.is_equal).then_inc(oh_ready, 1)
            v.wait_ge(ohb_ready, 1)
            link(v.tensor_copy(oh[:, :], PS[:, 2, 0:B * E1]))
            v.wait_ge(fw_ld, 32)
            for b in range(B):
                link(v.tensor_scalar(SW1[b][:, :], FW1[0], oh[:, b * E1:b * E1 + 1], None, ALU.mult))
                for e in range(1, E1):
                    link(v.scalar_tensor_tensor(SW1[b][:, :], FW1[e], oh[:, b * E1 + e:b * E1 + e + 1], SW1[b][:, :], ALU.mult, ALU.add))
            v.tensor_copy(oh[:, :], oh[:, :]).then_inc(sel1_done, 1)

            chan = lambda i: sc_aff[:, i, :].unsqueeze(1).broadcast_to([P, 2, DI])
            g2 = lambda t: t.rearrange("p (t c) -> p t c", t=2)
            y2, yl, o, on = wb[0], wb[1], wa[5][:, 0:2, :], wa[5][:, 2:4, :]

            def gated(k):
                v.wait_ge(z_ld, 32 * (k + 1))
                link(v.tensor_tensor(y2, g2(SG[0]), chan(0), ALU.mult))
                link(v.tensor_tensor(y2, y2, YS[:, bass.ds(2 * k, 2), :], ALU.add))
                link(v.tensor_tensor(y2, y2, g2(SG[1]), ALU.mult))
                statistics(v, ch, lambda t: y2[:, t, :], bns, mv[0], 2, var_ready, passed)

            def gated_norm(k, count):
                link(standardise(v, ch, lambda t: yl[:, t, :], lambda t: y2[:, t, :], mv[0], 2, std_ready, count))
                link(v.tensor_tensor(yl, yl, chan(1), ALU.mult))
                v.tensor_tensor(yl, yl, chan(2), ALU.add).then_inc(yl_ready, 1)

            def projected(k):
                v.wait_ge(pr_ready, k + 1)
                link(v.tensor_scalar(o, PS[:, 1, 0:2 * D].rearrange("p (t d) -> p t d", t=2), HMAX, -HMAX, ALU.min, ALU.max))
                statistics(v, ch, lambda t: o[:, t, :], bns, mv[1], 2, var_ready, passed)

            def projected_norm(k, count):
                link(standardise(v, ch, lambda t: on[:, t, :], lambda t: o[:, t, :], mv[1], 2, std_ready, count))
                link(v.tensor_tensor(on, on, affine[:, 6, :].unsqueeze(1).broadcast_to([P, 2, D]), ALU.mult))
                v.tensor_tensor(S2[:, bass.ds(2 * k, 2), :], on, affine[:, 7, :].unsqueeze(1).broadcast_to([P, 2, D]), ALU.add).then_inc(s2_done, 1)

            def gate(k, last=False):
                if not last:
                    gated(k + 1)
                projected(k)
                if not last:
                    gated_norm(k + 1, LN9 + 2 * k + 2)
                projected_norm(k, LN9 + 2 * k + 3 - last)

            def gate_in(j):
                v.wait_ge(fo_ready, j + 1)
                v.scalar_tensor_tensor(f_(wa[0]), PS[:, 5, :], 0.3, XN2[:, bass.ds(TB * j, TB), :].rearrange("p t d -> p (t d)"), ALU.mult, ALU.add).then_inc(gin_ready, 1)

            def finish(j):
                v.wait_ge(g_ready, j + 1)
                link(v.tensor_tensor(wa[1][:, :, :], wa[1][:, :, :], S2[:, bass.ds(TB * j, TB), :], ALU.mult))
                xb = X[:, bass.ds(TB * j, TB), :]
                v.tensor_tensor(xb, xb, wa[1][:, :, :], ALU.add).then_inc(fin_ready, 1)

            def block2(m, last=False):
                gate(2 * m)
                if last or not isinstance(m, int):
                    gate_in(m - 1)
                gate(2 * m + 1, last)
                if last or not isinstance(m, int):
                    finish(m - 1)
            gated(0)
            gated_norm(0, LN9 + 1)
            links = ch.n
            block2(0)
            loop_only(v, 1, NB - 1, block2, ch, ch.n - links + 1)
            block2(NB - 1, True)
            gate_in(NB - 1)
            v.wait_ge(s2_done, NT // 2)
            finish(NB - 1)
            v.wait_ge(fin_ready, NB)

        @block.scalar
        def _(act):
            act.wait_ge(c_ld, 16 * NCONST)

            def root_x(j, w):
                act.wait_ge(var_ready, j + 1)
                act.activation(mv[w][:, :, 1:2], mv[w][:, :, 1:2], ACT.Sqrt).then_inc(std_ready, 1)

            def ln_x(k, last=False):
                for w in range(2):
                    j = 2 * k + w
                    if not (last and w == 1):
                        root_x(j + 1, 1 - w)
                    act.wait_ge(xnT_ready, j + 1)
                    act.activation(XNT[:, bass.ds(j * 512, 512)], PS[:, 0, :], ACT.Copy).then_inc(xnT_out, 1)
            root_x(0, 0)
            repeat(act, NB // 2 - 1, ln_x)
            ln_x(NB // 2 - 1, True)

            act.wait_ge(lg_ready, 1)
            act.activation(gt[0].rearrange("p t e -> p (t e)"), PS[:, 0:2, :].rearrange("p a c -> p (a c)"), ACT.Copy).then_inc(lg_out, 1)
            act.wait_ge(exp_in, 1)
            act.activation(gt[1][:, :, :], gt[0][:, :, :], ACT.Exp).then_inc(exp_out, 1)

            def levels(j):
                for w in range(2):
                    act.wait_ge(h_state, 2 * j + w + 1)
                    act.activation(hst[1 - w].rearrange("p b d -> p (b d)"), PS[0:2, 4, 0:P], ACT.Copy).then_inc(h_carried, 1)
                    act.wait_ge(h_level, 2 * j + w + 1)
                    after(act, h_st[w], 16 * j)
                    act.activation(hout[w].rearrange("p b s -> p (b s)"), PS[0:DH, 5 + w, 0:B * P], ACT.Copy).then_inc(h_out, 1)
            repeat(act, TCH // 2, levels)

            def qkv_out(k):
                for w in range(2):
                    j = 2 * k + w
                    act.wait_ge(qk_ready, j + 1)
                    after(act, qs_ready, j - 1)
                    act.activation(f_(QF[w]), PS[:, 4, :], ACT.Identity, bias=bcol[:, 0:1]).then_inc(q_out, 1)
                    after(act, ks_ready, j - 1)
                    act.activation(f_(KF[w]), PS[:, 5, :], ACT.Identity, bias=bcol[:, 1:2]).then_inc(k_out, 1)
                    act.wait_ge(v_ready, j + 1)
                    act.activation(VP[:, bass.ds(j * TB, TB), :], PS[:, 6, :].rearrange("p (t c) -> p t c", c=P), ACT.Copy).then_inc(v_out, 1)
            repeat(act, NB // 2, qkv_out)

            def evac(u, trip_halves, half):
                act.wait_ge(pv_done, TCH * u + TCH // 2 * (half + 1))
                after(act, oe_st[half], 64 * u)
                act.activation(OE[half][:, :], PS[:, 4, :], ACT.Copy).then_inc(o_evac, 1)

            def unit_exp(u):
                for i in range(STEPS):
                    T = STEPS * u + i
                    act.wait_ge(sc_ready, T + 1)
                    if i % 2 == 0:
                        after(act, pv_done, TCH * u + i // 2 - 1)
                    act.activation(PR[i % 4][:, :], PS[:, 2 * (i % 2):2 * (i % 2) + 2, :].rearrange("p a c -> p (a c)"), ACT.Exp,
                                   scale=float(1.0 / np.sqrt(np.float32(DK)))).then_inc(exp_done, 1)
                    if i == TCH + 1:
                        evac(u, 0, 0)
                evac(u, 0, 1)

            def group_exp(k):
                for w in range(4):
                    unit_exp(4 * k + w)
            repeat(act, GROUPS, group_exp)

            def turned(e, w):
                act.wait_ge(xt_ready, e + 1)
                after(act, mh_ready, e - 1)
                act.activation(xeT[w % 2], PS[:, 0:2, :].rearrange("p a c -> p (a c)")[:, 0:CAP], ACT.Copy).then_inc(xt_out, 1)

            def experts(k, last=False):
                for w in range(4):
                    e = 4 * k + w
                    if not (last and w == 3):
                        turned(e + 1, w + 1)
                    act.wait_ge(mh_ready, e + 1)
                    after(act, hh_done, e - 1)
                    act.activation(sge[w % 2].rearrange("p (h c) -> p h c", h=2), PS[:, 2:4, 0:CAP // 2], ACT.Silu).then_inc(sg_done, 1)
            turned(0, 0)
            repeat(act, E // 4 - 1, experts)
            experts(E // 4 - 1, True)

            def root(count, groups):
                act.wait_ge(var_ready, count)
                act.activation(st[:, 2, 0:groups], st[:, 1, 0:groups], ACT.Sqrt).then_inc(std_ready, 1)

            def finish_attn(k, last=False):
                for w in range(2):
                    j, end = 2 * k + w, last and w == 1
                    act.wait_ge(yT_ready, j + 1)
                    act.activation(f_(wa[3]), PS[:, 1, :], ACT.Copy).then_inc(yT_out, 1)
                    for f in range(DFF // P):
                        act.wait_ge(f_ready, 4 * j + f + 1)
                        act.activation(FH[f][:, 0:512], PS[:, 2 + f, :], ACT.Relu, bias=bcol[:, 2 + f:3 + f]).then_inc(f_out, 1)
                    if not end:
                        root(LN4 + 2 * j + 2, 2 * TB)
                    root(LN4 + 2 * j + 3 - end, TB)
            root(LN4 + 1, 2 * TB)
            repeat(act, NB // 2 - 1, finish_attn)
            finish_attn(NB // 2 - 1, True)

            for half in range(2):
                act.wait_ge(oe_st[half], 64 * UNITS)

            def shared(k):
                for w in range(2):
                    act.wait_ge(mh_ready, E + 2 * k + w + 1)
                    act.wait_ge(hh_done, E + 2 * k + w - 1)
                    act.activation(SG[w][:, :], PS[:, w, :], ACT.Silu).then_inc(sg_done, 1)
            repeat(act, NB // 2, shared)
            act.wait_ge(ym_done, NB)
            act.activation(YM[:, :, :], YM[:, :, :], ACT.Silu).then_inc(g_done, 1)

            act.wait_ge(w1_ld, 16 * NCONST1)

            def root7(i, count):
                act.wait_ge(var_ready, count)
                act.activation(mv[i][:, :, 1:2], mv[i][:, :, 1:2], ACT.Sqrt).then_inc(std_ready, 1)

            def proj(j, last=False):
                act.wait_ge(xn_ready, NB + j + 1)
                act.activation(XN2[:, bass.ds(j * TB, TB), :], wa[1][:, :, :], ACT.Copy)
                act.wait_ge(xnT_ready, NB + j + 1)
                act.activation(XNT[:, bass.ds(j * 512, 512)], PS[:, 0, :], ACT.Copy).then_inc(xnT_out, 1)
                if not last:
                    root7(0, LN7 + 2 * j + 3)
                act.wait_ge(xnnT_ready, j + 1)
                act.activation(f_(wa[3]), PS[:, 1, :], ACT.Copy).then_inc(xnnT_out, 1)
                act.wait_ge(bct_ready, j + 1)
                after(act, bct_st, 32 * j)
                act.activation(HH[0][0:DS, :], PS[0:DS, 4, :], ACT.Copy).then_inc(bct_out, 1)
                act.activation(HH[1][0:DS, :], PS[0:DS, 5, :], ACT.Copy).then_inc(bct_out, 1)
                if not last:
                    root7(1, LN7 + 2 * j + 4)
                for t in range(TB):
                    act.wait_ge(zx_ready, TB * j + t + 1)
                    after(act, zx_st[t % 2], 32 * (2 * j + t // 2))
                    act.activation(SG[t % 2][:, 0:DI], PS[:, 2 + t % 2, 0:DI], ACT.Silu).then_inc(zx_out, 1)
                    act.activation(SG[t % 2][:, DI:2 * DI], PS[:, 2 + t % 2, DI:2 * DI], ACT.Copy).then_inc(zx_out, 1)
            root7(0, LN7 + 1)
            root7(1, LN7 + 2)
            repeat(act, NB - 1, proj)
            proj(NB - 1, True)
            act.wait_ge(exp_in, 2)
            act.activation(alog[:, 2, :], alog[:, 0, :], ACT.Exp)
            act.activation(dtt[:, 1, :, :], dtt[:, 0, :, :], ACT.Exp).then_inc(act_chain, 1)
            act.wait_ge(act_chain, 1)
            act.activation(dtt[:, 1, :, :], dtt[:, 1, :, :], ACT.Ln, bias=1.0).then_inc(exp_out, 1)

            def chunk_exps(c, w):
                act.wait_ge(dif_done, c + 1)
                act.activation(DE, DE, ACT.Exp).then_inc(d_done, 1)
                after(act, hs_done, c - 1)
                sums = PS[0:DS, 0:2, :].rearrange("p b c -> p (b c)")
                act.activation(E2[w].rearrange("p b h t -> p (b h t)"), sums, ACT.Exp).then_inc(el_done, 1)
                act.activation(E2b[w].rearrange("p b h t -> p (b h t)"), sums, ACT.Exp)
                act.wait_ge(dm_done, c + 1)
                act.activation(DMb[w], DM, ACT.Copy).then_inc(opb_ready, 1)

            def chunk_out(c):
                act.wait_ge(c_done, c + 1)
                for b in range(B):
                    act.activation(VR[32 * b:32 * b + 1, :, :], VS[32 * b:32 * b + 1, :, :], ACT.Copy).then_inc(vr_out, 1)
                act.activation(YS.rearrange("p (b c) n -> p b c n", b=B)[:, :, bass.ds(c, 1), :],
                               PS[:, 3, :].rearrange("p (b n) -> p b n", b=B).unsqueeze(2), ACT.Copy).then_inc(y_out, 1)

            def two_chunks(k, last=False):
                chunk_exps(2 * k + 1, 1)
                chunk_out(2 * k)
                if not last:
                    chunk_exps(2 * k + 2, 0)
                chunk_out(2 * k + 1)
            chunk_exps(0, 0)
            repeat(act, TCH // 2 - 1, two_chunks)
            two_chunks(TCH // 2 - 1, True)
            act.wait_ge(flag_set, 1)
            with act.If(act.value_load(flag[:, :], min_val=0, max_val=1) > 0):
                def clip_out(k):
                    act.wait_ge(g_ld, 8 * 16 * (k + 1))
                    act.activation(HH[1][:, 0:GT * NH1], HH[1][:, 0:GT * NH1], ACT.Exp).then_inc(g_dec_done, 1)
                    for i in range(2):
                        act.wait_ge(g_mm, 2 * k + i + 1)
                        if i == 0:
                            after(act, g_st, 16 * B * k)
                        act.activation(g_y[:, i * 2048:(i + 1) * 2048], PS[0:B, 0:4, :].rearrange("p a c -> p (a c)"), ACT.Copy).then_inc(g_y_out, 1)
                repeat(act, S // GT, clip_out)

            def gate_root(i, count):
                act.wait_ge(var_ready, count)
                act.activation(mv[i][:, 0:2, 1:2], mv[i][:, 0:2, 1:2], ACT.Sqrt).then_inc(std_ready, 1)

            def turned_out(k):
                act.wait_ge(yT_ready, NB + k + 1)
                act.activation(ylT[:, :], PS[:, 0, :], ACT.Copy).then_inc(yT_out, 1)

            def gate_roots(k, last=False):
                if not last:
                    gate_root(0, LN9 + 2 * k + 2)
                gate_root(1, LN9 + 2 * k + 3 - last)

            def silu(j):
                act.wait_ge(gin_ready, j + 1)
                after(act, fin_ready, j)
                act.activation(f_(wa[1]), f_(wa[0]), ACT.Silu).then_inc(g_ready, 1)

            def block2(m, b, last=False):
                gate_roots(2 * m)
                turned_out(2 * m + 1)
                for f in range(2):
                    act.wait_ge(fh_ready, 2 * m + f + 1)
                    act.activation(HH[f][:, :], PS[:, 2 + f, :], ACT.Gelu, bias=SW1[b][:, 2 * F1 + f:2 * F1 + f + 1]).then_inc(fh_out, 1)
                if last or not isinstance(m, int):
                    silu(m - 1)
                gate_roots(2 * m + 1, last)
                act.wait_ge(rt_ready, m + 1)
                act.activation(f_(wa[2]), PS[:, 4, :], ACT.Identity, bias=SW1[b][:, 2 * F1 + 2:2 * F1 + 3]).then_inc(rt_out, 1)
                if not last:
                    turned_out(2 * m + 2)

            act.wait_ge(a1_ready, 1)
            act.activation(hn[:, :], PS[:, 2, 0:B], ACT.Gelu, bias=wp[:, P:P + 1]).then_inc(a1_out, 1)
            act.wait_ge(exp_in, 3)
            act.activation(lg1[:, 1, :, :], lg1[:, 0, :, :], ACT.Exp).then_inc(exp_out, 1)
            act.wait_ge(sel1_done, 1)
            gate_root(0, LN9 + 1)
            turned_out(0)
            block2(0, 0)
            loop_only(act, 1, NB // B, lambda m: block2(m, 0))
            loop_only(act, NB // B, NB - 1, lambda m: block2(m, 1))
            block2(NB - 1, 1, True)
            silu(NB - 1)

        @block.gpsimd
        def _(pool):
            for i in range(4):
                pool.memset(VH[i][:, :, :], 1.0).then_inc(vh_set, 1)
            pool.wait_ge(ql_st, 48 * NB)
            pool.wait_ge(kl_st, 48 * NB)
            pool.wait_ge(vh_set, 4)
            for i in range(4):
                pool.memset(QS[i][64:96, :], 1.0).then_inc(ones_set, 1)
                pool.memset(KS[i][64:96, :], 1.0).then_inc(ones_set, 1)
            pool.wait_ge(ones_set, 8)
            pool.memset(zt[:, :], 0.0).then_inc(ones_set, 1)
            pool.wait_ge(ones_set, 9)
            pool.wait_ge(v_out, NB)

            def stage_rows(t, i, count, src, dst):
                pool.tensor_copy(rows_s[i][:, :].unsqueeze(1), ROWI[:, bass.ds(t, 1), :]).then_inc(staged, 1)
                pool.tensor_copy(dst, src).then_inc(staged, 1)
                pool.wait_ge(staged, count)
                pool.sem_inc(passed, 1)

            def prepare(k, scatter=False):
                for w in range(4):
                    u, g = 4 * k + w, 2 * k + w // 2
                    after(pool, pv_done, TCH * (u - 3))
                    pool.tensor_copy(VH[w][:, :, 0:DK], VP[:, (w % 2) * TCH:(w % 2 + 1) * TCH, bass.ds(g * DK, DK)]).then_inc(vh_ready, 1)
                    if scatter:
                        uses = 4 * (k - GROUPS // 2) + w
                        for i in range(2):
                            t = 2 * uses + i
                            after(pool, sc_st[i], 64 * uses)
                            stage_rows(t, i, 2 * t + 2, S0[:, bass.ds(t, 1), :], xn_s[i][:, :].unsqueeze(1))
                            for n in range(KTOP):
                                pool.indirect_dma_start(xe_d, bass.IndirectOffsetOnAxis(rows_s[i][:, n:n + 1], 0), xn_s[i][:, :], None,
                                                        bounds_check=E * CAP - 1, oob_is_err=False).then_inc(sc_st[i], 16)
            repeat(pool, GROUPS // 2, prepare)
            pool.wait_ge(rows_done, 1)
            pool.wait_ge(s0_ld, 16)
            pool.wait_ge(zero_st, 16 * (UNITS // 2 + 1))
            repeat(pool, GROUPS // 2, lambda k: prepare(k, True), start=GROUPS // 2)

            for i in range(2):
                pool.wait_ge(sc_st[i], 64 * NT // 2)
                pool.wait_ge(oes_st[i], 16 * E // 2)
            pool_links = Chain(pool, pool_chain)

            def gather(k):
                for i in range(2):
                    t = 2 * k + i
                    stage_rows(t, i, 2 * NT + 2 * t + 2, WK[:, bass.ds(t, 1), :], wk_s[i][:, :].unsqueeze(1))
                    for n in range(KTOP):
                        pool.indirect_dma_start(GB[i][:, n, :], None, oe_d, bass.IndirectOffsetOnAxis(rows_s[i][:, n:n + 1], 0),
                                                bounds_check=E * CAP, oob_is_err=False).then_inc(ga_ld[i], 16)
                for i in range(2):
                    pool.wait_ge(ga_ld[i], 64 * (k + 1))
                    pool_links.link(pool.tensor_tensor(GB[i], GB[i], wk_s[i][:, :].unsqueeze(2).broadcast_to([P, KTOP, D]), ALU.mult))
                    pool_links.link(pool.tensor_tensor(GB[i][:, 0:2, :], GB[i][:, 0:2, :], GB[i][:, 2:4, :], ALU.add))
                    pool.tensor_tensor(YM[:, bass.ds(2 * k + i, 1), :], GB[i][:, 0:1, :], GB[i][:, 1:2, :], ALU.add).then_inc(y_sum, 1)
                pool.wait_ge(y_sum, 2 * k + 2)
            repeat(pool, NT // 2, gather, pool_links)

        @block.tensor
        def _(pe):
            pe.wait_ge(c_ld, 16 * NCONST)

            def turn(j):
                pe.wait_ge(xn_ready, j + 1)
                after(pe, xnT_out, j)
                for t in range(TB):
                    mm = pe.transpose(PS[:, 0, t * P:(t + 1) * P], wa[1][:, t, :], ident[:, :])
                mm.then_inc(xnT_ready, 1)
            repeat(pe, NB, turn)
            pe.wait_ge(xnT_out, NB)
            for t in range(NT):
                mm = pe.matmul(PS[:, t // 16, (t % 16) * E:(t % 16 + 1) * E], XNT[:, t * P:(t + 1) * P], wgT[:, :], start=True, stop=True)
            mm.then_inc(lg_ready, 1)

            def holt(j):
                for w in range(2):
                    t = 2 * j + w
                    pe.wait_ge(hx_ld[w], 16 * (j + 1))
                    if w or not isinstance(j, int):
                        pe.wait_ge(h_carried, t)
                    else:
                        pe.wait_ge(hst_ld, 16)
                    o = PS[0:2, 4, 0:P]
                    pe.matmul(o, cst[:, P:P + 2], hx[w].rearrange("p b d -> p (b d)"), start=True, stop=False)
                    pe.matmul(o, rows[0:2, P:P + 2], hst[w].rearrange("p b d -> p (b d)"), start=False, stop=True).then_inc(h_state, 1)
                    after(pe, h_out, t - 1)
                    for b in range(B):
                        o = PS[0:DH, 5 + w, b * P:(b + 1) * P]
                        pe.matmul(o, hx[w][:, b, :], cst[:, 0:P], start=True, stop=False)
                        mm = pe.matmul(o, hst[w][:, b, :], rows[0:2, 0:P], start=False, stop=True)
                    mm.then_inc(h_level, 1)
            repeat(pe, TCH // 2, holt)
            pe.wait_ge(sel_done, 1)
            pe.wait_ge(lg_out, 1)
            for h in range(2):
                sel = gt[5][:, h * 16:(h + 1) * 16, :].rearrange("p t e -> p (t e)")
                pe.matmul(PS[:, h, :], cst[:, P + 2:2 * P + 2], sel, start=True, stop=True)
                mm = pe.matmul(PS[:, 2 + h, :], onesq[:, :], sel, start=True, stop=True)
            mm.then_inc(lg_ready, 1)
            pe.wait_ge(h_out, TCH)

            def qkv(k):
                for w in range(2):
                    j = 2 * k + w
                    pe.wait_ge(xc_ld[w], 16 * (k + 1))
                    after(pe, k_out, j)
                    pe.matmul(PS[:, 4, :], wsq[:, 0, :], f_(XC[w]), start=True, stop=True)
                    pe.matmul(PS[:, 5, :], wsq[:, 1, :], f_(XC[w]), start=True, stop=True).then_inc(qk_ready, 1)
                    after(pe, v_out, j)
                    for t in range(TB):
                        o = PS[:, 6, t * P:(t + 1) * P]
                        pe.matmul(o, XC[w][:, t, :], wsq[:, 2, :], start=True, stop=False)
                        mm = pe.matmul(o, ones1[:, :], brow[:, 0:P], start=False, stop=True)
                    mm.then_inc(v_ready, 1)
            repeat(pe, NB // 2, qkv)

            def max_scores(uu, n, w):
                back = n - 2 if n > 2 else (0, -2, -1)[n]
                if not (isinstance(uu, int) and 4 * TCH * uu + back <= 0):
                    pe.wait_ge(mx_done, 4 * TCH * uu + back)
                if n == TURN_N + 2:
                    after(pe, mt_out, uu)
                pe.matmul(MXB[n % 3], QS[w][0:KROWS, (n // 4) * P:(n // 4 + 1) * P], KS[w][0:KROWS, (n % 4) * 512:(n % 4 + 1) * 512],
                          start=True, stop=True).then_inc(mxs_ready, 1)

            def turn_max(uu):
                pe.wait_ge(spl_ready, uu + 1)
                if not (isinstance(uu, int) and uu == UNITS - 1):
                    pe.wait_ge(mx_done, 4 * TCH * (uu + 1) + TURN_N)
                after(pe, mt_out, uu)
                pe.transpose(PT[:, 0:P], spl.rearrange("p l c -> p (l c)"), identb[:, :]).then_inc(mt_ready, 1)

            def weigh(u, pair, w):
                pe.wait_ge(exp_done, STEPS * u + 2 * pair + 2)
                if pair % (TCH // 2) == 0:
                    after(pe, o_evac, 2 * u + pair // (TCH // 2))
                for odd in range(2):
                    i = 2 * pair + odd
                    kt = i % TCH
                    for qb in range(2):
                        jg = 2 * odd + qb
                        mm = pe.matmul(PS[32 * jg:32 * jg + 32, 4, :], VH[w][:, kt, :], PR[i % 4][:, qb * 512:(qb + 1) * 512],
                                       start=(kt < 2), stop=(kt >= TCH - 2))
                mm.then_inc(pv_done, 1)

            def unit(u, w, trip, last, final):
                nw = (w + 2) % 4
                pe.wait_ge(m_ld[w], 16 * (trip + 1))
                if not last:
                    pe.wait_ge(qk_ld[nw], 96 * (trip + 1 + (w >= 2)))
                n = 0
                for i in range(STEPS):
                    kt, qh = i % TCH, i // TCH
                    after(pe, exp_done, STEPS * u + i - 1)
                    for qb in range(2):
                        q0 = qh * 1024 + qb * 512
                        mm = pe.matmul(PS[:, 2 * (i % 2) + qb, :], KS[w][0:KROWS + 3, kt * P:(kt + 1) * P], QS[w][0:KROWS + 3, q0:q0 + 512],
                                       start=True, stop=True)
                    mm.then_inc(sc_ready, 1)
                    if not last:
                        max_scores(u + 2, n, nw)
                        n += 1
                    if i == 1:
                        pe.wait_ge(vh_ready, u + 1)
                    if i % 2 and i >= 3:
                        weigh(u, (i - 3) // 2, w)
                    if i % 2 and not last:
                        for _ in range(2):
                            max_scores(u + 2, n, nw)
                            n += 1
                    if i == TURN and not final:
                        turn_max(u + 1)
                weigh(u, TCH - 1, w)

            pe.wait_ge(v_out, NB)
            pe.wait_ge(rows_done, 1)
            for u in range(2):
                pe.wait_ge(qk_ld[u], 96)
                for n in range(4 * TCH):
                    max_scores(u, n, u)
                    if u == 1 and n == TURNED - 1:
                        turn_max(0)

            def group(k, last=False):
                for w in range(4):
                    unit(4 * k + w, w, k, last and w >= 2, last and w == 3)
            repeat(pe, GROUPS - 1, group)
            group(GROUPS - 1, True)

            pe.wait_ge(o_evac, 2 * UNITS)
            pe.wait_ge(exp_done, STEPS * UNITS)
            pe.wait_ge(mx_done, 4 * TCH * UNITS)
            pe.wait_ge(mt_out, UNITS)

            def turn_tokens(e, w, trip):
                pe.wait_ge(ew_ld[w], 32 * (trip + 1))
                after(pe, xt_out, e)
                for t in range(CAP // P):
                    mm = pe.transpose(PS[:, t // TB, (t % TB) * P:(t % TB + 1) * P], xe_in[w][:, t, :], ident[:, :])
                mm.then_inc(xt_ready, 1)

            def expert_out(e, w):
                pe.wait_ge(hh_done, e + 1)
                after(pe, oe_out, e)
                for t in range(CAP // P):
                    o = PS[:, 6, t * P:(t + 1) * P] if t < TB else PTF[:, 0:P]
                    mm = pe.matmul(o, hhe[w % 2][:, t * P:(t + 1) * P], EW[w][:, 2, :], start=True, stop=True)
                mm.then_inc(mo_ready, 1)

            def experts(k, last=False):
                for w in range(4):
                    e = 4 * k + w
                    if not (last and w == 3):
                        turn_tokens(e + 1, (w + 1) % 4, k + (w == 3))
                    pe.wait_ge(xt_out, e + 1)
                    after(pe, hh_done, e)
                    for m in range(2):
                        for h in range(2):
                            mm = pe.matmul(PS[:, 2 + 2 * m + h, 0:CAP // 2], EW[w][:, m, :], xeT[w % 2][:, h * CAP // 2:(h + 1) * CAP // 2], start=True, stop=True)
                    mm.then_inc(mh_ready, 1)
                    if w or last or not isinstance(k, int):
                        expert_out(e - 1, (w + 3) % 4)
            turn_tokens(0, 0, 0)
            repeat(pe, E // 4 - 1, experts)
            experts(E // 4 - 1, True)
            expert_out(E - 1, 3)

            pe.wait_ge(hh_done, E)

            def residual(w, trip, count):
                pe.wait_ge(at_sum, count)
                f = [AT[w][n].rearrange("p (t c) -> p t c", c=P) for n in (0, 4)]
                for t in range(TB):
                    o = RES[w][:, t * P:(t + 1) * P]
                    pe.matmul(o, f[0][:, t, :], wsq[:, 3, :], start=True, stop=False)
                    pe.matmul(o, f[1][:, t, :], ident[:, :], start=False, stop=False)
                    mm = pe.matmul(o, ones1[:, :], brow[:, P:2 * P], start=False, stop=True)
                mm.then_inc(r_ready, 1)

            def finish_attn(k, last=False):
                for w in range(2):
                    j = 2 * k + w
                    pe.wait_ge(y_ready, j + 1)
                    for t in range(TB):
                        mm = pe.transpose(PS[:, 1, t * P:(t + 1) * P], wa[2][:, t, :], ident[:, :])
                    mm.then_inc(yT_ready, 1)
                    pe.wait_ge(yT_out, j + 1)
                    for f in range(DFF // P):
                        pe.matmul(PS[:, 2 + f, :], wff1[:, f * P:(f + 1) * P], f_(wa[3]), start=True, stop=True).then_inc(f_ready, 1)
                    if not last:
                        residual(w, k + 1, j + 3)
                    pe.wait_ge(f_out, 4 * (j + 1))
                    after(pe, at_free, j)
                    for t in range(TB):
                        o = PTF[:, t * P:(t + 1) * P]
                        for f in range(DFF // P):
                            pe.matmul(o, FH[f][:, t * P:(t + 1) * P], wff2[:, f, :], start=(f == 0), stop=False)
                        pe.matmul(o, wa[3][:, t, :], ident[:, :], start=False, stop=False)
                        mm = pe.matmul(o, ones1[:, :], brow[:, 2 * P:3 * P], start=False, stop=True)
                    mm.then_inc(ff_ready, 1)
            pe.wait_ge(oe_out, E)
            residual(0, 0, 1)
            residual(1, 0, 2)
            repeat(pe, NB // 2 - 1, finish_attn)
            finish_attn(NB // 2 - 1, True)

            pe.wait_ge(at_free, NB)
            pe.wait_ge(ew_ld[0], 32 * (E // 4) + 16)

            def shared_project(j, w):
                pe.wait_ge(hh_done, E + j + 1)
                after(pe, ym_done, j - 1)
                for t in range(TB):
                    mm = pe.matmul(PS[:, 4 + w, t * P:(t + 1) * P], HH[w][:, t * P:(t + 1) * P], EW[0][:, 2, :], start=True, stop=True)
                mm.then_inc(mo_ready, 1)

            def shared(k):
                for w in range(2):
                    j = 2 * k + w
                    pe.wait_ge(hh_done, E + j - 1)
                    pe.matmul(PS[:, w, :], EW[0][:, 0, :], XNT[:, bass.ds(j * 512, 512)], start=True, stop=True)
                    pe.matmul(PS[:, 2 + w, :], EW[0][:, 1, :], XNT[:, bass.ds(j * 512, 512)], start=True, stop=True).then_inc(mh_ready, 1)
                    if not (w == 0 and isinstance(k, int)):
                        shared_project(j - 1, 1 - w)
            repeat(pe, NB // 2, shared)
            shared_project(NB - 1, 1)

            pe.wait_ge(w1_ld, 16 * NCONST1)
            pe.wait_ge(ym_done, NB)

            def proj(j):
                pe.wait_ge(xn_ready, NB + j + 1)
                after(pe, xnT_out, NB + j)
                for t in range(TB):
                    mm = pe.transpose(PS[:, 0, t * P:(t + 1) * P], wa[1][:, t, :], ident[:, :])
                mm.then_inc(xnT_ready, 1)
                pe.wait_ge(xnn_ready, j + 1)
                after(pe, xnnT_out, j)
                for t in range(TB):
                    mm = pe.transpose(PS[:, 1, t * P:(t + 1) * P], wa[4][:, t, :], ident[:, :])
                mm.then_inc(xnnT_ready, 1)
                pe.wait_ge(xnnT_out, j + 1)
                after(pe, bct_out, 2 * j)
                ob, oc = 2 * DI, 2 * DI + DS + NH1
                pe.matmul(PS[0:DS, 4, :], win[:, ob:ob + DS], f_(wa[3]), start=True, stop=True)
                pe.matmul(PS[0:DS, 5, :], win[:, oc:oc + DS], f_(wa[3]), start=True, stop=True).then_inc(bct_ready, 1)
                after(pe, bd_out, j)
                for t in range(TB):
                    mm = pe.matmul(PS[:, 6, t * (DS + NH1):(t + 1) * (DS + NH1)], wa[3][:, t, :], win[:, ob:oc], start=True, stop=True)
                mm.then_inc(bd_ready, 1)
                for t in range(TB):
                    after(pe, zx_out, 2 * (TB * j + t - 1))
                    pe.matmul(PS[:, 2 + t % 2, :], wa[3][:, t, :], win[:, 0:2 * DI], start=True, stop=True).then_inc(zx_ready, 1)
            repeat(pe, NB, proj)
            pe.wait_ge(zx_out, 2 * NT)
            pe.wait_ge(bd_out, NB)

            def chunk_sums(c, w, trip):
                pe.wait_ge(lb_set, c + 1)
                after(pe, ops_ready, c)
                after(pe, opb_ready, c)
                for b in range(B):
                    for h in range(NH1):
                        pe.matmul(PS[:, b, h * P:(h + 1) * P], lb[:, b * NH1 + h, :], TRI, start=True, stop=True)
                pe.matmul(PS[:, 2, 0:B * NH1], TRI, ldc.rearrange("p b h -> p (b h)"), start=True, stop=True)
                pe.wait_ge(c_ld8[w], 64 * (trip + 1))
                for b in range(B):
                    mm = pe.matmul(PS[:, 2, P + b * P:2 * P + b * P], HH[w][0:DS, b * P:(b + 1) * P], HH[w][0:DS, 256 + b * P:256 + (b + 1) * P],
                                   start=True, stop=True)
                mm.then_inc(la_ready, 1)

            def chunk_products(c, w):
                pe.wait_ge(ops_ready, c + 1)
                after(pe, hs_done, c)
                after(pe, y_out, c)
                for b in range(B):
                    for h in range(NH1):
                        i, n = b * NH1 + h, (b * NH1 + h) * HP
                        x = SG[w][:, n:n + HP]
                        pe.matmul(PS[:, 3, n:n + HP], MM[w][:, i, :], x, start=True, stop=False)
                        pe.matmul(PS[:, 3, n:n + HP], CTD[w][b][:, h, :], HS[:, b, h, :], start=False, stop=True)
                        pe.matmul(PS[0:DS, 4, n:n + HP], BD[w][:, b, h, :], x, start=True, stop=True)
                pe.wait_ge(opb_ready, c + 1)
                after(pe, vr_out, 2 * c)
                after(pe, bnd_read, c)
                for b in range(B):
                    r = slice(32 * b, 32 * b + 1)
                    for h in range(NH1):
                        o = PS[:, 5 + b, h * P:(h + 1) * P]
                        pe.matmul(o, DMb[w][:, b * NH1 + h, :], RB[w][:, b, h, :], start=True, stop=False)
                        pe.matmul(o, E2b[w][r, b, h, :], VR[r, h, :], start=False, stop=True)
                        o = VS[r, h, :]
                        pe.matmul(o, DMb[w][:, b * NH1 + h, P - 1:P], RB[w][:, b, h, :], start=True, stop=False)
                        mm = pe.matmul(o, E2b[w][r, b, h, P - 1:P], VR[r, h, :], start=False, stop=True)
                mm.then_inc(c_done, 1)

            def two_chunks(k, last=False):
                chunk_sums(2 * k + 1, 1, k)
                chunk_products(2 * k, 0)
                if not last:
                    chunk_sums(2 * k + 2, 0, k + 1)
                chunk_products(2 * k + 1, 1)
            chunk_sums(0, 0, 0)
            repeat(pe, TCH // 2 - 1, two_chunks)
            two_chunks(TCH // 2 - 1, True)
            pe.wait_ge(bnd_read, TCH)
            pe.wait_ge(y_out, TCH)
            pe.wait_ge(ok_ready, 1)
            pe.matmul(PS[0:1, 3, 0:1], okv[:, :], onesq[:, 0:1], start=True, stop=True).then_inc(cnt1_ready, 1)
            pe.wait_ge(flag_set, 1)
            with pe.If(pe.value_load(flag[:, :], min_val=0, max_val=1) > 0):
                def clip_mm(k):
                    pe.wait_ge(g_hc_done, k + 1)
                    for i in range(2):
                        after(pe, g_y_out, 2 * k + i)
                        for q in range(4):
                            t = 8 * i + 2 * q
                            mm = pe.matmul(PS[0:B, q, :], cst[:, 2 * P + 2:2 * P + 2 + B], g_hc[:, t:t + 2, :].rearrange("p t c -> p (t c)"), start=True, stop=True)
                        mm.then_inc(g_mm, 1)
                repeat(pe, S // GT, clip_mm)
                pe.wait_ge(g_y_out, 2 * S // GT)

            pe.wait_ge(xnT_out, 2 * NB)
            pe.matmul(PS[:, 2, 0:B], wp[:, 0:P], XNT.rearrange("p (b s) -> p b s", b=B)[:, :, S - 1], start=True, stop=True).then_inc(a1_ready, 1)
            pe.wait_ge(a1_out, 1)
            for b in range(B):
                o = PS[0:1, 2, b * E1:(b + 1) * E1]
                pe.matmul(o, hn[:, b:b + 1], wp[:, P + 1:P + 1 + E1], start=True, stop=False)
                mm = pe.matmul(o, ones1[:, 0:1], r1[:, 0:E1], start=False, stop=True)
            mm.then_inc(l1_ready, 1)
            pe.wait_ge(oh_ready, 1)
            pe.matmul(PS[:, 2, 0:B * E1], ones1[:, :], lg1[:, 3, :, :].rearrange("p b e -> p (b e)"), start=True, stop=True).then_inc(ohb_ready, 1)
            pe.wait_ge(sel1_done, 1)

            def gate(k):
                pe.wait_ge(yl_ready, k + 1)
                for i in range(4):
                    mm = pe.transpose(PS[:, 0, i * P:(i + 1) * P], wb[1].rearrange("p t (f c) -> p (t f) c", f=2)[:, i, :], ident[:, :])
                mm.then_inc(yT_ready, 1)
                pe.wait_ge(yT_out, NB + k + 1)
                after(pe, var_ready, LN9 + 2 * k + 1 if not isinstance(k, int) or k else 0)
                for t in range(2):
                    for f in range(2):
                        mm = pe.matmul(PS[:, 1, t * D:(t + 1) * D], ylT[:, (2 * t + f) * P:(2 * t + f + 1) * P], wout[:, f, :], start=(f == 0), stop=(f == 1))
                mm.then_inc(pr_ready, 1)

            def block2(m, b):
                gate(2 * m)
                xb = XNT[:, bass.ds(m * 512, 512)]
                for f in range(2):
                    pe.matmul(PS[:, 2 + f, :], SW1[b][:, f * P:(f + 1) * P], xb, start=True, stop=True).then_inc(fh_ready, 1)
                gate(2 * m + 1)
                pe.wait_ge(fh_out, 2 * m + 2)
                for f in range(2):
                    mm = pe.matmul(PS[:, 4, :], SW1[b][:, F1 + f * P:F1 + (f + 1) * P], HH[f][:, :], start=(f == 0), stop=(f == 1))
                mm.then_inc(rt_ready, 1)
                pe.wait_ge(rt_out, m + 1)
                after(pe, gin_ready, m)
                for t in range(TB):
                    o = PS[:, 5, t * P:(t + 1) * P]
                    pe.matmul(o, wa[2][:, t, :], wo1[:, :], start=True, stop=False)
                    mm = pe.matmul(o, ones1[:, :], r1[:, E1:E1 + D], start=False, stop=True)
                mm.then_inc(fo_ready, 1)
            block2(0, 0)
            loop_only(pe, 1, NB // B, lambda m: block2(m, 0))
            loop_only(pe, NB // B, NB, lambda m: block2(m, 1))


def holt_constants():
    al, be = np.float64(ALPHA), np.float64(BETA)
    F = np.array([[1 - al, 1 - al], [be * (1 - al) - be, be * (1 - al) + 1 - be]])
    g = np.array([al, be * al])
    pw = [np.eye(2)]
    for _ in range(P):
        pw.append(F @ pw[-1])
    level = np.zeros((P, P))
    for t in range(P):
        for s in range(t + 1):
            level[s, t] = (pw[t - s] @ g)[0]
    end = np.stack([pw[P - 1 - s] @ g for s in range(P)])
    state = np.stack([pw[t + 1][0] for t in range(P)], axis=1)
    return level, end, state, pw[P].T


_OUTS = [((2, 2048, 128), 'float32')]


def layout(x):
    f = np.float32
    g = lambda n: np.asarray(x[n])

    def pair(name, transpose=True):
        m = np.zeros((P, P), f)
        m[:DH, :DH] = g(f"L0_attn_{name}1").T
        m[DH:, DH:] = g(f"L0_attn_{name}2").T
        return m

    cat = lambda *n: np.concatenate([g("L0_attn_" + i) for i in n])
    level, end, state, full = holt_constants()
    wi = g("L1_attn_in_proj_w")
    tri = np.triu(np.ones((P, P)))
    rowc = np.zeros((P, P + 2), f)
    rowc[0:2, 0:P], rowc[0:2, P:P + 2] = state, full
    d = {
        "x": g("L0_attn_x"),
        "ident": np.eye(P, dtype=f),
        "consts": np.concatenate([level, end, tri, np.repeat(np.eye(B), DS, axis=0)], axis=1).astype(f),
        "rowc": rowc,
        "wsq": np.stack([pair("wq"), pair("wk"), pair("wv"), pair("wo")], axis=1),
        "wff1": g("L0_attn_w_ff1").T,
        "wff2": g("L0_attn_w_ff2").T.reshape(DFF // P, P, D).transpose(1, 0, 2),
        "bcol": np.stack([cat("bq1", "bq2"), cat("bk1", "bk2")] + list(g("L0_attn_b_ff1").reshape(DFF // P, P)), axis=1),
        "brow": np.concatenate([cat("bv1", "bv2"), cat("bo1", "bo2"), g("L0_attn_b_ff2")])[None],
        "affine": np.stack([cat("g1", "g2"), cat("be1", "be2"), g("L0_attn_g_ff"), g("L0_attn_be_ff"),
                            g("L1_attn_ni_w"), g("L1_attn_ni_b"), g("L1_attn_no_w"), g("L1_attn_no_b")]),
        "win": np.concatenate([wi[:2 * DI + DS], wi[2 * DI + 2 * DS:], wi[2 * DI + DS:2 * DI + 2 * DS]]).T,
        "wout": g("L1_attn_out_proj_w").T.reshape(2, P, D).transpose(1, 0, 2),
        "alog": np.stack([g("L1_attn_A_log"), g("L1_attn_dt_bias")]),
        "sc_aff": np.stack([np.repeat(g("L1_attn_Dparam"), HP), g("L1_attn_ln_w"), g("L1_attn_ln_b")]),
        "ew1": np.concatenate([g("L1_ffn_W1").transpose(1, 0, 2), g("L1_ffn_W2").reshape(E1, 2, P, D).transpose(2, 0, 1, 3).reshape(P, E1, F1),
                               g("L1_ffn_b1").reshape(E1, 2, P).transpose(2, 0, 1), g("L1_ffn_b2").T[:, :, None]], axis=2),
        "wp": np.concatenate([g("L1_ffn_Wp1"), g("L1_ffn_bp1")[:, None], g("L1_ffn_Wp2")], axis=1),
        "wo1": g("L1_ffn_Wo"),
        "r1": np.concatenate([g("L1_ffn_bp2"), g("L1_ffn_bo")])[None],
        "io1": np.arange(E1, dtype=f)[None] - 64,
        "ones": np.ones((1, P), f),
        "onesq": np.ones((P, P), f),
        "wgT": g("L0_ffn_wg").T,
        "io": np.arange(E, dtype=f) - 64,
        "ltg": np.tril(np.ones((NG, NG), f), -1),
        "ew": np.concatenate([np.stack([g("L0_ffn_w1"), g("L0_ffn_w3"), g("L0_ffn_w2")], axis=2),
                              np.stack([g("L0_ffn_sw1"), g("L0_ffn_sw3"), g("L0_ffn_sw2")], axis=1)[None]]),
    }
    return {n: np.ascontiguousarray(v) for n, v in d.items()}


def kernel(**inputs):
    import concourse.bacc as _bacc
    from concourse.bass_utils import run_bass_kernel_spmd as _run

    nc = _bacc.Bacc("TRN2", target_bir_lowering=False, num_devices=1)
    arrays, args = {}, {}
    for name, v in layout(inputs).items():
        arrays[f"in_{name}_dram"] = v
        args[name] = nc.dram_tensor(f"in_{name}_dram", v.shape, mybir.dt.from_np(v.dtype), kind="ExternalInput").ap()
    out = nc.dram_tensor("out_0_dram", _OUTS[0][0], F32, kind="ExternalOutput").ap()
    build(nc, args, out)
    r = _run(nc, [arrays], core_ids=[0])
    return r.results[0]["out_0_dram"]
```
